# Optimizing a Trainium2 kernel written in Bass

```python
import numpy as np
import jax
import jax.numpy as jnp

def _softmax(x, axis=-1):
    return jax.nn.softmax(x, axis=axis)

def _gelu(x):
    return jax.nn.gelu(x, approximate=True)

def _silu(x):
    return jax.nn.silu(x)

def _sigmoid(x):
    return jax.nn.sigmoid(x)

def _layernorm(x, axis=-1, eps=1e-05):
    m = jnp.mean(x, axis=axis, keepdims=True)
    v = jnp.var(x, axis=axis, keepdims=True)
    return (x - m) / jnp.sqrt(v + eps)

def _scatter_add(tgt, idx, src, axis=0):
    return tgt.at[idx].add(src)

def _segment_sum(src, seg, n):
    return jax.ops.segment_sum(src, seg, n)
kernel_name = 'mk_adj_ffn_d1_adj_r2_c4f5c9'

def setup_inputs(seed: int=0):
    np.random.seed(seed)
    _w = jnp.asarray

    def _rec_inputs():
        import jax
        import jax.numpy as jnp
        _gk = jax.random.key(seed)
        x = 7.22e-05 + 1 * jax.random.normal(jax.random.fold_in(_gk, 1), (128, 128, 128), jnp.float32)
        _w = (1.0 + jnp.arange(128, dtype=jnp.float32)) ** (-0.5)
        _w = _w / _w.mean()
        _pij = jnp.clip(0.125 * _w[:, None] * _w[None, :], 0.0, 1.0)
        _a = jax.random.uniform(jax.random.fold_in(_gk, 2), (128, 128, 128)) < _pij
        _a = jnp.logical_or(_a, jnp.swapaxes(_a, -1, -2))
        _a = jnp.logical_or(_a, jnp.eye(128, dtype=bool))
        _af = _a.astype(jnp.float32)
        adj = _af
        return (x, adj)
    x, adj = _rec_inputs()

    def _L0_gnn_setup():
        import jax, jax.numpy as jnp
        import numpy as np
        from jax import lax
        DIM = 128
        EPS = 1e-05

        def _bn(h, g, b, m, v):
            scale = g / jnp.sqrt(v + EPS)
            return h * scale[None, :, None] + (b - m * scale)[None, :, None]

        def _conv1d(h, w, pad):
            return lax.conv_general_dilated(h, w, window_strides=(1,), padding=[(pad, pad)], dimension_numbers=('NCH', 'OIH', 'NCH'))
        key = jax.random.key(seed)
        ks = jax.random.split(key, 16)
        bs, n, d = (16, 1024, DIM)
        s = 0.05
        return {'x': jax.random.normal(ks[0], (bs, n, d), jnp.float32), 'mask': jnp.ones((bs, n, n), jnp.float32), 'w_se': jax.random.normal(ks[1], (3, d), jnp.float32) * s, 'b_se': jnp.zeros((3,), jnp.float32), 'conv1_w': jax.random.normal(ks[2], (d, d, 1), jnp.float32) * s, 'bn1_g': jnp.ones((d,), jnp.float32), 'bn1_b': jnp.zeros((d,), jnp.float32), 'bn1_m': jnp.zeros((d,), jnp.float32), 'bn1_v': jnp.ones((d,), jnp.float32), 'conv2_w': jax.random.normal(ks[3], (d, d, 17), jnp.float32) * s, 'bn2_g': jnp.ones((d,), jnp.float32), 'bn2_b': jnp.zeros((d,), jnp.float32), 'bn2_m': jnp.zeros((d,), jnp.float32), 'bn2_v': jnp.ones((d,), jnp.float32), 'w_msg': jax.random.normal(ks[4], (d, d), jnp.float32) * s, 'b_msg': jnp.zeros((d,), jnp.float32), 'w_ih': jax.random.normal(ks[5], (3 * d, 2 * d), jnp.float32) * s, 'b_ih': jnp.zeros((3 * d,), jnp.float32), 'w_hh': jax.random.normal(ks[6], (3 * d, d), jnp.float32) * s, 'b_hh': jnp.zeros((3 * d,), jnp.float32)}
    _L0_gnn_all = _L0_gnn_setup()
    _L0_gnn_in = {k: v for k, v in _L0_gnn_all.items() if k in ('w_se', 'b_se', 'conv1_w', 'bn1_g', 'bn1_b', 'bn1_m', 'bn1_v', 'conv2_w', 'bn2_g', 'bn2_b', 'bn2_m', 'bn2_v', 'w_msg', 'b_msg', 'w_ih', 'b_ih', 'w_hh', 'b_hh')}
    del _L0_gnn_all

    def _L0_ffn_setup():
        import jax, jax.numpy as jnp
        import numpy as np
        N_EXPERTS = 8
        TOP_K = 2
        key = jax.random.key(seed)
        ks = jax.random.split(key, 5)
        B, T, C, E, H = (8, 1024, 128, 8, 341)
        scale = 1.0 / np.sqrt(C)
        return {'x': jax.random.normal(ks[0], (B, T, C), dtype=jnp.float32), 'router_w': jax.random.normal(ks[1], (E, C), dtype=jnp.float32) * scale, 'w1': jax.random.normal(ks[2], (E, H, C), dtype=jnp.float32) * scale, 'w2': jax.random.normal(ks[3], (E, C, H), dtype=jnp.float32) * (1.0 / np.sqrt(H)), 'w3': jax.random.normal(ks[4], (E, H, C), dtype=jnp.float32) * scale}
    _L0_ffn_all = _L0_ffn_setup()
    _L0_ffn_in = {k: v for k, v in _L0_ffn_all.items() if k in ('router_w', 'w1', 'w2', 'w3')}
    del _L0_ffn_all
    return {'x': x, 'adj': adj, 'L0_gnn_w_se': _L0_gnn_in['w_se'], 'L0_gnn_b_se': _L0_gnn_in['b_se'], 'L0_gnn_conv1_w': _L0_gnn_in['conv1_w'], 'L0_gnn_bn1_g': _L0_gnn_in['bn1_g'], 'L0_gnn_bn1_b': _L0_gnn_in['bn1_b'], 'L0_gnn_bn1_m': _L0_gnn_in['bn1_m'], 'L0_gnn_bn1_v': _L0_gnn_in['bn1_v'], 'L0_gnn_conv2_w': _L0_gnn_in['conv2_w'], 'L0_gnn_bn2_g': _L0_gnn_in['bn2_g'], 'L0_gnn_bn2_b': _L0_gnn_in['bn2_b'], 'L0_gnn_bn2_m': _L0_gnn_in['bn2_m'], 'L0_gnn_bn2_v': _L0_gnn_in['bn2_v'], 'L0_gnn_w_msg': _L0_gnn_in['w_msg'], 'L0_gnn_b_msg': _L0_gnn_in['b_msg'], 'L0_gnn_w_ih': _L0_gnn_in['w_ih'], 'L0_gnn_b_ih': _L0_gnn_in['b_ih'], 'L0_gnn_w_hh': _L0_gnn_in['w_hh'], 'L0_gnn_b_hh': _L0_gnn_in['b_hh'], 'L0_ffn_router_w': _L0_ffn_in['router_w'], 'L0_ffn_w1': _L0_ffn_in['w1'], 'L0_ffn_w2': _L0_ffn_in['w2'], 'L0_ffn_w3': _L0_ffn_in['w3']}

def reference(x, adj, L0_gnn_w_se, L0_gnn_b_se, L0_gnn_conv1_w, L0_gnn_bn1_g, L0_gnn_bn1_b, L0_gnn_bn1_m, L0_gnn_bn1_v, L0_gnn_conv2_w, L0_gnn_bn2_g, L0_gnn_bn2_b, L0_gnn_bn2_m, L0_gnn_bn2_v, L0_gnn_w_msg, L0_gnn_b_msg, L0_gnn_w_ih, L0_gnn_b_ih, L0_gnn_w_hh, L0_gnn_b_hh, L0_ffn_router_w, L0_ffn_w1, L0_ffn_w2, L0_ffn_w3):
    import jax
    import jax.numpy as jnp

    def _L0_gnn_ref(x, mask, w_se, b_se, conv1_w, bn1_g, bn1_b, bn1_m, bn1_v, conv2_w, bn2_g, bn2_b, bn2_m, bn2_v, w_msg, b_msg, w_ih, b_ih, w_hh, b_hh):
        import jax, jax.numpy as jnp
        import numpy as np
        from jax import lax
        DIM = 128
        EPS = 1e-05

        def _bn(h, g, b, m, v):
            scale = g / jnp.sqrt(v + EPS)
            return h * scale[None, :, None] + (b - m * scale)[None, :, None]

        def _conv1d(h, w, pad):
            return lax.conv_general_dilated(h, w, window_strides=(1,), padding=[(pad, pad)], dimension_numbers=('NCH', 'OIH', 'NCH'))
        d = x.shape[-1]
        xc = jnp.transpose(x, (0, 2, 1))
        h = _bn(_conv1d(xc, conv1_w, 0), bn1_g, bn1_b, bn1_m, bn1_v)
        h = jax.nn.relu(h)
        h = _bn(_conv1d(h, conv2_w, 8), bn2_g, bn2_b, bn2_m, bn2_v)
        x_conv = jnp.transpose(jax.nn.relu(h + xc), (0, 2, 1))
        s = x @ w_se.T + b_se
        sq = jnp.sum(s * s, axis=-1)
        dist = sq[:, :, None] + sq[:, None, :] - 2.0 * jnp.einsum('bnd,bmd->bnm', s, s)
        A = jnp.exp(-dist) * mask
        msg = jax.nn.relu(x @ w_msg.T + b_msg)
        x_nmp = jnp.einsum('bnm,bmd->bnd', A, msg)
        x_in = jnp.concatenate([x_conv, x_nmp], axis=-1)
        gi = x_in @ w_ih.T + b_ih
        gh = x @ w_hh.T + b_hh
        gi_r, gi_z, gi_n = (gi[..., :d], gi[..., d:2 * d], gi[..., 2 * d:])
        gh_r, gh_z, gh_n = (gh[..., :d], gh[..., d:2 * d], gh[..., 2 * d:])
        r = jax.nn.sigmoid(gi_r + gh_r)
        z = jax.nn.sigmoid(gi_z + gh_z)
        nn_ = jnp.tanh(gi_n + r * gh_n)
        return (1.0 - z) * nn_ + z * x

    def _L0_ffn_ref(x, router_w, w1, w2, w3):
        import jax, jax.numpy as jnp
        import numpy as np
        N_EXPERTS = 8
        TOP_K = 2
        B, T, C = x.shape
        flat = x.reshape(-1, C)
        logits = flat @ router_w.T
        probs = jax.nn.softmax(logits, axis=-1)
        topk_probs, topk_idx = jax.lax.top_k(probs, TOP_K)
        topk_probs = topk_probs / (jnp.sum(topk_probs, axis=-1, keepdims=True) + 1e-09)
        onehot = jax.nn.one_hot(topk_idx, N_EXPERTS, dtype=flat.dtype)
        gates = jnp.einsum('nk,nke->ne', topk_probs, onehot)
        h1 = jnp.einsum('nc,ehc->neh', flat, w1)
        h3 = jnp.einsum('nc,ehc->neh', flat, w3)
        h = jax.nn.silu(h1) * h3
        y = jnp.einsum('neh,ech->nec', h, w2)
        out = jnp.einsum('ne,nec->nc', gates, y)
        return out.reshape(B, T, C)
    x = x + _L0_gnn_ref(_layernorm(x, axis=-1), adj, L0_gnn_w_se, L0_gnn_b_se, L0_gnn_conv1_w, L0_gnn_bn1_g, L0_gnn_bn1_b, L0_gnn_bn1_m, L0_gnn_bn1_v, L0_gnn_conv2_w, L0_gnn_bn2_g, L0_gnn_bn2_b, L0_gnn_bn2_m, L0_gnn_bn2_v, L0_gnn_w_msg, L0_gnn_b_msg, L0_gnn_w_ih, L0_gnn_b_ih, L0_gnn_w_hh, L0_gnn_b_hh)
    x = x + _L0_ffn_ref(_layernorm(x, axis=-1), L0_ffn_router_w, L0_ffn_w1, L0_ffn_w2, L0_ffn_w3)
    return x

_drawn_inputs = setup_inputs


def setup_inputs(seed=0):
    import zlib

    import numpy as np

    out = dict(_drawn_inputs(seed))
    spreads = {'L0_gnn_b_se': (0.0, 0.8),
     'L0_gnn_bn1_g': (1.0, 0.2),
     'L0_gnn_bn1_b': (0.0, 0.274),
     'L0_gnn_bn1_m': (0.0, 0.1),
     'L0_gnn_bn1_v': (1.0, 0.6),
     'L0_gnn_bn2_g': (1.0, 0.2),
     'L0_gnn_bn2_b': (0.0, 0.335),
     'L0_gnn_bn2_m': (0.0, 0.342),
     'L0_gnn_bn2_v': (1.0, 0.6),
     'L0_gnn_b_msg': (0.0, 0.1),
     'L0_gnn_b_ih': (0.0, 0.1),
     'L0_gnn_b_hh': (0.0, 0.1)}
    factors = {}
    for name, (base, spread) in spreads.items():
        noise = np.random.default_rng([zlib.crc32(name.encode()), seed]).standard_normal(out[name].shape)
        drawn = base * np.exp(spread * noise) if base else spread * noise
        out[name] = jnp.asarray(drawn.astype(out[name].dtype))
    for name, factor in factors.items():
        out[name] = (out[name] * factor).astype(out[name].dtype)
    return out
```

```python
from contextlib import ExitStack

import concourse.bass as bass
from concourse import mybir

F32 = mybir.dt.float32
F16 = mybir.dt.float16
I32 = mybir.dt.int32
ALU = mybir.AluOpType
ACT = mybir.ActivationFunctionType
AX = mybir.AxisListType

P = 128
GB = 4
W = GB * P
WS = 16.0
EPS = 1e-5
TAPS = 17
HALF_TAPS = TAPS // 2
EC = 3
ROW = P + 2
VECS = 14


def build(nc, x, adj, w_se, b_se, conv1_w, bn1_g, bn1_b, bn1_m, bn1_v, conv2_w, bn2_g, bn2_b, bn2_m, bn2_v,
          w_msg, b_msg, w_ih, b_ih, w_hh, b_hh, router_w, w1, w2, w3, out):
    NB = x.shape[0]
    N = NB * P
    NG = NB // GB
    NE, H, _ = w1.shape
    HC = -(-H // EC)
    HL = H - (EC - 1) * HC
    TOPK = 2
    NT = N * TOPK // W + NE
    REGION = N + W
    XROWS = NE * REGION + NE * W
    YROWS = TOPK * N + 2 * W
    assert x.shape[1] == P and x.shape[2] == P and NG % 2 == 0 and NT % 2 == 0

    routed = nc.dram_tensor("routed", [XROWS, ROW], F32).ap()
    expert_out = nc.dram_tensor("expert_out", [YROWS, P], F32).ap()

    with ExitStack() as ctx:
        def sb(name, shape, dt=F32):
            return ctx.enter_context(nc.sbuf_tensor(name, shape, dt))

        def sem(name):
            return ctx.enter_context(nc.semaphore(name))

        xres = sb("xres", [P, NB, P])
        gwh = sb("gwh", [P, 28, P], F16)
        gwl = sb("gwl", [P, 28, P], F16)
        w1h = sb("w1h", [P, NE * EC * HC], F16)
        w1l = sb("w1l", [P, NE * EC * HC], F16)
        w3h = sb("w3h", [P, NE * EC * HC], F16)
        w3l = sb("w3l", [P, NE * EC * HC], F16)
        w2h = sb("w2h", [P, NE * EC * P], F16)
        w2l = sb("w2l", [P, NE * EC * P], F16)
        ident = sb("ident", [P, P])
        tri = sb("tri", [P, P], F16)
        ones = sb("ones", [P, P], F16)
        vecs = sb("vecs", [P, VECS])
        coef = sb("coef", [P, 12])
        bse = sb("bse", [P, 2])
        wseh = sb("wseh", [P, 67], F16)
        wsel = sb("wsel", [P, 67], F16)
        routerT = sb("routerT", [P, NE])
        bmsg = sb("bmsg", [2, W], F16)
        em = sb("em", [P, GB, NE])
        region0 = sb("region0", [P, GB, NE])
        half = sb("half", [P, GB])
        carry = sb("carry", [P, NE], F16)
        filler = sb("filler", [P, GB, ROW])
        upto = sb("upto", [P, NE, NE])
        tilenum = sb("tilenum", [P, NT])
        tile_row = sb("tile_row", [P, NT], I32)
        tile_exp = sb("tile_exp", [P, NT], I32)
        fill_row = sb("fill_row", [P, NE], I32)
        arena = sb("arena", [P, 18560])

        RAWG = 16 * (7 + 8 + 13)
        VSTEPS = 16
        ROUTE_STEPS = 23
        spot = [0]

        def carve(cols, dt=F32):
            a = arena[:, spot[0]:spot[0] + cols]
            spot[0] += cols
            return a if dt == F32 else a.bitcast(dt)

        HP = EC * HC
        w1raw = carve(NE * EC * P).rearrange("p (t c) -> p t c", c=P)
        w3raw = carve(NE * EC * P).rearrange("p (t c) -> p t c", c=P)
        w2raw = carve(NE * HP).rearrange("p (e h) -> p e h", h=HP)
        c2raw = carve(P * TAPS).rearrange("p (c k) -> p c k", k=TAPS)
        wihraw = carve(6 * P).rearrange("p (t c) -> p t c", c=P)
        whhraw = carve(3 * P).rearrange("p (t c) -> p t c", c=P)
        c1raw = carve(P)
        msgraw = carve(P)
        vecraw = carve(P)
        wseraw = carve(P)
        routraw = carve(P)
        bmraw = carve(W)
        bmh = carve(W)
        bml = carve(W)
        vtmp = carve(8)

        spot[0] = 0
        adjb = [carve(W).rearrange("p (b c) -> p b c", b=GB) for _ in range(2)]
        xn = carve(W)
        xT = [carve(W) for _ in range(2)]
        xTh = [carve(W // 2, F16) for _ in range(2)]
        xTl = [carve(W // 2, F16) for _ in range(2)]
        h1 = carve(W)
        h1h = [carve(W // 2, F16) for _ in range(2)]
        h1l = [carve(W // 2, F16) for _ in range(2)]
        sL = carve(W)
        sR = carve(W)
        kern = carve(W)
        A = carve(W)
        Ah = carve(W // 2, F16)
        Al = carve(W // 2, F16)
        msgh = carve(W // 2, F16)
        msgl = carve(W // 2, F16)
        nmph = [carve(W // 2, F16) for _ in range(2)]
        nmpl = [carve(W // 2, F16) for _ in range(2)]
        ysum = carve(W)
        y = carve(W)
        yh = carve(W // 2, F16)
        yl = carve(W // 2, F16)
        rt = carve(W)
        zt = carve(W)
        hn = carve(W)
        rhn = carve(W)
        npre = carve(W)
        nn = carve(W)
        dxn = carve(W)
        zd = carve(W)
        gru = carve(W)
        rows = [[carve(GB * ROW).rearrange("p (b c) -> p b c", b=GB) for _ in range(TOPK)] for _ in range(2)]
        xn2T = carve(W)
        bn6 = [carve(GB * 6).rearrange("p (b c) -> p b c", b=GB) for _ in range(2)]
        mv = [carve(GB * 2).rearrange("p (b c) -> p b c", b=GB) for _ in range(2)]
        varp = [carve(GB) for _ in range(2)]
        rstd = [carve(GB) for _ in range(2)]

        def small(n=GB * NE):
            return carve(n).rearrange("p (b e) -> p b e", b=GB)

        lmax, lsum, lrec, p1, p2, k1, k2, den, dinv = [carve(GB) for _ in range(9)]
        lshift, lexp, prob, eq, cand, prob2, rk = [small() for _ in range(7)]
        picks = [carve(TOPK * GB * NE).rearrange("p (k b e) -> p k b e", k=TOPK, b=GB) for _ in range(2)]
        rank_of = carve(TOPK * GB * NE).rearrange("p (k b e) -> p k b e", k=TOPK, b=GB)
        picked = [carve(GB * NE // 2, F16).rearrange("p (b e) -> p b e", b=GB) for _ in range(2)]
        pickedsum = carve(NE)
        slotf = carve(TOPK * GB).rearrange("p (k b) -> p k b", k=TOPK)
        slot = [carve(TOPK * GB).bitcast(I32).rearrange("p (k b) -> p k b", k=TOPK) for _ in range(2)]

        spot[0] = 0
        total = carve(NE)
        totali = carve(NE).bitcast(I32)
        tiles = carve(NE)
        tiles_le = carve(NE * NE).rearrange("p (a e) -> p a e", e=NE)
        tile_end = carve(NE)
        past = carve(NT * NE).rearrange("p (t e) -> p t e", e=NE)
        pastn = carve(NT * NE).rearrange("p (t e) -> p t e", e=NE)
        tile_e = carve(NT)
        tile_s = carve(NT)
        tile_f = carve(NT)
        fill_f = carve(NE)
        spot[0] = 2048
        tile = [carve(GB * ROW).rearrange("p (b c) -> p b c", b=GB) for _ in range(2)]
        tTh = [carve(W // 2, F16) for _ in range(2)]
        tTl = [carve(W // 2, F16) for _ in range(2)]
        act1 = [carve(W) for _ in range(EC)]
        hid = [carve(W) for _ in range(EC)]
        hidh = [[carve(W // 2, F16) for _ in range(EC)] for _ in range(2)]
        hidl = [[carve(W // 2, F16) for _ in range(EC)] for _ in range(2)]
        yo = [carve(W).rearrange("p (b c) -> p b c", b=GB) for _ in range(2)]
        tgate = [carve(GB) for _ in range(2)]
        pad = [carve(GB) for _ in range(2)]
        dest = [carve(GB).bitcast(I32) for _ in range(2)]
        CG = 8
        NCH = NB // CG
        CB = 3
        spot[0] = 0
        chosen = [[carve(CG * P).rearrange("p (b c) -> p b c", b=CG) for _ in range(TOPK)] for _ in range(CB)]

        bank = [ctx.enter_context(nc.psum_tensor(f"bank{i}", [P, W], F32)) for i in range(8)]

        def graphs(ap):
            return ap.rearrange("p (b c) -> p b c", b=GB)

        s_raw = sem("raw_landed")
        s_rawg = sem("raw_gnn_landed")
        s_zero = sem("raw_zeroed")
        s_const = sem("consts_ready")
        s_cst = sem("const_step")
        s_tp = sem("weights_transposed")
        s_hi = sem("weights_high")
        s_lo = sem("weights_low")
        s_vec = sem("vecs_step")
        s_vecp = sem("vec_power")

        gsrc = []
        for gate in range(3):
            gsrc += [wihraw[:, 2 * gate, :], wihraw[:, 2 * gate + 1, :], whhraw[:, gate, :]]
        gsrc += [c1raw[:, :], msgraw[:, :]] + [c2raw[:, :, k] for k in range(TAPS)]
        CONV1, MSG, CONV2 = 9, 10, 11
        jobs = []
        for t in range(0, 28, 4):
            jobs.append((gwh[:, t:t + 4, :].rearrange("p t c -> p (t c)"), gwl[:, t:t + 4, :].rearrange("p t c -> p (t c)"), gsrc[t:t + 4], P, P))
        for raw, hi, lo in ((w1raw, w1h, w1l), (w3raw, w3h, w3l)):
            for t in range(0, NE * EC, 4):
                jobs.append((hi[:, t * HC:(t + 4) * HC], lo[:, t * HC:(t + 4) * HC],
                             [raw[0:HC, t + j, :] for j in range(4)], P, HC))
        for t in range(0, NE * EC, 4):
            jobs.append((w2h[0:HC, t * P:(t + 4) * P], w2l[0:HC, t * P:(t + 4) * P],
                         [w2raw[:, (t + j) // EC, (t + j) % EC * HC:((t + j) % EC + 1) * HC] for j in range(4)], HC, P))
        NGJ = 7
        JB = 4

        ctxb = ctx.enter_context(nc.Block())
        block = ctxb

        x_landed = [sem(f"x_landed{i}") for i in range(2)]
        adj_landed = [sem(f"adj_landed{i}") for i in range(2)]
        (ln1_stats, ln1_rstd, xn_ready, xnT_ps, xT_ready, xTh_ready, xTl_ready, conv1_ps, h1_ready, h1h_ready,
         h1l_ready, s_ps, sLR_ready, msg_ps, msgh_ready, msgl_ready, maskT_ps, dist_ps, kern_ready, A_ready,
         Ah_ready, Al_ready, nmp_ps, nmph_ready, nmpl_ready, conv2_ps, ysum_ready, y_ready, yh_ready, yl_ready,
         hn_ps, gates_ps, rt_ready, zt_ready, hn_ready, rhn_ready, npre_ready, nn_ready, dxn_ready, zd_ready,
         gru_ready, gruT_ps, x2_ready, ln2_stats, ln2_rstd, rows_ready, rows2_ready, xn2T_ps, xn2T_ready,
         logits_ps, lshift_ready, lexp_ready, picks_ready, rank_ps, slots_ready) = [sem(n) for n in (
            "ln1_stats ln1_rstd xn_ready xnT_ps xT_ready xTh_ready xTl_ready conv1_ps h1_ready h1h_ready "
            "h1l_ready s_ps sLR_ready msg_ps msgh_ready msgl_ready maskT_ps dist_ps kern_ready A_ready "
            "Ah_ready Al_ready nmp_ps nmph_ready nmpl_ready conv2_ps ysum_ready y_ready yh_ready yl_ready "
            "hn_ps gates_ps rt_ready zt_ready hn_ready rhn_ready npre_ready nn_ready dxn_ready zd_ready "
            "gru_ready gruT_ps x2_ready ln2_stats ln2_rstd rows_ready rows2_ready xn2T_ps xn2T_ready "
            "logits_ps lshift_ready lexp_ready picks_ready rank_ps slots_ready").split()]
        ln_step = sem("ln_step")
        route_step = sem("route_step")
        scattered = [sem(f"scattered{i}") for i in range(2)]
        routed_landed = sem("routed_landed")
        table_step = sem("table_step")
        totals_ps = sem("totals_ps")
        table_ready = sem("table_ready")
        fill_landed = sem("fill_landed")
        tile_landed = [sem(f"tile_landed{i}") for i in range(2)]
        (tileT_ps, meta_ready, meta_step, tTh_ready, tTl_ready, h13_ps, act1_ready, hid_ready, hidh_ready,
         hidl_ready, y_ps, yo_ready) = [sem("tile_" + n) for n in (
            "tileT_ps meta_ready meta_step tTh_ready tTl_ready h13_ps act1_ready hid_ready hidh_ready "
            "hidl_ready y_ps yo_ready").split()]
        out_scattered = [sem(f"out_scattered{i}") for i in range(2)]
        chosen_landed = [sem(f"chosen_landed{i}") for i in range(CB)]
        sum_step = sem("sum_step")
        summed = sem("summed")
        out_stored = sem("out_stored")
        eo_v = expert_out[0:TOPK * N, :].rearrange("(b n) c -> n b c", n=P)
        out_v = out.rearrange("b n c -> n b c")

        def after(eng, s, n):
            if isinstance(n, int) and n <= 0:
                return
            eng.wait_ge(s, n)

        waited_apart = sem("waited_apart")

        def after_apart(eng, s, n):
            after(eng, s, n)
            if not isinstance(n, int):
                eng.sem_inc(waited_apart, 1)

        class Step:

            def __init__(self, i, par, bounded, total):
                self.i, self.par, self.bounded, self.total = i, par, bounded, total

            def g(self, off=0):
                return self.i * 2 + (self.par + off)

            def half(self, off=0):
                return self.i + (self.par + off) // 2

            def side(self, off=0):
                return (self.par + off) % 2

            def has(self, off=0):
                return not self.bounded or 0 <= self.g(off) < self.total

        def gnn_loop(eng, body):
            for g in range(-2, 4):
                body(Step(g // 2, g % 2, True, NG))
            with eng.Fori(2, NG // 2 - 1) as i:
                body(Step(i, 0, False, NG))
                body(Step(i, 1, False, NG))
            for g in range(NG - 2, NG + 2):
                body(Step(g // 2, g % 2, True, NG))

        def tile_loop(eng, body):
            for t in range(-1, 4):
                body(Step(t // 2, t % 2, True, NT))
            with eng.Fori(2, NT // 2 - 1) as i:
                body(Step(i, 0, False, NT))
                body(Step(i, 1, False, NT))
            for t in range(NT - 2, NT + 1):
                body(Step(t // 2, t % 2, True, NT))

        x_v = x.rearrange("b n c -> n b c")
        adj_v = adj.rearrange("b n m -> n b m")

        SC1, SH1, SC2, SH2, BR, BZ, BIN, BHN = range(8)

        @block.sync
        def _(sp):
            n = 0
            for dst, src in (
                (wihraw, w_ih.rearrange("(g o) (h c) -> o g h c", o=P, c=P)),
                (whhraw, w_hh.rearrange("(g o) c -> o g c", o=P)),
                (c1raw, conv1_w.rearrange("o c k -> o (c k)")),
                (msgraw, w_msg),
                (c2raw, conv2_w),
                (wseraw[0:3, :], w_se),
                (routraw[0:NE, :], router_w),
            ):
                if dst is wihraw:
                    dst = wihraw.rearrange("p (g h) c -> p g h c", h=2)
                sp.dma_start(dst, src).then_inc(s_rawg, 16)
                n += 16
            for r, v in enumerate((bn1_g, bn1_b, bn1_m, bn1_v, bn2_g, bn2_b, bn2_m, bn2_v)):
                sp.dma_start(vecraw[r:r + 1, :], v.rearrange("(a c) -> a c", a=1)).then_inc(s_rawg, 16)
                n += 16
            sp.dma_start(vecraw[8:11, :], b_ih.rearrange("(g c) -> g c", c=P)).then_inc(s_rawg, 16)
            sp.dma_start(vecraw[11:14, :], b_hh.rearrange("(g c) -> g c", c=P)).then_inc(s_rawg, 16)
            sp.wait_ge(s_zero, 1)
            for q in (0, 32, 64):
                sp.dma_start(bse[q:q + 3, 0:1], b_se.rearrange("(c a) -> c a", a=1)).then_inc(s_rawg, 16)
            for r in range(2):
                for b in range(GB):
                    sp.dma_start(bmraw[r:r + 1, b * P:(b + 1) * P], b_msg.rearrange("(a c) -> a c", a=1)).then_inc(s_rawg, 16)
            n += 16 * 13
            assert n == RAWG
            for raw, src in ((w1raw, w1), (w3raw, w3)):
                rv = raw.rearrange("p (e k) c -> p e k c", k=EC)
                for k in range(EC):
                    hk = HC if k < EC - 1 else HL
                    sp.dma_start(rv[0:hk, :, k, :],
                                 src[:, k * HC:k * HC + hk, :].rearrange("e h c -> h e c")).then_inc(s_raw, 16)
            sp.dma_start(w2raw[:, :, 0:H], w2.rearrange("e c h -> c e h")).then_inc(s_raw, 16)
            sp.wait_ge(s_tp, len(jobs) + 1)

            def body(st):
                if st.has(2):
                    g, p = st.g(2), st.side(2)
                    after(sp, ln1_stats, st.g(0) + 1)
                    sp.dma_start(xres[:, bass.ds(g * GB, GB), :], x_v[:, bass.ds(g * GB, GB), :]).then_inc(x_landed[p], 16)
                    after(sp, maskT_ps, st.g(0) + 1)
                    sp.dma_start(adjb[p], adj_v[:, bass.ds(g * GB, GB), :]).then_inc(adj_landed[p], 16)

            for g in range(-2, 0):
                body(Step(g // 2, g % 2, True, NG))
            with sp.Fori(0, NG // 2 - 1) as i:
                body(Step(i, 0, False, NG))
                body(Step(i, 1, False, NG))

            sp.wait_ge(routed_landed, 1)
            sp.wait_ge(fill_landed, 2 * NE * 16)
            sp.wait_ge(table_ready, 1)

            def load_tile(st):
                p = st.side(0)
                after(sp, tileT_ps, st.g(-2) + 1)
                after(sp, meta_ready, st.g(-2) + 1)
                row = sp.value_load(tile_row[0:1, bass.ds(st.g(0), 1)], min_val=0, max_val=XROWS - W)
                sp.dma_start(tile[p], routed[bass.ds(row, W), :].rearrange("(p r) c -> p r c", p=P)).then_inc(tile_landed[p], 16)

            for t in range(2):
                load_tile(Step(0, t, True, NT))
            with sp.Fori(1, NT // 2) as i:
                load_tile(Step(i, 0, False, NT))
                load_tile(Step(i, 1, False, NT))

            for p in range(2):
                sp.wait_ge(out_scattered[p], NT // 2 * GB * 16)
            for n in range(NCH):
                if n >= CB:
                    sp.wait_ge(summed, n - CB + 1)
                for c in range(TOPK):
                    sp.dma_start(chosen[n % CB][c], eo_v[:, c * NB + n * CG:c * NB + (n + 1) * CG, :]).then_inc(chosen_landed[n % CB], 16)
            sp.wait_ge(out_stored, NCH * 16)

        @block.gpsimd
        def _(pool):
            k = [0]

            def link(ins):
                k[0] += 1
                ins.then_inc(s_cst, 1)
                pool.wait_ge(s_cst, k[0])

            for raw in (w1raw, w3raw):
                link(pool.memset(raw[96:HC, :, :].rearrange("p (e k) c -> p e k c", k=EC)[:, :, EC - 1, :], 0.0))
            link(pool.memset(bse[:, :], 0.0))
            pool.memset(w2raw[:, :, H:HP], 0.0).then_inc(s_zero, 1)
            pool.wait_ge(s_zero, 1)
            link(pool.memset(ident[:, :], 0.0))
            link(pool.affine_select(out=ident[:, :], in_=ident[:, :], compare_op=ALU.not_equal, fill=1.0, base=0,
                                    pattern=[[-1, P]], channel_multiplier=1))
            link(pool.memset(ones[:, :], 1.0))
            link(pool.affine_select(out=tri[:, :], in_=ones[:, :], compare_op=ALU.is_gt, fill=0.0, base=0,
                                    pattern=[[1, P]], channel_multiplier=-1))
            link(pool.memset(half[:, :], -0.5))
            link(pool.memset(carry[:, :], 0.0))
            link(pool.iota(rank_of[:, 0, :, :].bitcast(I32), pattern=[[0, GB], [1, NE]], base=-NE, channel_multiplier=0))
            link(pool.tensor_copy(em[:, :, :], rank_of[:, 0, :, :].bitcast(I32)))
            link(pool.tensor_scalar(region0[:, :, :], em[:, :, :], float(NE), float(REGION), ALU.add, ALU.mult))
            link(pool.memset(wseh[:, :], 0.0))
            link(pool.memset(filler[:, :, :], 0.0))
            link(pool.iota(rank_of[:, 1, 0, 0:GB].bitcast(I32), pattern=[[1, GB]], base=TOPK * N, channel_multiplier=GB))
            link(pool.tensor_copy(filler[:, :, P + 1], rank_of[:, 1, 0, 0:GB].bitcast(I32)))
            link(pool.memset(upto[:, :, :], 1.0))
            link(pool.affine_select(out=upto[:, :, :], in_=upto[:, :, :], compare_op=ALU.is_ge, fill=0.0, base=0,
                                    pattern=[[1, NE], [-1, NE]], channel_multiplier=0))
            link(pool.iota(tile_row[:, :], pattern=[[1, NT]], base=0, channel_multiplier=0))
            link(pool.tensor_copy(tilenum[:, :], tile_row[:, :]))
            pool.memset(wsel[:, :], 0.0).then_inc(s_const, 1)
            pool.wait_ge(s_vec, 2)
            pool.tensor_tensor(vtmp[:, 4:6], vtmp[:, 0:2], half[:, 0:2], ALU.pow).then_inc(s_vecp, 1)
            pool.wait_ge(s_lo, len(jobs) + 2)
            k1_ = k[0]
            for p in range(2):
                for c in range(TOPK):
                    link(pool.iota(slot[p][:, c, :], pattern=[[P, GB]], base=c * N + (p - 2) * W, channel_multiplier=1))
                    link(pool.tensor_copy(rows[p][c][:, :, P + 1], slot[p][:, c, :]))
            link(pool.memset(sL[0:67, :], 0.0))
            link(pool.memset(sR[0:67, :], 0.0))
            link(pool.memset(sL[64:67, :], 1.0))
            pool.memset(sR[32:35, :], 1.0).then_inc(s_const, 1)
            pool.wait_ge(s_const, 2)

            def body(st):
                g = st.g
                if st.has(-1):
                    after(pool, nn_ready, g(-1) + 1)
                    pool.tensor_tensor(dxn, xT[st.side(-1)], nn, ALU.subtract).then_inc(dxn_ready, 1)
                if st.has(-2):
                    p = st.side(-2)
                    after_apart(pool, slots_ready, g(-2) + 1)
                    for c in range(TOPK):
                        for b in range(GB):
                            pool.indirect_dma_start(routed, bass.IndirectOffsetOnAxis(ap=slot[p][:, c, b:b + 1], axis=0),
                                                    rows[p][c][:, b, :], None).then_inc(scattered[p], 16)
                if st.has(-1):
                    after(pool, ln2_stats, g(-1) + 1)
                    pool.tensor_tensor(rstd[1], varp[1], half[:, :], ALU.pow).then_inc(ln2_rstd, 1)
                if st.has(1):
                    after(pool, Ah_ready, g(1) + 1)
                    after(pool, nmp_ps, g(1))
                    pool.tensor_tensor(Al, A, Ah, ALU.subtract).then_inc(Al_ready, 1)
                if st.has(2):
                    after(pool, ln1_stats, g(2) + 1)
                    pool.tensor_tensor(rstd[0], varp[0], half[:, :], ALU.pow).then_inc(ln1_rstd, 1)

            gnn_loop(pool, body)
            for p in range(2):
                pool.wait_ge(scattered[p], NG // 2 * TOPK * GB * 16)
            pool.sem_inc(routed_landed, 1)

            def scatter_out(st):
                if st.has(-1):
                    p = st.side(-1)
                    after(pool, out_scattered[p], st.half(-1) * GB * 16)
                    after_apart(pool, yo_ready, st.g(-1) + 1)
                    for b in range(GB):
                        pool.indirect_dma_start(expert_out, bass.IndirectOffsetOnAxis(ap=dest[p][:, b:b + 1], axis=0),
                                                yo[p][:, b, :], None).then_inc(out_scattered[p], 16)

            tile_loop(pool, scatter_out)

        @block.scalar
        def _(act):
            for n, (hi, lo, srcs, m, w) in enumerate(jobs):
                act.wait_ge(s_tp, n + 1)
                act.activation(hi, bank[n % JB][0:m, 0:w * len(srcs)], ACT.Copy, scale=WS).then_inc(s_hi, 1)
            act.wait_ge(s_tp, len(jobs) + 1)
            act.wait_ge(s_const, 1)
            for t in range(NE):
                r0 = NE * REGION + t * W
                act.dma_start(routed[r0:r0 + W, :].rearrange("(p r) c -> p r c", p=P), filler[:, :, :]).then_inc(fill_landed, 16)
            for q in (0, 32, 64):
                last = act.activation(wseh[:, q:q + 3], bank[4][:, 0:3], ACT.Copy, scale=WS)
            last.then_inc(s_hi, 1)

            act.wait_ge(s_vec, VSTEPS)
            act.wait_ge(s_const, 2)

            def body(st):
                g = st.g
                if st.has(-1):
                    after(act, hn_ps, g(-1) + 1)
                    after(act, rhn_ready, g(-2) + 1)
                    act.activation(hn, bank[4][:, :], ACT.Identity, bias=coef[:, BHN:BHN + 1], scale=0.5 / WS).then_inc(hn_ready, 1)
                    after(act, gates_ps, g(-1) + 1)
                    act.activation(rt, bank[1][:, :], ACT.Tanh, bias=coef[:, BR:BR + 1], scale=0.5 / WS).then_inc(rt_ready, 1)
                    after(act, zd_ready, g(-2) + 1)
                    act.activation(zt, bank[2][:, :], ACT.Tanh, bias=coef[:, BZ:BZ + 1], scale=0.5 / WS).then_inc(zt_ready, 1)
                    after(act, npre_ready, g(-1) + 1)
                    after(act, gru_ready, g(-2) + 1)
                    act.activation(nn, npre, ACT.Tanh, bias=coef[:, BIN:BIN + 1]).then_inc(nn_ready, 1)
                if st.has(1):
                    p = st.side(1)
                    after(act, xnT_ps, g(1) + 1)
                    after(act, dxn_ready, g(-1) + 1)
                    act.activation(xT[p], bank[5][:, :], ACT.Copy).then_inc(xT_ready, 1)
                    after(act, conv1_ps, g(1) + 1)
                    after(act, h1l_ready, g(0) + 1)
                    act.activation(h1, bank[1][:, :], ACT.Relu, bias=coef[:, SH1:SH1 + 1], scale=coef[:, SC1:SC1 + 1]).then_inc(h1_ready, 1)
                    after(act, s_ps, g(1) + 1)
                    after(act, dist_ps, g(0) + 1)
                    act.activation(sL[0:3, :], bank[2][0:3, :], ACT.Identity, bias=bse[0:3, 0:1], scale=1.0 / WS)
                    act.activation(sL[32:35, :], bank[2][32:35, :], ACT.Square, bias=bse[32:35, 0:1], scale=1.0 / WS)
                    act.activation(sR[0:3, :], bank[2][0:3, :], ACT.Identity, bias=bse[0:3, 1:2], scale=-2.0 / WS)
                    act.activation(sR[64:67, :], bank[2][64:67, :], ACT.Square, bias=bse[64:67, 0:1], scale=1.0 / WS).then_inc(sLR_ready, 1)
                    after(act, msg_ps, g(1) + 1)
                    after(act, nmp_ps, g(0) + 1)
                    act.activation(msgh, bank[3][:, :], ACT.Relu).then_inc(msgh_ready, 1)
                if st.has(1):
                    after(act, dist_ps, g(1) + 1)
                    after(act, A_ready, g(0) + 1)
                    act.activation(kern, bank[5][:, :], ACT.Exp, scale=-1.0).then_inc(kern_ready, 1)
                if st.has(-1):
                    after(act, xn2T_ps, g(-1) + 1)
                    after(act, logits_ps, g(-2) + 1)
                    act.activation(xn2T, bank[7][:, :], ACT.Copy).then_inc(xn2T_ready, 1)
                if st.has(0):
                    after(act, ysum_ready, g(0) + 1)
                    after(act, yl_ready, g(-1) + 1)
                    act.activation(y, ysum, ACT.Relu, bias=coef[:, SH2:SH2 + 1]).then_inc(y_ready, 1)
                if st.has(-1):
                    after(act, lshift_ready, g(-1) + 1)
                    act.activation(lexp, lshift, ACT.Exp).then_inc(lexp_ready, 1)
                if st.has(1):
                    after(act, nmp_ps, g(1) + 1)
                    after(act, gates_ps, g(-1) + 1)
                    act.activation(nmph[st.side(1)], bank[6][:, :], ACT.Copy, scale=1.0 / WS).then_inc(nmph_ready, 1)

            gnn_loop(act, body)

            act.wait_ge(table_ready, 1)
            for e in range(NE):
                row = act.value_load(fill_row[0:1, e:e + 1], min_val=0, max_val=NE * REGION - W)
                act.dma_start(routed[bass.ds(row, W), :].rearrange("(p r) c -> p r c", p=P), filler[:, :, :]).then_inc(fill_landed, 16)

            def silu(st, c):
                after(act, h13_ps, st.g() * EC + c + 1)
                act.activation(act1[c][0:HC, :], bank[2 * c][0:HC, :], ACT.Silu, scale=1.0 / WS).then_inc(act1_ready, 1)

            def tile_body(st):
                if st.has(0):
                    silu(st, 0)
                    silu(st, 1)
                if st.has(-1):
                    p = st.side(-1)
                    after(act, out_scattered[p], st.half(-1) * GB * 16)
                    after(act, y_ps, st.g(-1) + 1)
                    for b in range(GB):
                        ins = act.activation(yo[p][:, b, :], bank[7][:, b * P:(b + 1) * P], ACT.Identity, scale=tgate[p][:, b:b + 1])
                    ins.then_inc(yo_ready, 1)
                if st.has(1):
                    p = st.side(1)
                    after(act, tileT_ps, st.g(1) + 1)
                    after(act, h13_ps, (st.g(-1) + 1) * EC)
                    act.activation(tTh[p], bank[6][:, :], ACT.Copy).then_inc(tTh_ready, 1)
                if st.has(0):
                    silu(st, 2)

            tile_loop(act, tile_body)
            for n in range(NCH):
                act.wait_ge(summed, n + 1)
                act.dma_start(out_v[:, n * CG:(n + 1) * CG, :], xres[:, n * CG:(n + 1) * CG, :]).then_inc(out_stored, 16)
            act.wait_ge(out_stored, NCH * 16)

        @block.vector
        def _(dve):
            v = [0]

            def link(ins):
                v[0] += 1
                ins.then_inc(s_vec, 1)
                dve.wait_ge(s_vec, v[0])

            def low(n):
                hi, lo, srcs, m, w = jobs[n]
                dve.wait_ge(s_hi, n + 1)
                dve.scalar_tensor_tensor(out=lo, in0=bank[n % JB][0:m, 0:w * len(srcs)], scalar=WS, in1=hi,
                                         op0=ALU.mult, op1=ALU.subtract).then_inc(s_lo, 1)

            for n in range(len(jobs)):
                low(n)
            dve.wait_ge(s_hi, len(jobs) + 1)
            for q in (0, 32, 64):
                last = dve.scalar_tensor_tensor(out=wsel[:, q:q + 3], in0=bank[4][:, 0:3], scalar=WS, in1=wseh[:, q:q + 3],
                                                op0=ALU.mult, op1=ALU.subtract)
            last.then_inc(s_lo, 1)
            dve.tensor_copy(routerT[:, :], bank[5][:, 0:NE]).then_inc(s_lo, 1)
            link(dve.tensor_copy(vecs[:, :], bank[6][:, 0:VECS]))
            vv = vecs[:, 0:8].rearrange("p (n k) -> p n k", k=4)
            cc = coef[:, 0:4].rearrange("p (n k) -> p n k", k=2)
            link(dve.tensor_scalar(vtmp[:, 0:2], vv[:, :, 3], EPS, None, ALU.add))
            dve.wait_ge(s_vecp, 1)
            link(dve.tensor_tensor(vtmp[:, 0:2], vtmp[:, 4:6], vv[:, :, 0], ALU.mult))
            link(dve.tensor_tensor(vtmp[:, 2:4], vtmp[:, 0:2], vv[:, :, 2], ALU.mult))
            link(dve.tensor_tensor(cc[:, :, 1], vv[:, :, 1], vtmp[:, 2:4], ALU.subtract))
            link(dve.tensor_scalar(cc[:, :, 0], vtmp[:, 0:2], 1.0 / WS, None, ALU.mult))
            link(dve.tensor_tensor(vtmp[:, 6:8], vecs[:, 8:10], vecs[:, 11:13], ALU.add))
            link(dve.tensor_scalar(coef[:, BR:BZ + 1], vtmp[:, 6:8], 0.5, None, ALU.mult))
            link(dve.tensor_copy(coef[:, BIN:BIN + 1], vecs[:, 10:11]))
            link(dve.tensor_scalar(coef[:, BHN:BHN + 1], vecs[:, 13:14], 0.5, None, ALU.mult))
            link(dve.tensor_scalar(bse[:, 1:2], bse[:, 0:1], -2.0, None, ALU.mult))
            link(dve.tensor_scalar(bmraw[0:2, :], bmraw[0:2, :], WS, None, ALU.mult))
            link(dve.tensor_copy(bmh.bitcast(F16)[0:2, 0:W], bmraw[0:2, :]))
            link(dve.tensor_tensor(bml[0:2, :], bmraw[0:2, :], bmh.bitcast(F16)[0:2, 0:W], ALU.subtract))
            link(dve.tensor_scalar(bml[0:2, :], bml[0:2, :], ident[0:2, 1:2], None, ALU.mult))
            link(dve.scalar_tensor_tensor(out=bmsg[:, :], in0=bmh.bitcast(F16)[0:2, 0:W], scalar=ident[0:2, 0:1],
                                          in1=bml[0:2, :], op0=ALU.mult, op1=ALU.add))
            assert v[0] == VSTEPS, v[0]
            dve.wait_ge(s_const, 2)

            def ln1_before(st):
                return st.g() + 2 + max(0, st.g()) if st.bounded else st.g() * 2 + 2

            def ln2_before(st):
                return min(NG, st.g() + 2) + st.g() - 1 if st.bounded else st.g() * 2 + 1

            def stats(src, which, count, done):
                for b in range(GB):
                    ins = dve.bn_stats(bn6[which][:, b, :], src(b))
                ins.then_inc(ln_step, 1)
                after_apart(dve, ln_step, count * 2 + 1)
                for b in range(GB):
                    ins = dve.bn_aggr(mv[which][:, b, :], bn6[which][:, b, :])
                ins.then_inc(ln_step, 1)
                dve.wait_ge(ln_step, count * 2 + 2)
                dve.tensor_scalar(varp[which], mv[which][:, :, 1], EPS, None, ALU.add).then_inc(done, 1)

            def body(st):
                g = st.g
                if st.has(-1):
                    after(dve, hn_ready, g(-1) + 1)
                    after(dve, rt_ready, g(-1) + 1)
                    after(dve, npre_ready, g(-2) + 1)
                    dve.scalar_tensor_tensor(out=rhn, in0=rt, scalar=1.0, in1=hn, op0=ALU.add, op1=ALU.mult).then_inc(rhn_ready, 1)
                    after(dve, rhn_ready, g(-1) + 1)
                    after(dve, nn_ready, g(-2) + 1)
                    dve.scalar_tensor_tensor(out=npre, in0=bank[3][:, :], scalar=1.0 / WS, in1=rhn, op0=ALU.mult, op1=ALU.add).then_inc(npre_ready, 1)
                if st.has(1):
                    p = st.side(1)
                    after(dve, xT_ready, g(1) + 1)
                    after(dve, gates_ps, g(-1) + 1)
                    dve.tensor_copy(xTh[p], xT[p]).then_inc(xTh_ready, 1)
                    after(dve, xTh_ready, g(1) + 1)
                    dve.tensor_tensor(xTl[p], xT[p], xTh[p], ALU.subtract).then_inc(xTl_ready, 1)
                if st.has(-1):
                    after(dve, dxn_ready, g(-1) + 1)
                    after(dve, zt_ready, g(-1) + 1)
                    dve.scalar_tensor_tensor(out=zd, in0=zt, scalar=1.0, in1=dxn, op0=ALU.add, op1=ALU.mult).then_inc(zd_ready, 1)
                    after(dve, zd_ready, g(-1) + 1)
                    after(dve, gruT_ps, g(-2) + 1)
                    dve.scalar_tensor_tensor(out=gru, in0=zd, scalar=0.5, in1=nn, op0=ALU.mult, op1=ALU.add).then_inc(gru_ready, 1)
                if st.has(1):
                    p = st.side(1)
                    after(dve, h1_ready, g(1) + 1)
                    after(dve, conv2_ps, g(-1) + 1)
                    dve.tensor_copy(h1h[p], h1).then_inc(h1h_ready, 1)
                    after(dve, h1h_ready, g(1) + 1)
                    dve.tensor_tensor(h1l[p], h1, h1h[p], ALU.subtract).then_inc(h1l_ready, 1)
                    after(dve, msgh_ready, g(1) + 1)
                    dve.scalar_tensor_tensor(out=msgl, in0=bank[3][:, :], scalar=0.0, in1=msgh, op0=ALU.max, op1=ALU.subtract).then_inc(msgl_ready, 1)
                if st.has(-1):
                    p = st.side(-1)
                    after(dve, gruT_ps, g(-1) + 1)
                    res = xres[:, bass.ds(g(-1) * GB, GB), :]
                    dve.tensor_tensor(res, graphs(bank[6][:, :]), res, ALU.add).then_inc(x2_ready, 1)
                    after_apart(dve, x2_ready, g(-1) + 1)
                    stats(lambda b: xres[:, bass.ds(g(-1) * GB + b, 1), :].rearrange("p b c -> p (b c)"), 1, ln2_before(st), ln2_stats)
                if st.has(1):
                    after(dve, kern_ready, g(1) + 1)
                    after(dve, maskT_ps, g(1) + 1)
                    after(dve, Al_ready, g(0) + 1)
                    dve.tensor_tensor(A, bank[4][:, :], kern, ALU.mult).then_inc(A_ready, 1)
                    after(dve, A_ready, g(1) + 1)
                    after(dve, nmp_ps, g(0) + 1)
                    dve.tensor_copy(Ah, A).then_inc(Ah_ready, 1)
                if st.has(-1):
                    p = st.side(-1)
                    after(dve, ln2_rstd, g(-1) + 1)
                    after(dve, scattered[p], (st.half(-1)) * TOPK * GB * 16)
                    for b in range(GB):
                        src = xres[:, bass.ds(g(-1) * GB + b, 1), :].rearrange("p b c -> p (b c)")
                        ins = dve.tensor_scalar(rows[p][0][:, b, 0:P], src, mv[1][:, b, 0:1], rstd[1][:, b:b + 1], ALU.subtract, ALU.mult)
                    ins.then_inc(rows_ready, 1)
                    after(dve, rows_ready, g(-1) + 1)
                    dve.tensor_copy(rows[p][1][:, :, 0:P], rows[p][0][:, :, 0:P])
                    for c in range(TOPK):
                        ids = rows[p][c][:, :, P + 1]
                        dve.tensor_scalar(ids, ids, float(2 * W), None, ALU.add)
                if st.has(0):
                    after(dve, conv2_ps, g(0) + 1)
                    after(dve, y_ready, g(-1) + 1)
                    dve.scalar_tensor_tensor(out=ysum, in0=bank[0][:, :], scalar=coef[:, SC2:SC2 + 1], in1=xT[st.side(0)],
                                             op0=ALU.mult, op1=ALU.add).then_inc(ysum_ready, 1)
                    after(dve, y_ready, g(0) + 1)
                    after(dve, gates_ps, g(-1) + 1)
                    dve.tensor_copy(yh, y).then_inc(yh_ready, 1)
                    after(dve, yh_ready, g(0) + 1)
                    dve.tensor_tensor(yl, y, yh, ALU.subtract).then_inc(yl_ready, 1)
                if st.has(-1):
                    p = st.side(-1)
                    n = [0]

                    def step(ins):
                        n[0] += 1
                        ins.then_inc(route_step, 1)
                        dve.wait_ge(route_step, g(-1) * ROUTE_STEPS + n[0])

                    logits = bank[7][:, 0:GB * NE].rearrange("p (b e) -> p b e", b=GB)

                    def wide(a):
                        return a.unsqueeze(2).to_broadcast([P, GB, NE])

                    after(dve, logits_ps, g(-1) + 1)
                    step(dve.tensor_reduce(lmax, logits, AX.X, ALU.max))
                    dve.tensor_tensor(lshift, logits, wide(lmax), ALU.subtract).then_inc(lshift_ready, 1)
                    dve.wait_ge(lexp_ready, g(-1) + 1)
                    step(dve.tensor_reduce(lsum, lexp, AX.X, ALU.add))
                    step(dve.reciprocal(lrec, lsum))
                    step(dve.tensor_tensor(prob, lexp, wide(lrec), ALU.mult))
                    for c, (pk, kk, src) in enumerate(((p1, k1, prob), (p2, k2, prob2))):
                        step(dve.tensor_reduce(pk, src, AX.X, ALU.max))
                        step(dve.tensor_tensor(eq, src, wide(pk), ALU.is_equal))
                        step(dve.tensor_tensor(cand, eq, em[:, :, :], ALU.mult))
                        step(dve.tensor_reduce(kk, cand, AX.X, ALU.min))
                        step(dve.tensor_tensor(picks[p][:, c, :, :], em[:, :, :], wide(kk), ALU.is_equal))
                        if c == 0:
                            step(dve.scalar_tensor_tensor(out=prob2, in0=picks[p][:, 0, :, :], scalar=-2.0, in1=prob, op0=ALU.mult, op1=ALU.add))
                    dve.tensor_tensor(picked[p], picks[p][:, 0, :, :], picks[p][:, 1, :, :], ALU.add).then_inc(picks_ready, 1)
                    step(dve.tensor_tensor(den, p1, p2, ALU.add))
                    step(dve.tensor_scalar(den, den, 1e-9, None, ALU.add))
                    step(dve.reciprocal(dinv, den))
                    dve.tensor_tensor(rows[p][0][:, :, P], p1, dinv, ALU.mult)
                    dve.tensor_tensor(rows[p][1][:, :, P], p2, dinv, ALU.mult).then_inc(rows2_ready, 1)
                if st.has(1):
                    after(dve, nmph_ready, g(1) + 1)
                    dve.scalar_tensor_tensor(out=nmpl[st.side(1)], in0=bank[6][:, :], scalar=1.0 / WS, in1=nmph[st.side(1)],
                                             op0=ALU.mult, op1=ALU.subtract).then_inc(nmpl_ready, 1)
                if st.has(-1):
                    p = st.side(-1)
                    after(dve, rank_ps, g(-1) + 1)
                    step2 = step
                    step2(dve.tensor_reduce(pickedsum, picked[p].rearrange("p b e -> p e b"), AX.X, ALU.add))
                    step2(dve.tensor_tensor(carry[:, :], carry[:, :], pickedsum, ALU.add))
                    step2(dve.tensor_tensor(rk, bank[7][:, 64:64 + GB * NE].rearrange("p (b e) -> p b e", b=GB), region0[:, :, :], ALU.add))
                    for c in range(TOPK):
                        ins = dve.tensor_tensor(rank_of[:, c, :, :], picks[p][:, c, :, :], rk, ALU.mult)
                    step2(ins)
                    step(dve.tensor_reduce(slotf, rank_of, AX.X, ALU.add))
                    dve.tensor_copy(slot[p], slotf).then_inc(slots_ready, 1)
                    assert n[0] == ROUTE_STEPS, n[0]
                if st.has(2):
                    after_apart(dve, x_landed[st.side(2)], (st.half(2) + 1) * 16)
                    stats(lambda b: xres[:, bass.ds(g(2) * GB + b, 1), :].rearrange("p b c -> p (b c)"), 0, ln1_before(st), ln1_stats)
                    dve.wait_ge(ln1_rstd, g(2) + 1)
                    after(dve, xnT_ps, g(1) + 1)
                    for b in range(GB):
                        src = xres[:, bass.ds(g(2) * GB + b, 1), :].rearrange("p b c -> p (b c)")
                        ins = dve.tensor_scalar(xn[:, b * P:(b + 1) * P], src, mv[0][:, b, 0:1], rstd[0][:, b:b + 1], ALU.subtract, ALU.mult)
                    ins.then_inc(xn_ready, 1)

            gnn_loop(dve, body)

            k = [0]

            def tstep(ins):
                k[0] += 1
                ins.then_inc(table_step, 1)
                dve.wait_ge(table_step, k[0])

            def by_tile(a):
                return a.unsqueeze(1).to_broadcast([P, NT, NE])

            dve.wait_ge(totals_ps, 1)
            tstep(dve.tensor_copy(total, bank[0][:, 0:NE]))
            tstep(dve.tensor_tensor(fill_f, total, region0[:, 0, :], ALU.add))
            tstep(dve.tensor_copy(fill_row[:, :], fill_f))
            tstep(dve.tensor_scalar(totali, total, float(W - 1), None, ALU.add))
            tstep(dve.tensor_scalar(totali, totali, W.bit_length() - 1, None, ALU.arith_shift_right))
            tstep(dve.tensor_copy(tiles, totali))
            tstep(dve.tensor_tensor(tiles_le, upto[:, :, :], tiles.unsqueeze(1).to_broadcast([P, NE, NE]), ALU.mult))
            tstep(dve.tensor_reduce(tile_end, tiles_le, AX.X, ALU.add))
            tstep(dve.tensor_tensor(past, tilenum[:, :].unsqueeze(2).to_broadcast([P, NT, NE]), by_tile(tile_end), ALU.is_ge))
            tstep(dve.tensor_reduce(tile_e, past, AX.X, ALU.add))
            tstep(dve.tensor_tensor(pastn, past, by_tile(tiles), ALU.mult))
            tstep(dve.tensor_reduce(tile_s, pastn, AX.X, ALU.add))
            tstep(dve.tensor_tensor(tile_s, tilenum[:, :], tile_s, ALU.subtract))
            tstep(dve.tensor_scalar(tile_s, tile_s, float(W), None, ALU.mult))
            tstep(dve.scalar_tensor_tensor(out=tile_f, in0=tile_e, scalar=float(REGION), in1=tile_s, op0=ALU.mult, op1=ALU.add))
            tstep(dve.tensor_copy(tile_row[:, :], tile_f))
            tstep(dve.tensor_scalar(tile_e, tile_e, float(NE - 1), None, ALU.min))
            dve.tensor_copy(tile_exp[:, :], tile_e).then_inc(table_ready, 1)

            def hidden(st, c):
                p, n = st.side(0), st.g() * EC + c + 1
                after(dve, act1_ready, n)
                dve.scalar_tensor_tensor(out=hid[c][0:HC, :], in0=bank[2 * c + 1][0:HC, :], scalar=1.0 / WS, in1=act1[c][0:HC, :],
                                         op0=ALU.mult, op1=ALU.mult).then_inc(hid_ready, 1)
                after(dve, hid_ready, n)
                after(dve, y_ps, st.g(-2) + 1)
                dve.tensor_copy(hidh[p][c][0:HC, :], hid[c][0:HC, :]).then_inc(hidh_ready, 1)
                after(dve, hidh_ready, n)
                dve.tensor_tensor(hidl[p][c][0:HC, :], hid[c][0:HC, :], hidh[p][c][0:HC, :], ALU.subtract).then_inc(hidl_ready, 1)

            def tile_body(st):
                if st.has(0):
                    hidden(st, 0)
                    hidden(st, 1)
                if st.has(1):
                    p = st.side(1)
                    after(dve, tTh_ready, st.g(1) + 1)
                    dve.tensor_tensor(tTl[p], bank[6][:, :], tTh[p], ALU.subtract).then_inc(tTl_ready, 1)
                    after(dve, out_scattered[p], st.half(1) * GB * 16)
                    after(dve, yo_ready, st.g(-1) + 1)
                    after(dve, tile_landed[p], (st.half(1) + 1) * 16)
                    dve.tensor_scalar(tgate[p], tile[p][:, :, P], 1.0 / WS, None, ALU.mult)
                    dve.tensor_scalar(pad[p], tile[p][:, :, P + 1], float(TOPK * N), float(p * W), ALU.is_ge, ALU.mult).then_inc(meta_step, 1)
                    after(dve, meta_step, st.g(1) + 1)
                    dve.tensor_tensor(dest[p], tile[p][:, :, P + 1], pad[p], ALU.add).then_inc(meta_ready, 1)
                if st.has(0):
                    hidden(st, 2)

            tile_loop(dve, tile_body)
            for n in range(NCH):
                dve.wait_ge(chosen_landed[n % CB], (n // CB + 1) * TOPK * 16)
                o = xres[:, n * CG:(n + 1) * CG, :]
                dve.tensor_tensor(o, o, chosen[n % CB][0], ALU.add).then_inc(sum_step, 1)
                dve.wait_ge(sum_step, n + 1)
                dve.tensor_tensor(o, o, chosen[n % CB][1], ALU.add).then_inc(summed, 1)

        @block.tensor
        def _(pe):
            pe.wait_ge(s_rawg, RAWG)
            pe.wait_ge(s_cst, 5)
            for n, (hi, lo, srcs, m, w) in enumerate(jobs):
                if n == NGJ:
                    pe.wait_ge(s_raw, 16 * 7)
                if n >= JB:
                    pe.wait_ge(s_lo, n - JB + 1)
                for j, src in enumerate(srcs):
                    ins = pe.transpose(bank[n % JB][0:m, j * w:(j + 1) * w], src, ident[0:src.shape[0], 0:src.shape[0]])
                ins.then_inc(s_tp, 1)
            pe.transpose(bank[4][:, 0:3], wseraw[0:3, :], ident[0:3, 0:3])
            pe.transpose(bank[5][:, 0:NE], routraw[0:NE, :], ident[0:NE, 0:NE])
            pe.transpose(bank[6][:, 0:VECS], vecraw[0:VECS, :], ident[0:VECS, 0:VECS]).then_inc(s_tp, 1)

            pe.wait_ge(s_vec, VSTEPS)
            pe.wait_ge(s_lo, len(jobs) + 2)
            pe.wait_ge(s_const, 2)

            def product(o, wt, xh, xl, first, last):
                pe.matmul(o, gwh[:, wt, :], xh, start=first, stop=False)
                pe.matmul(o, gwh[:, wt, :], xl, start=False, stop=False)
                return pe.matmul(o, gwl[:, wt, :], xh, start=False, stop=last)

            taps = [HALF_TAPS] + [k for k in range(TAPS) if k != HALF_TAPS]

            def conv2(st, which):
                p = st.side(0)
                o = graphs(bank[0][:, :])
                for k in which:
                    s = k - HALF_TAPS
                    a, b = max(0, -s), min(P, P - s)
                    ins = product(o[:, :, a:b], CONV2 + k, graphs(h1h[p])[:, :, a + s:b + s], graphs(h1l[p])[:, :, a + s:b + s],
                                  k == taps[0], k == taps[-1])
                return ins

            def body(st):
                g = st.g
                if st.has(0):
                    after(pe, h1l_ready, g(0) + 1)
                    after(pe, ysum_ready, g(-1) + 1)
                    conv2(st, taps[0:6])
                if st.has(1):
                    after(pe, xn_ready, g(1) + 1)
                    after(pe, kern_ready, g(0) + 1)
                    for b in range(GB):
                        ins = pe.transpose(bank[5][:, b * P:(b + 1) * P], xn[:, b * P:(b + 1) * P], ident[:, :])
                    ins.then_inc(xnT_ps, 1)
                if st.has(0):
                    conv2(st, taps[6:11])
                if st.has(1):
                    p = st.side(1)
                    after(pe, xTl_ready, g(1) + 1)
                    after(pe, rt_ready, g(-1) + 1)
                    after(pe, h1_ready, g(0) + 1)
                    product(bank[1][:, :], CONV1, xTh[p], xTl[p], True, True).then_inc(conv1_ps, 1)
                    after(pe, zt_ready, g(-1) + 1)
                    pe.matmul(bank[2][0:67, :], wseh[:, :], xTh[p], start=True, stop=False)
                    pe.matmul(bank[2][0:67, :], wseh[:, :], xTl[p], start=False, stop=False)
                    pe.matmul(bank[2][0:67, :], wsel[:, :], xTh[p], start=False, stop=True).then_inc(s_ps, 1)
                    after(pe, npre_ready, g(-1) + 1)
                    pe.matmul(bank[3][:, :], ones[0:2, :], bmsg[:, :], start=True, stop=False)
                    for b in range(GB):
                        o = bank[3][:, b * P:(b + 1) * P]
                        th, tl = xTh[p][:, b * P:(b + 1) * P], xTl[p][:, b * P:(b + 1) * P]
                        pe.matmul(o, th, gwh[:, MSG, :], start=False, stop=False)
                        pe.matmul(o, th, gwl[:, MSG, :], start=False, stop=False)
                        ins = pe.matmul(o, tl, gwh[:, MSG, :], start=False, stop=b == GB - 1)
                    ins.then_inc(msg_ps, 1)
                if st.has(-1):
                    after(pe, gru_ready, g(-1) + 1)
                    after(pe, nmpl_ready, g(0) + 1 if st.has(0) else NG)
                    for b in range(GB):
                        ins = pe.transpose(bank[6][:, b * P:(b + 1) * P], gru[:, b * P:(b + 1) * P], ident[:, :])
                    ins.then_inc(gruT_ps, 1)
                if st.has(0):
                    conv2(st, taps[11:14])
                if st.has(1):
                    p = st.side(1)
                    after(pe, adj_landed[p], (st.half(1) + 1) * 16)
                    after(pe, hn_ready, g(-1) + 1)
                    for b in range(GB):
                        ins = pe.transpose(bank[4][:, b * P:(b + 1) * P], adjb[p][:, b, :], ident[:, :])
                    ins.then_inc(maskT_ps, 1)
                    after(pe, sLR_ready, g(1) + 1)
                    after(pe, xT_ready, g(1) + 1)
                    for b in range(GB):
                        cols = slice(b * P, (b + 1) * P)
                        ins = pe.matmul(bank[5][:, cols], sL[0:67, cols], sR[0:67, cols], start=True, stop=True)
                    ins.then_inc(dist_ps, 1)
                if st.has(0):
                    conv2(st, taps[14:17]).then_inc(conv2_ps, 1)
                if st.has(-1):
                    p = st.side(-1)
                    after(pe, rows_ready, g(-1) + 1)
                    after(pe, slots_ready, g(-2) + 1)
                    for b in range(GB):
                        ins = pe.transpose(bank[7][:, b * P:(b + 1) * P], rows[p][0][:, b, 0:P], ident[:, :])
                    ins.then_inc(xn2T_ps, 1)
                if st.has(0):
                    p = st.side(0)
                    if st.has(1):
                        after(pe, h1_ready, g(1) + 1)
                        after(pe, sLR_ready, g(1) + 1)
                    for gate, o in ((0, 1), (1, 2)):
                        product(bank[o][:, :], gate * 3 + 2, xTh[p], xTl[p], True, False)
                    for gate, o in ((0, 1), (1, 2)):
                        product(bank[o][:, :], gate * 3 + 1, nmph[p], nmpl[p], False, False)
                    if st.has(1):
                        after(pe, msgl_ready, g(1) + 1)
                    product(bank[3][:, :], 2 * 3 + 1, nmph[p], nmpl[p], True, False)
                if st.has(-1):
                    after(pe, xn2T_ready, g(-1) + 1)
                    for b in range(GB):
                        ins = pe.matmul(bank[7][:, b * NE:(b + 1) * NE], xn2T[:, b * P:(b + 1) * P], routerT[:, :], start=True, stop=True)
                    ins.then_inc(logits_ps, 1)
                if st.has(0):
                    if st.has(1):
                        after(pe, A_ready, g(1) + 1)
                    product(bank[4][:, :], 2 * 3 + 2, xTh[p], xTl[p], True, True).then_inc(hn_ps, 1)
                    after(pe, yl_ready, g(0) + 1)
                    for gate, o in ((0, 1), (1, 2), (2, 3)):
                        ins = product(bank[o][:, :], gate * 3, yh, yl, False, True)
                    ins.then_inc(gates_ps, 1)
                if st.has(1):
                    p = st.side(1)
                    after(pe, Al_ready, g(1) + 1)
                    if st.has(-1):
                        after(pe, x2_ready, g(-1) + 1)
                    for b in range(GB):
                        cols = slice(b * P, (b + 1) * P)
                        o = bank[6][:, cols]
                        pe.matmul(o, msgh[:, cols], Ah[:, cols], start=True, stop=False)
                        pe.matmul(o, msgh[:, cols], Al[:, cols], start=False, stop=False)
                        ins = pe.matmul(o, msgl[:, cols], Ah[:, cols], start=False, stop=True)
                    ins.then_inc(nmp_ps, 1)
                if st.has(-1):
                    p = st.side(-1)
                    after(pe, picks_ready, g(-1) + 1)
                    rank = bank[7][:, 64:64 + GB * NE].rearrange("p (b e) -> p b e", b=GB)
                    pk = picked[p]
                    pe.matmul(rank, tri[:, :], pk, start=True, stop=False)
                    pe.matmul(rank, ones[:, :], carry[:, :].unsqueeze(1).to_broadcast([P, GB, NE]), start=False, stop=False)
                    for d in range(1, GB):
                        ins = pe.matmul(rank[:, d:GB, :], ones[:, :], pk[:, 0:GB - d, :], start=False, stop=d == GB - 1)
                    ins.then_inc(rank_ps, 1)

            gnn_loop(pe, body)

            pe.wait_ge(slots_ready, NG)
            pe.matmul(bank[0][:, 0:NE], ones[:, :], carry[:, :], start=True, stop=True).then_inc(totals_ps, 1)
            pe.wait_ge(table_ready, 1)

            def chunk(st, c, e):
                p = st.side(0)
                if c == 0:
                    after(pe, tTl_ready, st.g() + 1)
                after(pe, hid_ready, st.g(-1) * EC + c + 1)
                for hi, lo, o in ((w1h, w1l, bank[2 * c]), (w3h, w3l, bank[2 * c + 1])):
                    at = bass.ds(e * (EC * HC) + c * HC, HC)
                    pe.matmul(o[0:HC, :], hi[:, at], tTh[p], start=True, stop=False)
                    pe.matmul(o[0:HC, :], hi[:, at], tTl[p], start=False, stop=False)
                    ins = pe.matmul(o[0:HC, :], lo[:, at], tTh[p], start=False, stop=True)
                ins.then_inc(h13_ps, 1)

            def load_expert(t):
                return pe.value_load(tile_exp[0:1, bass.ds(t, 1)], min_val=0, max_val=NE - 1)

            def tile_body(st):
                if st.has(0):
                    e = load_expert(st.g(0))
                    chunk(st, 0, e)
                    chunk(st, 1, e)
                if st.has(-1):
                    p = st.side(-1)
                    eb = load_expert(st.g(-1))
                    after(pe, hidl_ready, st.g(-1) * EC + EC)
                    after(pe, yo_ready, st.g(-2) + 1)
                    for b in range(GB):
                        o = bank[7][:, b * P:(b + 1) * P]
                        cols = slice(b * P, (b + 1) * P)
                        for c in range(EC):
                            at = bass.ds(eb * (EC * P) + c * P, P)
                            pe.matmul(o, hidh[p][c][0:HC, cols], w2h[0:HC, at], start=c == 0, stop=False)
                            pe.matmul(o, hidh[p][c][0:HC, cols], w2l[0:HC, at], start=False, stop=False)
                            ins = pe.matmul(o, hidl[p][c][0:HC, cols], w2h[0:HC, at], start=False, stop=c == EC - 1)
                    ins.then_inc(y_ps, 1)
                if st.has(1):
                    p = st.side(1)
                    after(pe, tile_landed[p], (st.half(1) + 1) * 16)
                    after(pe, tTl_ready, st.g(0) + 1)
                    for b in range(GB):
                        ins = pe.transpose(bank[6][:, b * P:(b + 1) * P], tile[p][:, b, 0:P], ident[:, :])
                    ins.then_inc(tileT_ps, 1)
                if st.has(0):
                    chunk(st, 2, e)

            tile_loop(pe, tile_body)


_INS = ["x", "adj"] + ["L0_gnn_" + n for n in (
    "w_se b_se conv1_w bn1_g bn1_b bn1_m bn1_v conv2_w bn2_g bn2_b bn2_m bn2_v w_msg b_msg w_ih b_ih w_hh b_hh").split()]
_INS += ["L0_ffn_" + n for n in "router_w w1 w2 w3".split()]
_OUTS = [((128, 128, 128), "float32")]


def kernel(**inputs):
    import numpy as _np
    import concourse.bacc as _bacc
    from concourse import mybir as _mybir
    from concourse.bass_utils import run_bass_kernel_spmd as _run

    nc = _bacc.Bacc("TRN2", target_bir_lowering=False, num_devices=1)
    arrays, args = {}, []
    for name in _INS:
        a = _np.ascontiguousarray(inputs[name])
        arrays[f"in_{name}_dram"] = a
        args.append(nc.dram_tensor(f"in_{name}_dram", a.shape, _mybir.dt.from_np(a.dtype), kind="ExternalInput").ap())
    for i, (shape, dtype) in enumerate(_OUTS):
        dt = _mybir.dt.from_np(_np.dtype(dtype))
        args.append(nc.dram_tensor(f"out_{i}_dram", shape, dt, kind="ExternalOutput").ap())
    build(nc, *args)
    r = _run(nc, [arrays], core_ids=[0])
    return r.results[0]["out_0_dram"]
```

```python
from contextlib import ExitStack

import concourse.bass as bass
from concourse import mybir

F32 = mybir.dt.float32
F16 = mybir.dt.float16
I32 = mybir.dt.int32
ALU = mybir.AluOpType
ACT = mybir.ActivationFunctionType
AX = mybir.AxisListType

P = 128
GB = 4
W = GB * P
WS = 16.0
EPS = 1e-5
TAPS = 17
HALF_TAPS = TAPS // 2
EC = 3
ROW = P + 2
VECS = 14


def build(nc, x, adj, w_se, b_se, conv1_w, bn1_g, bn1_b, bn1_m, bn1_v, conv2_w, bn2_g, bn2_b, bn2_m, bn2_v,
          w_msg, b_msg, w_ih, b_ih, w_hh, b_hh, router_w, w1, w2, w3, out):
    NB = x.shape[0]
    N = NB * P
    NG = NB // GB
    NE, H, _ = w1.shape
    HC = -(-H // EC)
    HL = H - (EC - 1) * HC
    TOPK = 2
    NT = N * TOPK // W + NE
    REGION = N + W
    XROWS = NE * REGION + NE * W
    assert out.shape[0] == N + W
    assert REGION % P == 0 and (NE - 1) * (REGION // P) + NB < 2048
    assert x.shape[1] == P and x.shape[2] == P and NG % 2 == 0 and NT % 2 == 0

    routed = nc.dram_tensor("routed", [XROWS, ROW], F32).ap()

    with ExitStack() as ctx:
        def sb(name, shape, dt=F32):
            return ctx.enter_context(nc.sbuf_tensor(name, shape, dt))

        def sem(name):
            return ctx.enter_context(nc.semaphore(name))

        xres = sb("xres", [P, NB, P])
        gwh = sb("gwh", [P, 28, P], F16)
        gwl = sb("gwl", [P, 28, P], F16)
        w1h = sb("w1h", [P, NE * EC * HC], F16)
        w1l = sb("w1l", [P, NE * EC * HC], F16)
        w3h = sb("w3h", [P, NE * EC * HC], F16)
        w3l = sb("w3l", [P, NE * EC * HC], F16)
        w2h = sb("w2h", [P, NE * EC * P], F16)
        w2l = sb("w2l", [P, NE * EC * P], F16)
        ident = sb("ident", [P, P])
        tri = sb("tri", [P, P], F16)
        ones = sb("ones", [P, P], F16)
        vecs = sb("vecs", [P, VECS])
        coef = sb("coef", [P, 12])
        bse = sb("bse", [P, 2])
        wseh = sb("wseh", [P, 67], F16)
        wsel = sb("wsel", [P, 67], F16)
        routerT = sb("routerT", [P, NE])
        bmsg = sb("bmsg", [2, W], F16)
        enum = sb("enum", [P, GB, NE])
        half = sb("half", [P, GB])
        carry = sb("carry", [P, NE], F16)
        filler = sb("filler", [P, GB, ROW])
        upto = sb("upto", [P, NE, NE])
        tilenum = sb("tilenum", [P, NT])
        tile_row = sb("tile_row", [P, NT], I32)
        tile_exp = sb("tile_exp", [P, NT], I32)
        fill_row = sb("fill_row", [P, NE], I32)
        arena = sb("arena", [P, 18560])

        RAWG = 16 * (7 + 8 + 13)
        VSTEPS = 16
        PICK_STEPS = 8
        SLOT_STEPS = 4
        spot = [0]

        def carve(cols, dt=F32):
            a = arena[:, spot[0]:spot[0] + cols]
            spot[0] += cols
            return a if dt == F32 else a.bitcast(dt)

        HP = EC * HC
        w1raw = carve(NE * EC * P).rearrange("p (t c) -> p t c", c=P)
        w3raw = carve(NE * EC * P).rearrange("p (t c) -> p t c", c=P)
        w2raw = carve(NE * HP).rearrange("p (e h) -> p e h", h=HP)
        c2raw = carve(P * TAPS).rearrange("p (c k) -> p c k", k=TAPS)
        wihraw = carve(6 * P).rearrange("p (t c) -> p t c", c=P)
        whhraw = carve(3 * P).rearrange("p (t c) -> p t c", c=P)
        c1raw = carve(P)
        msgraw = carve(P)
        vecraw = carve(P)
        wseraw = carve(P)
        routraw = carve(P)
        bmraw = carve(W)
        bmh = carve(W)
        bml = carve(W)
        vtmp = carve(8)

        spot[0] = 0
        adjb = [carve(W).rearrange("p (b c) -> p b c", b=GB) for _ in range(2)]
        xn = carve(W)
        xT = [carve(W) for _ in range(2)]
        xTh = [carve(W // 2, F16) for _ in range(2)]
        xTl = [carve(W // 2, F16) for _ in range(2)]
        h1 = carve(W)
        h1h = [carve(W // 2, F16) for _ in range(2)]
        h1l = [carve(W // 2, F16) for _ in range(2)]
        sL = carve(W)
        sR = carve(W)
        kern = carve(W)
        A = carve(W)
        Ah = carve(W // 2, F16)
        Al = carve(W // 2, F16)
        msgh = carve(W // 2, F16)
        msgl = carve(W // 2, F16)
        nmph = [carve(W // 2, F16) for _ in range(2)]
        nmpl = [carve(W // 2, F16) for _ in range(2)]
        ysum = carve(W)
        y = carve(W)
        yh = carve(W // 2, F16)
        yl = carve(W // 2, F16)
        rt = carve(W)
        zt = carve(W)
        hn = carve(W)
        rhn = carve(W)
        npre = carve(W)
        nn = carve(W)
        dxn = carve(W)
        zd = carve(W)
        gru = carve(W)
        rows = [[carve(GB * ROW).rearrange("p (b c) -> p b c", b=GB) for _ in range(TOPK)] for _ in range(2)]
        xn2T = carve(W)
        bn6 = [carve(GB * 6).rearrange("p (b c) -> p b c", b=GB) for _ in range(2)]
        mv = [carve(GB * 2).rearrange("p (b c) -> p b c", b=GB) for _ in range(2)]
        varp = [carve(GB) for _ in range(2)]
        rstd = [carve(GB) for _ in range(2)]

        def small(n=GB * NE):
            return carve(n).rearrange("p (b e) -> p b e", b=GB)

        lsum, lrec, den, dinv = [carve(GB) for _ in range(4)]
        top, lshift, lexp = [small() for _ in range(3)]
        topi = carve(GB * NE).bitcast(mybir.dt.uint32).rearrange("p (b e) -> p b e", b=GB)
        prob = carve(GB * TOPK).rearrange("p (b k) -> p b k", b=GB)
        picks = [carve(TOPK * GB * NE).rearrange("p (k b e) -> p k b e", k=TOPK, b=GB) for _ in range(2)]
        rank_of = carve(TOPK * GB * NE).rearrange("p (k b e) -> p k b e", k=TOPK, b=GB)
        picked = [carve(GB * NE // 2, F16).rearrange("p (b e) -> p b e", b=GB) for _ in range(2)]
        pickedsum = carve(NE)
        slotf = carve(TOPK * GB).rearrange("p (k b) -> p k b", k=TOPK)
        slot = [carve(TOPK * GB).bitcast(I32).rearrange("p (k b) -> p k b", k=TOPK) for _ in range(2)]

        spot[0] = 0
        total = carve(NE)
        totali = carve(NE).bitcast(I32)
        tiles = carve(NE)
        tiles_le = carve(NE * NE).rearrange("p (a e) -> p a e", e=NE)
        tile_end = carve(NE)
        past = carve(NT * NE).rearrange("p (t e) -> p t e", e=NE)
        pastn = carve(NT * NE).rearrange("p (t e) -> p t e", e=NE)
        tile_e = carve(NT)
        tile_s = carve(NT)
        tile_f = carve(NT)
        spot[0] = 2048
        tile = [carve(GB * ROW).rearrange("p (b c) -> p b c", b=GB) for _ in range(2)]
        tTh = [carve(W // 2, F16) for _ in range(2)]
        tTl = [carve(W // 2, F16) for _ in range(2)]
        act1 = [carve(W) for _ in range(EC)]
        hid = [carve(W) for _ in range(EC)]
        hidh = [[carve(W // 2, F16) for _ in range(EC)] for _ in range(2)]
        hidl = [[carve(W // 2, F16) for _ in range(EC)] for _ in range(2)]
        yo = [carve(W).rearrange("p (b c) -> p b c", b=GB) for _ in range(2)]
        meta = [carve(GB * 2).rearrange("p (b c) -> p b c", b=GB) for _ in range(2)]
        tgate = [carve(GB) for _ in range(2)]
        dest = [carve(GB).bitcast(I32) for _ in range(2)]

        bank = [ctx.enter_context(nc.psum_tensor(f"bank{i}", [P, W], F32)) for i in range(8)]

        def graphs(ap):
            return ap.rearrange("p (b c) -> p b c", b=GB)

        s_raw = sem("raw_landed")
        s_rawg = sem("raw_gnn_landed")
        s_zero = sem("raw_zeroed")
        s_const = sem("consts_ready")
        s_cst = sem("const_step")
        s_tp = sem("weights_transposed")
        s_hi = sem("weights_high")
        s_lo = sem("weights_low")
        s_vec = sem("vecs_step")
        s_vecp = sem("vec_power")

        gsrc = []
        for gate in range(3):
            gsrc += [wihraw[:, 2 * gate, :], wihraw[:, 2 * gate + 1, :], whhraw[:, gate, :]]
        gsrc += [c1raw[:, :], msgraw[:, :]] + [c2raw[:, :, k] for k in range(TAPS)]
        CONV1, MSG, CONV2 = 9, 10, 11
        jobs = []
        for t in range(0, 28, 4):
            jobs.append((gwh[:, t:t + 4, :].rearrange("p t c -> p (t c)"), gwl[:, t:t + 4, :].rearrange("p t c -> p (t c)"), gsrc[t:t + 4], P, P))
        for raw, hi, lo in ((w1raw, w1h, w1l), (w3raw, w3h, w3l)):
            for t in range(0, NE * EC, 4):
                jobs.append((hi[:, t * HC:(t + 4) * HC], lo[:, t * HC:(t + 4) * HC],
                             [raw[0:HC, t + j, :] for j in range(4)], P, HC))
        for t in range(0, NE * EC, 4):
            jobs.append((w2h[0:HC, t * P:(t + 4) * P], w2l[0:HC, t * P:(t + 4) * P],
                         [w2raw[:, (t + j) // EC, (t + j) % EC * HC:((t + j) % EC + 1) * HC] for j in range(4)], HC, P))
        NGJ = 7
        JB = 4

        ctxb = ctx.enter_context(nc.Block())
        block = ctxb

        x_landed = [sem(f"x_landed{i}") for i in range(2)]
        adj_landed = [sem(f"adj_landed{i}") for i in range(2)]
        (ln1_stats, ln1_rstd, xn_ready, xnT_ps, xT_ready, xTh_ready, xTl_ready, conv1_ps, h1_ready, h1h_ready,
         h1l_ready, s_ps, sLR_ready, msg_ps, msgh_ready, msgl_ready, maskT_ps, dist_ps, kern_ready, A_ready,
         Ah_ready, Al_ready, nmp_ps, nmph_ready, nmpl_ready, conv2_ps, ysum_ready, y_ready, yh_ready, yl_ready,
         hn_ps, gates_ps, rt_ready, zt_ready, hn_ready, rhn_ready, npre_ready, nn_ready, dxn_ready, zd_ready,
         gru_ready, gruT_ps, x2_ready, ln2_stats, ln2_rstd, rows_ready, xn2T_ps, xn2T_ready,
         logits_ps, lshift_ready, lexp_ready, picks_ready, rank_ps, slots_ready) = [sem(n) for n in (
            "ln1_stats ln1_rstd xn_ready xnT_ps xT_ready xTh_ready xTl_ready conv1_ps h1_ready h1h_ready "
            "h1l_ready s_ps sLR_ready msg_ps msgh_ready msgl_ready maskT_ps dist_ps kern_ready A_ready "
            "Ah_ready Al_ready nmp_ps nmph_ready nmpl_ready conv2_ps ysum_ready y_ready yh_ready yl_ready "
            "hn_ps gates_ps rt_ready zt_ready hn_ready rhn_ready npre_ready nn_ready dxn_ready zd_ready "
            "gru_ready gruT_ps x2_ready ln2_stats ln2_rstd rows_ready xn2T_ps xn2T_ready "
            "logits_ps lshift_ready lexp_ready picks_ready rank_ps slots_ready").split()]
        ln_step = sem("ln_step")
        pick_step = sem("pick_step")
        slot_step = sem("slot_step")
        scattered = [sem(f"scattered{i}") for i in range(2)]
        routed_landed = sem("routed_landed")
        table_step = sem("table_step")
        totals_ps = sem("totals_ps")
        table_ready = sem("table_ready")
        fill_landed = sem("fill_landed")
        tile_landed = [sem(f"tile_landed{i}") for i in range(2)]
        (tileT_ps, meta_taken, meta_ready, tTh_ready, tTl_ready, h13_ps, act1_ready, hid_ready, hidh_ready,
         hidl_ready, y_ps, yo_ready) = [sem("tile_" + n) for n in (
            "tileT_ps meta_taken meta_ready tTh_ready tTl_ready h13_ps act1_ready hid_ready hidh_ready "
            "hidl_ready y_ps yo_ready").split()]
        out_scattered = [sem(f"out_scattered{i}") for i in range(2)]
        x2_stored = sem("x2_stored")
        out_v = out[0:N, :].rearrange("(b n) c -> n b c", n=P)

        def after(eng, s, n):
            if isinstance(n, int) and n <= 0:
                return
            eng.wait_ge(s, n)

        waited_apart = sem("waited_apart")

        def after_apart(eng, s, n):
            after(eng, s, n)
            if not isinstance(n, int):
                eng.sem_inc(waited_apart, 1)

        class Step:

            def __init__(self, i, par, bounded, total):
                self.i, self.par, self.bounded, self.total = i, par, bounded, total

            def g(self, off=0):
                return self.i * 2 + (self.par + off)

            def half(self, off=0):
                return self.i + (self.par + off) // 2

            def side(self, off=0):
                return (self.par + off) % 2

            def has(self, off=0):
                return not self.bounded or 0 <= self.g(off) < self.total

        def gnn_loop(eng, body):
            for g in range(-2, 4):
                body(Step(g // 2, g % 2, True, NG))
            with eng.Fori(2, NG // 2 - 1) as i:
                body(Step(i, 0, False, NG))
                body(Step(i, 1, False, NG))
            for g in range(NG - 2, NG + 2):
                body(Step(g // 2, g % 2, True, NG))

        def tile_loop(eng, body):
            for t in range(-1, 4):
                body(Step(t // 2, t % 2, True, NT))
            with eng.Fori(2, NT // 2 - 1) as i:
                body(Step(i, 0, False, NT))
                body(Step(i, 1, False, NT))
            for t in range(NT - 2, NT + 1):
                body(Step(t // 2, t % 2, True, NT))

        x_v = x.rearrange("b n c -> n b c")
        adj_v = adj.rearrange("b n m -> n b m")

        SC1, SH1, SC2, SH2, BR, BZ, BIN, BHN = range(8)

        @block.sync
        def _(sp):
            n = 0
            for dst, src in (
                (wihraw, w_ih.rearrange("(g o) (h c) -> o g h c", o=P, c=P)),
                (whhraw, w_hh.rearrange("(g o) c -> o g c", o=P)),
                (c1raw, conv1_w.rearrange("o c k -> o (c k)")),
                (msgraw, w_msg),
                (c2raw, conv2_w),
                (wseraw[0:3, :], w_se),
                (routraw[0:NE, :], router_w),
            ):
                if dst is wihraw:
                    dst = wihraw.rearrange("p (g h) c -> p g h c", h=2)
                sp.dma_start(dst, src).then_inc(s_rawg, 16)
                n += 16
            for r, v in enumerate((bn1_g, bn1_b, bn1_m, bn1_v, bn2_g, bn2_b, bn2_m, bn2_v)):
                sp.dma_start(vecraw[r:r + 1, :], v.rearrange("(a c) -> a c", a=1)).then_inc(s_rawg, 16)
                n += 16
            sp.dma_start(vecraw[8:11, :], b_ih.rearrange("(g c) -> g c", c=P)).then_inc(s_rawg, 16)
            sp.dma_start(vecraw[11:14, :], b_hh.rearrange("(g c) -> g c", c=P)).then_inc(s_rawg, 16)
            sp.wait_ge(s_zero, 1)
            for q in (0, 32, 64):
                sp.dma_start(bse[q:q + 3, 0:1], b_se.rearrange("(c a) -> c a", a=1)).then_inc(s_rawg, 16)
            for r in range(2):
                for b in range(GB):
                    sp.dma_start(bmraw[r:r + 1, b * P:(b + 1) * P], b_msg.rearrange("(a c) -> a c", a=1)).then_inc(s_rawg, 16)
            n += 16 * 13
            assert n == RAWG
            for raw, src in ((w1raw, w1), (w3raw, w3)):
                rv = raw.rearrange("p (e k) c -> p e k c", k=EC)
                for k in range(EC):
                    hk = HC if k < EC - 1 else HL
                    sp.dma_start(rv[0:hk, :, k, :],
                                 src[:, k * HC:k * HC + hk, :].rearrange("e h c -> h e c")).then_inc(s_raw, 16)
            sp.dma_start(w2raw[:, :, 0:H], w2.rearrange("e c h -> c e h")).then_inc(s_raw, 16)
            sp.wait_ge(s_tp, len(jobs) + 1)

            def body(st):
                if st.has(2):
                    g, p = st.g(2), st.side(2)
                    after(sp, ln1_stats, st.g(0) + 1)
                    sp.dma_start(xres[:, bass.ds(g * GB, GB), :], x_v[:, bass.ds(g * GB, GB), :]).then_inc(x_landed[p], 16)
                    after(sp, maskT_ps, st.g(0) + 1)
                    sp.dma_start(adjb[p], adj_v[:, bass.ds(g * GB, GB), :]).then_inc(adj_landed[p], 16)

                if st.has(-2):
                    g2 = st.g(-2)
                    after(sp, x2_ready, g2 + 1)
                    sp.dma_start(out_v[:, bass.ds(g2 * GB, GB), :], xres[:, bass.ds(g2 * GB, GB), :]).then_inc(x2_stored, 16)

            gnn_loop(sp, body)

            sp.wait_ge(routed_landed, 1)
            sp.wait_ge(fill_landed, 2 * NE * 16)
            sp.wait_ge(table_ready, 1)

            def load_tile(st):
                p = st.side(0)
                after(sp, tileT_ps, st.g(-2) + 1)
                after(sp, meta_taken, st.g(-2) + 1)
                row = sp.value_load(tile_row[0:1, bass.ds(st.g(0), 1)], min_val=0, max_val=XROWS - W)
                sp.dma_start(tile[p], routed[bass.ds(row, W), :].rearrange("(p r) c -> p r c", p=P)).then_inc(tile_landed[p], 16)

            for t in range(2):
                load_tile(Step(0, t, True, NT))
            with sp.Fori(1, NT // 2) as i:
                load_tile(Step(i, 0, False, NT))
                load_tile(Step(i, 1, False, NT))

        @block.gpsimd
        def _(pool):
            k = [0]

            def link(ins):
                k[0] += 1
                ins.then_inc(s_cst, 1)
                pool.wait_ge(s_cst, k[0])

            for raw in (w1raw, w3raw):
                link(pool.memset(raw[96:HC, :, :].rearrange("p (e k) c -> p e k c", k=EC)[:, :, EC - 1, :], 0.0))
            link(pool.memset(bse[:, :], 0.0))
            pool.memset(w2raw[:, :, H:HP], 0.0).then_inc(s_zero, 1)
            pool.wait_ge(s_zero, 1)
            link(pool.memset(ident[:, :], 0.0))
            link(pool.affine_select(out=ident[:, :], in_=ident[:, :], compare_op=ALU.not_equal, fill=1.0, base=0,
                                    pattern=[[-1, P]], channel_multiplier=1))
            link(pool.memset(ones[:, :], 1.0))
            link(pool.affine_select(out=tri[:, :], in_=ones[:, :], compare_op=ALU.is_gt, fill=0.0, base=0,
                                    pattern=[[1, P]], channel_multiplier=-1))
            link(pool.memset(half[:, :], -0.5))
            link(pool.iota(rank_of[:, 0, :, :].bitcast(I32), pattern=[[0, GB], [1, NE]], base=0, channel_multiplier=0))
            link(pool.tensor_copy(enum[:, :, :], rank_of[:, 0, :, :].bitcast(I32)))
            link(pool.tensor_scalar(carry[:, :], enum[:, 0, :], float(REGION // P), None, ALU.mult))
            link(pool.memset(wseh[:, :], 0.0))
            link(pool.memset(filler[:, :, :], 0.0))
            link(pool.iota(rank_of[:, 1, 0, 0:GB].bitcast(I32), pattern=[[1, GB]], base=N, channel_multiplier=GB))
            link(pool.tensor_copy(filler[:, :, P + 1], rank_of[:, 1, 0, 0:GB].bitcast(I32)))
            link(pool.memset(upto[:, :, :], 1.0))
            link(pool.affine_select(out=upto[:, :, :], in_=upto[:, :, :], compare_op=ALU.is_ge, fill=0.0, base=0,
                                    pattern=[[1, NE], [-1, NE]], channel_multiplier=0))
            link(pool.iota(tile_row[:, :], pattern=[[1, NT]], base=0, channel_multiplier=0))
            link(pool.tensor_copy(tilenum[:, :], tile_row[:, :]))
            pool.memset(wsel[:, :], 0.0).then_inc(s_const, 1)
            pool.wait_ge(s_vec, 2)
            pool.tensor_tensor(vtmp[:, 4:6], vtmp[:, 0:2], half[:, 0:2], ALU.pow).then_inc(s_vecp, 1)
            pool.wait_ge(s_lo, len(jobs) + 2)
            k1_ = k[0]
            for p in range(2):
                for c in range(TOPK):
                    link(pool.iota(slot[p][:, c, :], pattern=[[P, GB]], base=(p - 2) * W, channel_multiplier=1))
                    link(pool.tensor_copy(rows[p][c][:, :, P + 1], slot[p][:, c, :]))
            link(pool.memset(sL[0:67, :], 0.0))
            link(pool.memset(sR[0:67, :], 0.0))
            link(pool.memset(sL[64:67, :], 1.0))
            pool.memset(sR[32:35, :], 1.0).then_inc(s_const, 1)
            pool.wait_ge(s_const, 2)

            def body(st):
                g = st.g
                def scatter(which):
                    if st.has(-2):
                        p = st.side(-2)
                        after_apart(pool, slots_ready, g(-2) + 1)
                        for c, b in which:
                            pool.indirect_dma_start(routed, bass.IndirectOffsetOnAxis(ap=slot[p][:, c, b:b + 1], axis=0),
                                                    rows[p][c][:, b, :], None).then_inc(scattered[p], 16)

                if st.has(-1):
                    after(pool, nn_ready, g(-1) + 1)
                    pool.tensor_tensor(dxn, xT[st.side(-1)], nn, ALU.subtract).then_inc(dxn_ready, 1)
                scatter([(0, b) for b in range(GB)])
                if st.has(2):
                    after(pool, ln1_stats, g(2) + 1)
                    pool.tensor_tensor(rstd[0], varp[0], half[:, :], ALU.pow).then_inc(ln1_rstd, 1)
                if st.has(-1):
                    after(pool, ln2_stats, g(-1) + 1)
                    pool.tensor_tensor(rstd[1], varp[1], half[:, :], ALU.pow).then_inc(ln2_rstd, 1)
                scatter([(1, b) for b in range(GB // 2)])
                if st.has(1):
                    after(pool, Ah_ready, g(1) + 1)
                    after(pool, nmp_ps, g(1))
                    pool.tensor_tensor(Al, A, Ah, ALU.subtract).then_inc(Al_ready, 1)
                scatter([(1, b) for b in range(GB // 2, GB)])

            gnn_loop(pool, body)
            for p in range(2):
                pool.wait_ge(scattered[p], NG // 2 * TOPK * GB * 16)
            pool.sem_inc(routed_landed, 1)

            def scatter_out(st):
                if st.has(-1):
                    p = st.side(-1)
                    if st.has(-2):
                        after(pool, out_scattered[st.side(-2)], (st.half(-2) + 1) * GB * 16)
                    after_apart(pool, yo_ready, st.g(-1) + 1)
                    for b in range(GB):
                        pool.indirect_dma_start(out, bass.IndirectOffsetOnAxis(ap=dest[p][:, b:b + 1], axis=0),
                                                yo[p][:, b, :], None, compute_op=ALU.add).then_inc(out_scattered[p], 16)

            pool.wait_ge(x2_stored, (NG + 1) * 16)
            tile_loop(pool, scatter_out)
            for p in range(2):
                pool.wait_ge(out_scattered[p], NT // 2 * GB * 16)

        @block.scalar
        def _(act):
            for n, (hi, lo, srcs, m, w) in enumerate(jobs):
                act.wait_ge(s_tp, n + 1)
                act.activation(hi, bank[n % JB][0:m, 0:w * len(srcs)], ACT.Copy, scale=WS).then_inc(s_hi, 1)
            act.wait_ge(s_tp, len(jobs) + 1)
            act.wait_ge(s_const, 1)
            for t in range(NE):
                r0 = NE * REGION + t * W
                act.dma_start(routed[r0:r0 + W, :].rearrange("(p r) c -> p r c", p=P), filler[:, :, :]).then_inc(fill_landed, 16)
            act.dma_start(out[N:N + W, :].rearrange("(p r) c -> p r c", p=P), filler[:, :, 0:P]).then_inc(x2_stored, 16)
            for q in (0, 32, 64):
                last = act.activation(wseh[:, q:q + 3], bank[4][:, 0:3], ACT.Copy, scale=WS)
            last.then_inc(s_hi, 1)

            act.wait_ge(s_vec, VSTEPS)
            act.wait_ge(s_const, 2)

            def body(st):
                g = st.g
                if st.has(-1):
                    after(act, gates_ps, g(-1) + 1)
                    act.activation(rt, bank[1][:, :], ACT.Tanh, bias=coef[:, BR:BR + 1], scale=0.5 / WS).then_inc(rt_ready, 1)
                if st.has(0):
                    after(act, nmp_ps, g(0) + 1)
                    after(act, gates_ps, g(-2) + 1)
                    act.activation(nmph[st.side(0)], bank[6][:, :], ACT.Copy, scale=1.0 / WS).then_inc(nmph_ready, 1)
                if st.has(-1):
                    after(act, zd_ready, g(-2) + 1)
                    act.activation(zt, bank[2][:, :], ACT.Tanh, bias=coef[:, BZ:BZ + 1], scale=0.5 / WS).then_inc(zt_ready, 1)
                    after(act, npre_ready, g(-1) + 1)
                    after(act, gru_ready, g(-2) + 1)
                    act.activation(nn, npre, ACT.Tanh, bias=coef[:, BIN:BIN + 1]).then_inc(nn_ready, 1)
                if st.has(1):
                    p = st.side(1)
                    after(act, xnT_ps, g(1) + 1)
                    after(act, gates_ps, g(-1) + 1)
                    act.activation(xTh[p], bank[5][:, :], ACT.Copy).then_inc(xTh_ready, 1)
                    after(act, dxn_ready, g(-1) + 1)
                    act.activation(xT[p], bank[5][:, :], ACT.Copy).then_inc(xT_ready, 1)
                    after(act, conv1_ps, g(1) + 1)
                    after(act, h1l_ready, g(0) + 1)
                    act.activation(h1, bank[1][:, :], ACT.Relu, bias=coef[:, SH1:SH1 + 1], scale=coef[:, SC1:SC1 + 1]).then_inc(h1_ready, 1)
                    after(act, conv2_ps, g(-1) + 1)
                    act.activation(h1h[p], bank[1][:, :], ACT.Relu, bias=coef[:, SH1:SH1 + 1], scale=coef[:, SC1:SC1 + 1]).then_inc(h1h_ready, 1)
                    after(act, s_ps, g(1) + 1)
                    after(act, dist_ps, g(0) + 1)
                    act.activation(sL[0:3, :], bank[2][0:3, :], ACT.Identity, bias=bse[0:3, 0:1], scale=1.0 / WS)
                    act.activation(sL[32:35, :], bank[2][32:35, :], ACT.Square, bias=bse[32:35, 0:1], scale=1.0 / WS)
                    act.activation(sR[0:3, :], bank[2][0:3, :], ACT.Identity, bias=bse[0:3, 1:2], scale=-2.0 / WS)
                    act.activation(sR[64:67, :], bank[2][64:67, :], ACT.Square, bias=bse[64:67, 0:1], scale=1.0 / WS).then_inc(sLR_ready, 1)
                    after(act, msg_ps, g(1) + 1)
                    after(act, nmp_ps, g(0) + 1)
                    act.activation(msgh, bank[3][:, :], ACT.Relu).then_inc(msgh_ready, 1)
                    after(act, dist_ps, g(1) + 1)
                    after(act, Al_ready, g(0) + 1)
                    act.activation(kern, bank[5][:, :], ACT.Exp, scale=-1.0).then_inc(kern_ready, 1)
                    after(act, A_ready, g(1) + 1)
                    act.activation(Ah, A, ACT.Copy).then_inc(Ah_ready, 1)
                if st.has(-1):
                    after(act, xn2T_ps, g(-1) + 1)
                    after(act, logits_ps, g(-2) + 1)
                    act.activation(xn2T, bank[7][:, :], ACT.Copy).then_inc(xn2T_ready, 1)
                if st.has(0):
                    after(act, ysum_ready, g(0) + 1)
                    after(act, yl_ready, g(-1) + 1)
                    act.activation(y, ysum, ACT.Relu, bias=coef[:, SH2:SH2 + 1]).then_inc(y_ready, 1)
                    after(act, gates_ps, g(-1) + 1)
                    act.activation(yh, ysum, ACT.Relu, bias=coef[:, SH2:SH2 + 1]).then_inc(yh_ready, 1)
                if st.has(-1):
                    after(act, lshift_ready, g(-1) + 1)
                    act.activation(lexp, lshift, ACT.Exp).then_inc(lexp_ready, 1)
                if st.has(0):
                    after(act, hn_ps, g(0) + 1)
                    after(act, rhn_ready, g(-1) + 1)
                    act.activation(hn, bank[4][:, :], ACT.Identity, bias=coef[:, BHN:BHN + 1], scale=0.5 / WS).then_inc(hn_ready, 1)

            gnn_loop(act, body)

            act.wait_ge(table_ready, 1)
            for e in range(NE):
                row = act.value_load(fill_row[0:1, e:e + 1], min_val=0, max_val=NE * REGION - W)
                act.dma_start(routed[bass.ds(row, W), :].rearrange("(p r) c -> p r c", p=P), filler[:, :, :]).then_inc(fill_landed, 16)

            def silu(st, c):
                after(act, h13_ps, st.g() * EC + c + 1)
                act.activation(act1[c][0:HC, :], bank[2 * c][0:HC, :], ACT.Silu, scale=1.0 / WS).then_inc(act1_ready, 1)

            def hidden_high(st, off, c):
                after(act, hid_ready, st.g(off) * EC + c + 1)
                after(act, y_ps, st.g(off - 2) + 1)
                act.activation(hidh[st.side(off)][c][0:HC, :], hid[c][0:HC, :], ACT.Copy).then_inc(hidh_ready, 1)

            def tile_body(st):
                if st.has(-1):
                    hidden_high(st, -1, 2)
                if st.has(0):
                    silu(st, 0)
                if st.has(1):
                    p = st.side(1)
                    after(act, tileT_ps, st.g(1) + 1)
                    after(act, h13_ps, (st.g(-1) + 1) * EC)
                    act.activation(tTh[p], bank[6][:, :], ACT.Copy).then_inc(tTh_ready, 1)
                if st.has(0):
                    hidden_high(st, 0, 0)
                    silu(st, 1)
                    hidden_high(st, 0, 1)
                if st.has(-1):
                    p = st.side(-1)
                    after(act, out_scattered[p], st.half(-1) * GB * 16)
                    after(act, y_ps, st.g(-1) + 1)
                    for b in range(GB):
                        ins = act.activation(yo[p][:, b, :], bank[7][:, b * P:(b + 1) * P], ACT.Identity, scale=tgate[p][:, b:b + 1])
                    ins.then_inc(yo_ready, 1)
                if st.has(0):
                    silu(st, 2)

            tile_loop(act, tile_body)

        @block.vector
        def _(dve):
            v = [0]

            def link(ins):
                v[0] += 1
                ins.then_inc(s_vec, 1)
                dve.wait_ge(s_vec, v[0])

            def low(n):
                hi, lo, srcs, m, w = jobs[n]
                dve.wait_ge(s_hi, n + 1)
                dve.scalar_tensor_tensor(out=lo, in0=bank[n % JB][0:m, 0:w * len(srcs)], scalar=WS, in1=hi,
                                         op0=ALU.mult, op1=ALU.subtract).then_inc(s_lo, 1)

            for n in range(len(jobs)):
                low(n)
            dve.wait_ge(s_hi, len(jobs) + 1)
            for q in (0, 32, 64):
                last = dve.scalar_tensor_tensor(out=wsel[:, q:q + 3], in0=bank[4][:, 0:3], scalar=WS, in1=wseh[:, q:q + 3],
                                                op0=ALU.mult, op1=ALU.subtract)
            last.then_inc(s_lo, 1)
            dve.tensor_copy(routerT[:, :], bank[5][:, 0:NE]).then_inc(s_lo, 1)
            link(dve.tensor_copy(vecs[:, :], bank[6][:, 0:VECS]))
            vv = vecs[:, 0:8].rearrange("p (n k) -> p n k", k=4)
            cc = coef[:, 0:4].rearrange("p (n k) -> p n k", k=2)
            link(dve.tensor_scalar(vtmp[:, 0:2], vv[:, :, 3], EPS, None, ALU.add))
            dve.wait_ge(s_vecp, 1)
            link(dve.tensor_tensor(vtmp[:, 0:2], vtmp[:, 4:6], vv[:, :, 0], ALU.mult))
            link(dve.tensor_tensor(vtmp[:, 2:4], vtmp[:, 0:2], vv[:, :, 2], ALU.mult))
            link(dve.tensor_tensor(cc[:, :, 1], vv[:, :, 1], vtmp[:, 2:4], ALU.subtract))
            link(dve.tensor_scalar(cc[:, :, 0], vtmp[:, 0:2], 1.0 / WS, None, ALU.mult))
            link(dve.tensor_tensor(vtmp[:, 6:8], vecs[:, 8:10], vecs[:, 11:13], ALU.add))
            link(dve.tensor_scalar(coef[:, BR:BZ + 1], vtmp[:, 6:8], 0.5, None, ALU.mult))
            link(dve.tensor_copy(coef[:, BIN:BIN + 1], vecs[:, 10:11]))
            link(dve.tensor_scalar(coef[:, BHN:BHN + 1], vecs[:, 13:14], 0.5, None, ALU.mult))
            link(dve.tensor_scalar(bse[:, 1:2], bse[:, 0:1], -2.0, None, ALU.mult))
            link(dve.tensor_scalar(bmraw[0:2, :], bmraw[0:2, :], WS, None, ALU.mult))
            link(dve.tensor_copy(bmh.bitcast(F16)[0:2, 0:W], bmraw[0:2, :]))
            link(dve.tensor_tensor(bml[0:2, :], bmraw[0:2, :], bmh.bitcast(F16)[0:2, 0:W], ALU.subtract))
            link(dve.tensor_scalar(bml[0:2, :], bml[0:2, :], ident[0:2, 1:2], None, ALU.mult))
            link(dve.scalar_tensor_tensor(out=bmsg[:, :], in0=bmh.bitcast(F16)[0:2, 0:W], scalar=ident[0:2, 0:1],
                                          in1=bml[0:2, :], op0=ALU.mult, op1=ALU.add))
            assert v[0] == VSTEPS, v[0]
            dve.wait_ge(s_const, 2)

            def ln1_before(st):
                return st.g() + 2 + max(0, st.g() - 1) if st.bounded else st.g() * 2 + 1

            def ln2_before(st):
                return min(NG, st.g() + 3) + st.g() - 1 if st.bounded else st.g() * 2 + 2

            def stats(src, which, count, done):
                for b in range(GB):
                    ins = dve.bn_stats(bn6[which][:, b, :], src(b))
                ins.then_inc(ln_step, 1)
                after_apart(dve, ln_step, count * 2 + 1)
                for b in range(GB):
                    ins = dve.bn_aggr(mv[which][:, b, :], bn6[which][:, b, :])
                ins.then_inc(ln_step, 1)
                dve.wait_ge(ln_step, count * 2 + 2)
                dve.tensor_scalar(varp[which], mv[which][:, :, 1], EPS, None, ALU.add).then_inc(done, 1)

            def body(st):
                g = st.g
                if st.has(-1):
                    after(dve, hn_ready, g(-1) + 1)
                    after(dve, rt_ready, g(-1) + 1)
                    after(dve, npre_ready, g(-2) + 1)
                    dve.scalar_tensor_tensor(out=rhn, in0=rt, scalar=1.0, in1=hn, op0=ALU.add, op1=ALU.mult).then_inc(rhn_ready, 1)
                    after(dve, rhn_ready, g(-1) + 1)
                    after(dve, nn_ready, g(-2) + 1)
                    dve.scalar_tensor_tensor(out=npre, in0=bank[3][:, :], scalar=1.0 / WS, in1=rhn, op0=ALU.mult, op1=ALU.add).then_inc(npre_ready, 1)
                if st.has(-2):
                    p = st.side(-2)
                    n2 = [0]

                    def place(ins):
                        n2[0] += 1
                        ins.then_inc(slot_step, 1)
                        return g(-2) * SLOT_STEPS + n2[0]

                    rank = bank[7][:, 64:64 + GB * NE].rearrange("p (b e) -> p b e", b=GB)
                    after(dve, rank_ps, g(-2) + 1)
                    n_rank = place(dve.tensor_tensor(rank_of, picks[p], rank.unsqueeze(1).to_broadcast([P, TOPK, GB, NE]), ALU.mult))
                    n_sum = place(dve.tensor_reduce(pickedsum, picked[p].rearrange("p b e -> p e b"), AX.X, ALU.add))
                    dve.wait_ge(slot_step, n_rank)
                    n_slot = place(dve.tensor_reduce(slotf, rank_of, AX.X, ALU.add))
                    dve.wait_ge(slot_step, n_sum)
                    place(dve.tensor_tensor(carry[:, :], carry[:, :], pickedsum, ALU.add))
                    dve.wait_ge(slot_step, n_slot)
                    dve.tensor_copy(slot[p], slotf).then_inc(slots_ready, 1)
                    assert n2[0] == SLOT_STEPS
                if st.has(0):
                    after(dve, nmph_ready, g(0) + 1)
                    dve.scalar_tensor_tensor(out=nmpl[st.side(0)], in0=bank[6][:, :], scalar=1.0 / WS, in1=nmph[st.side(0)],
                                             op0=ALU.mult, op1=ALU.subtract).then_inc(nmpl_ready, 1)
                if st.has(2):
                    after_apart(dve, x_landed[st.side(2)], (st.half(2) + 1) * 16)
                    stats(lambda b: xres[:, bass.ds(g(2) * GB + b, 1), :].rearrange("p b c -> p (b c)"), 0, ln1_before(st), ln1_stats)
                if st.has(1):
                    p = st.side(1)
                    after(dve, xT_ready, g(1) + 1)
                    dve.tensor_tensor(xTl[p], xT[p], xTh[p], ALU.subtract).then_inc(xTl_ready, 1)
                if st.has(-1):
                    after(dve, dxn_ready, g(-1) + 1)
                    after(dve, zt_ready, g(-1) + 1)
                    dve.scalar_tensor_tensor(out=zd, in0=zt, scalar=1.0, in1=dxn, op0=ALU.add, op1=ALU.mult).then_inc(zd_ready, 1)
                    after(dve, zd_ready, g(-1) + 1)
                    after(dve, gruT_ps, g(-2) + 1)
                    dve.scalar_tensor_tensor(out=gru, in0=zd, scalar=0.5, in1=nn, op0=ALU.mult, op1=ALU.add).then_inc(gru_ready, 1)
                if st.has(1):
                    p = st.side(1)
                    after(dve, h1h_ready, g(1) + 1)
                    dve.tensor_tensor(h1l[p], h1, h1h[p], ALU.subtract).then_inc(h1l_ready, 1)
                if st.has(-1):
                    after(dve, gruT_ps, g(-1) + 1)
                    res = xres[:, bass.ds(g(-1) * GB, GB), :]
                    dve.tensor_tensor(res, graphs(bank[6][:, :]), res, ALU.add).then_inc(x2_ready, 1)
                    after_apart(dve, x2_ready, g(-1) + 1)
                    stats(lambda b: xres[:, bass.ds(g(-1) * GB + b, 1), :].rearrange("p b c -> p (b c)"), 1, ln2_before(st), ln2_stats)
                if st.has(2):
                    dve.wait_ge(ln1_rstd, g(2) + 1)
                    after(dve, xnT_ps, g(1) + 1)
                    for b in range(GB):
                        src = xres[:, bass.ds(g(2) * GB + b, 1), :].rearrange("p b c -> p (b c)")
                        ins = dve.tensor_scalar(xn[:, b * P:(b + 1) * P], src, mv[0][:, b, 0:1], rstd[0][:, b:b + 1], ALU.subtract, ALU.mult)
                    ins.then_inc(xn_ready, 1)
                if st.has(-1):
                    p = st.side(-1)
                    after(dve, ln2_rstd, g(-1) + 1)
                    after(dve, scattered[p], (st.half(-1)) * TOPK * GB * 16)
                    for b in range(GB):
                        src = xres[:, bass.ds(g(-1) * GB + b, 1), :].rearrange("p b c -> p (b c)")
                        ins = dve.tensor_scalar(rows[p][0][:, b, 0:P], src, mv[1][:, b, 0:1], rstd[1][:, b:b + 1], ALU.subtract, ALU.mult)
                    ins.then_inc(rows_ready, 1)
                if st.has(1):
                    after(dve, msgh_ready, g(1) + 1)
                    dve.scalar_tensor_tensor(out=msgl, in0=bank[3][:, :], scalar=0.0, in1=msgh, op0=ALU.max, op1=ALU.subtract).then_inc(msgl_ready, 1)
                    after(dve, kern_ready, g(1) + 1)
                    after(dve, maskT_ps, g(1) + 1)
                    after(dve, Al_ready, g(0) + 1)
                    dve.tensor_tensor(A, bank[4][:, :], kern, ALU.mult).then_inc(A_ready, 1)
                if st.has(0):
                    after(dve, conv2_ps, g(0) + 1)
                    after(dve, yh_ready, g(-1) + 1)
                    dve.scalar_tensor_tensor(out=ysum, in0=bank[0][:, :], scalar=coef[:, SC2:SC2 + 1], in1=xT[st.side(0)],
                                             op0=ALU.mult, op1=ALU.add).then_inc(ysum_ready, 1)
                if st.has(-1):
                    after(dve, rows_ready, g(-1) + 1)
                    dve.tensor_copy(rows[p][1][:, :, 0:P], rows[p][0][:, :, 0:P])
                    for c in range(TOPK):
                        ids = rows[p][c][:, :, P + 1]
                        dve.tensor_scalar(ids, ids, float(2 * W), None, ALU.add)
                if st.has(0):
                    after(dve, yh_ready, g(0) + 1)
                    dve.tensor_tensor(yl, y, yh, ALU.subtract).then_inc(yl_ready, 1)
                if st.has(-1):
                    p = st.side(-1)
                    n = [0]

                    def step(ins):
                        n[0] += 1
                        ins.then_inc(pick_step, 1)
                        after_apart(dve, pick_step, g(-1) * PICK_STEPS + n[0])

                    logits = bank[7][:, 0:GB * NE].rearrange("p (b e) -> p b e", b=GB)
                    after_apart(dve, logits_ps, g(-1) + 1)
                    for b in range(GB):
                        ins = dve.max(top[:, b, :], logits[:, b, :])
                    step(ins)
                    dve.tensor_tensor(lshift, top, top[:, :, 0:1].to_broadcast([P, GB, NE]), ALU.subtract).then_inc(lshift_ready, 1)
                    for b in range(GB):
                        ins = dve.max_index(topi[:, b, :], top[:, b, :], logits[:, b, :])
                    step(ins)
                    step(dve.tensor_tensor(picks[p], enum[:, :, :].unsqueeze(1).to_broadcast([P, TOPK, GB, NE]),
                                           topi[:, :, 0:TOPK].rearrange("p b k -> p k b").unsqueeze(3).to_broadcast([P, TOPK, GB, NE]),
                                           ALU.is_equal))
                    dve.tensor_tensor(picked[p], picks[p][:, 0, :, :], picks[p][:, 1, :, :], ALU.add).then_inc(picks_ready, 1)
                    dve.wait_ge(lexp_ready, g(-1) + 1)
                    step(dve.tensor_reduce(lsum, lexp, AX.X, ALU.add))
                    step(dve.reciprocal(lrec, lsum))
                    step(dve.tensor_tensor(prob, lexp[:, :, 0:TOPK], lrec.unsqueeze(2).to_broadcast([P, GB, TOPK]), ALU.mult))
                    step(dve.scalar_tensor_tensor(out=den, in0=prob[:, :, 0], scalar=1e-9, in1=prob[:, :, 1], op0=ALU.add, op1=ALU.add))
                    step(dve.reciprocal(dinv, den))
                    dve.tensor_tensor(rows[p][0][:, :, P], prob[:, :, 0], dinv, ALU.mult)
                    dve.tensor_tensor(rows[p][1][:, :, P], prob[:, :, 1], dinv, ALU.mult)
                    assert n[0] == PICK_STEPS, n[0]

            gnn_loop(dve, body)

            k = [0]

            def tstep(ins):
                k[0] += 1
                ins.then_inc(table_step, 1)
                dve.wait_ge(table_step, k[0])

            def by_tile(a):
                return a.unsqueeze(1).to_broadcast([P, NT, NE])

            dve.wait_ge(totals_ps, 1)
            tstep(dve.tensor_copy(fill_row[:, :], bank[0][:, 0:NE]))
            tstep(dve.scalar_tensor_tensor(out=total, in0=enum[:, 0, :], scalar=float(-REGION), in1=bank[0][:, 0:NE],
                                           op0=ALU.mult, op1=ALU.add))
            tstep(dve.tensor_scalar(totali, total, float(W - 1), None, ALU.add))
            tstep(dve.tensor_scalar(totali, totali, W.bit_length() - 1, None, ALU.arith_shift_right))
            tstep(dve.tensor_copy(tiles, totali))
            tstep(dve.tensor_tensor(tiles_le, upto[:, :, :], tiles.unsqueeze(1).to_broadcast([P, NE, NE]), ALU.mult))
            tstep(dve.tensor_reduce(tile_end, tiles_le, AX.X, ALU.add))
            tstep(dve.tensor_tensor(past, tilenum[:, :].unsqueeze(2).to_broadcast([P, NT, NE]), by_tile(tile_end), ALU.is_ge))
            tstep(dve.tensor_reduce(tile_e, past, AX.X, ALU.add))
            tstep(dve.tensor_tensor(pastn, past, by_tile(tiles), ALU.mult))
            tstep(dve.tensor_reduce(tile_s, pastn, AX.X, ALU.add))
            tstep(dve.tensor_tensor(tile_s, tilenum[:, :], tile_s, ALU.subtract))
            tstep(dve.tensor_scalar(tile_s, tile_s, float(W), None, ALU.mult))
            tstep(dve.scalar_tensor_tensor(out=tile_f, in0=tile_e, scalar=float(REGION), in1=tile_s, op0=ALU.mult, op1=ALU.add))
            tstep(dve.tensor_copy(tile_row[:, :], tile_f))
            tstep(dve.tensor_scalar(tile_e, tile_e, float(NE - 1), None, ALU.min))
            dve.tensor_copy(tile_exp[:, :], tile_e).then_inc(table_ready, 1)

            def hidden(st, off, c):
                after(dve, act1_ready, st.g(off) * EC + c + 1)
                dve.scalar_tensor_tensor(out=hid[c][0:HC, :], in0=bank[2 * c + 1][0:HC, :], scalar=1.0 / WS, in1=act1[c][0:HC, :],
                                         op0=ALU.mult, op1=ALU.mult).then_inc(hid_ready, 1)

            def hidden_low(st, off, c):
                p = st.side(off)
                after(dve, hidh_ready, st.g(off) * EC + c + 1)
                dve.tensor_tensor(hidl[p][c][0:HC, :], hid[c][0:HC, :], hidh[p][c][0:HC, :], ALU.subtract).then_inc(hidl_ready, 1)

            def tile_body(st):
                if st.has(-1):
                    hidden(st, -1, 2)
                    hidden_low(st, -1, 2)
                if st.has(0):
                    hidden(st, 0, 0)
                if st.has(1):
                    p = st.side(1)
                    after(dve, tTh_ready, st.g(1) + 1)
                    dve.tensor_tensor(tTl[p], bank[6][:, :], tTh[p], ALU.subtract).then_inc(tTl_ready, 1)
                    after(dve, tile_landed[p], (st.half(1) + 1) * 16)
                    after(dve, meta_ready, st.g(-1) + 1)
                    dve.tensor_copy(meta[p][:, :, :], tile[p][:, :, P:P + 2]).then_inc(meta_taken, 1)
                if st.has(0):
                    hidden_low(st, 0, 0)
                    hidden(st, 0, 1)
                    hidden_low(st, 0, 1)
                    p = st.side(0)
                    after(dve, out_scattered[p], st.half(0) * GB * 16)
                    after(dve, yo_ready, st.g(-2) + 1)
                    after(dve, meta_taken, st.g(0) + 1)
                    dve.tensor_scalar(tgate[p], meta[p][:, :, 0], 1.0 / WS, None, ALU.mult)
                    dve.tensor_copy(dest[p], meta[p][:, :, 1]).then_inc(meta_ready, 1)

            tile_loop(dve, tile_body)

        @block.tensor
        def _(pe):
            pe.wait_ge(s_rawg, RAWG)
            pe.wait_ge(s_cst, 5)
            for n, (hi, lo, srcs, m, w) in enumerate(jobs):
                if n == NGJ:
                    pe.wait_ge(s_raw, 16 * 7)
                if n >= JB:
                    pe.wait_ge(s_lo, n - JB + 1)
                for j, src in enumerate(srcs):
                    ins = pe.transpose(bank[n % JB][0:m, j * w:(j + 1) * w], src, ident[0:src.shape[0], 0:src.shape[0]])
                ins.then_inc(s_tp, 1)
            pe.transpose(bank[4][:, 0:3], wseraw[0:3, :], ident[0:3, 0:3])
            pe.transpose(bank[5][:, 0:NE], routraw[0:NE, :], ident[0:NE, 0:NE])
            pe.transpose(bank[6][:, 0:VECS], vecraw[0:VECS, :], ident[0:VECS, 0:VECS]).then_inc(s_tp, 1)

            pe.wait_ge(s_vec, VSTEPS)
            pe.wait_ge(s_lo, len(jobs) + 2)
            pe.wait_ge(s_const, 2)

            def product(o, wt, xh, xl, first, last):
                pe.matmul(o, gwh[:, wt, :], xh, start=first, stop=False)
                pe.matmul(o, gwh[:, wt, :], xl, start=False, stop=False)
                return pe.matmul(o, gwl[:, wt, :], xh, start=False, stop=last)

            taps = [HALF_TAPS] + [k for k in range(TAPS) if k != HALF_TAPS]

            def conv2(st, which):
                p = st.side(0)
                o = graphs(bank[0][:, :])
                for k in which:
                    s = k - HALF_TAPS
                    a, b = max(0, -s), min(P, P - s)
                    ins = product(o[:, :, a:b], CONV2 + k, graphs(h1h[p])[:, :, a + s:b + s], graphs(h1l[p])[:, :, a + s:b + s],
                                  k == taps[0], k == taps[-1])
                return ins

            def body(st):
                g = st.g
                if st.has(0):
                    after(pe, h1l_ready, g(0) + 1)
                    after(pe, ysum_ready, g(-1) + 1)
                    conv2(st, taps[0:2])
                if st.has(-2):
                    p = st.side(-2)
                    after(pe, picks_ready, g(-2) + 1)
                    rank = bank[7][:, 64:64 + GB * NE].rearrange("p (b e) -> p b e", b=GB)
                    pk = picked[p]
                    pe.matmul(rank, tri[:, :], pk, start=True, stop=False)
                    pe.matmul(rank, ones[:, :], carry[:, :].unsqueeze(1).to_broadcast([P, GB, NE]), start=False, stop=False)
                    for d in range(1, GB):
                        ins = pe.matmul(rank[:, d:GB, :], ones[:, :], pk[:, 0:GB - d, :], start=False, stop=d == GB - 1)
                    ins.then_inc(rank_ps, 1)
                if st.has(0):
                    conv2(st, taps[2:6])
                if st.has(1):
                    after(pe, xn_ready, g(1) + 1)
                    after(pe, kern_ready, g(0) + 1)
                    for b in range(GB):
                        ins = pe.transpose(bank[5][:, b * P:(b + 1) * P], xn[:, b * P:(b + 1) * P], ident[:, :])
                    ins.then_inc(xnT_ps, 1)
                if st.has(0):
                    conv2(st, taps[6:11])
                if st.has(1):
                    p = st.side(1)
                    after(pe, xTl_ready, g(1) + 1)
                    after(pe, rt_ready, g(-1) + 1)
                    after(pe, h1_ready, g(0) + 1)
                    product(bank[1][:, :], CONV1, xTh[p], xTl[p], True, True).then_inc(conv1_ps, 1)
                    after(pe, zt_ready, g(-1) + 1)
                    pe.matmul(bank[2][0:67, :], wseh[:, :], xTh[p], start=True, stop=False)
                    pe.matmul(bank[2][0:67, :], wseh[:, :], xTl[p], start=False, stop=False)
                    pe.matmul(bank[2][0:67, :], wsel[:, :], xTh[p], start=False, stop=True).then_inc(s_ps, 1)
                    after(pe, npre_ready, g(-1) + 1)
                    pe.matmul(bank[3][:, :], ones[0:2, :], bmsg[:, :], start=True, stop=False)
                    for b in range(GB):
                        o = bank[3][:, b * P:(b + 1) * P]
                        th, tl = xTh[p][:, b * P:(b + 1) * P], xTl[p][:, b * P:(b + 1) * P]
                        pe.matmul(o, th, gwh[:, MSG, :], start=False, stop=False)
                        pe.matmul(o, th, gwl[:, MSG, :], start=False, stop=False)
                        ins = pe.matmul(o, tl, gwh[:, MSG, :], start=False, stop=b == GB - 1)
                    ins.then_inc(msg_ps, 1)
                if st.has(-1):
                    after(pe, gru_ready, g(-1) + 1)
                    after(pe, nmpl_ready, g(0) + 1 if st.has(0) else NG)
                    for b in range(GB):
                        ins = pe.transpose(bank[6][:, b * P:(b + 1) * P], gru[:, b * P:(b + 1) * P], ident[:, :])
                    ins.then_inc(gruT_ps, 1)
                if st.has(0):
                    conv2(st, taps[11:14])
                if st.has(1):
                    p = st.side(1)
                    after(pe, adj_landed[p], (st.half(1) + 1) * 16)
                    after(pe, hn_ready, g(-1) + 1)
                    for b in range(GB):
                        ins = pe.transpose(bank[4][:, b * P:(b + 1) * P], adjb[p][:, b, :], ident[:, :])
                    ins.then_inc(maskT_ps, 1)
                    after(pe, sLR_ready, g(1) + 1)
                    after(pe, xT_ready, g(1) + 1)
                    for b in range(GB):
                        cols = slice(b * P, (b + 1) * P)
                        ins = pe.matmul(bank[5][:, cols], sL[0:67, cols], sR[0:67, cols], start=True, stop=True)
                    ins.then_inc(dist_ps, 1)
                if st.has(0):
                    conv2(st, taps[14:17]).then_inc(conv2_ps, 1)
                if st.has(-1):
                    p = st.side(-1)
                    after(pe, rows_ready, g(-1) + 1)
                    after(pe, slots_ready, g(-2) + 1)
                    for b in range(GB):
                        ins = pe.transpose(bank[7][:, b * P:(b + 1) * P], rows[p][0][:, b, 0:P], ident[:, :])
                    ins.then_inc(xn2T_ps, 1)
                if st.has(0):
                    p = st.side(0)
                    if st.has(1):
                        after(pe, h1_ready, g(1) + 1)
                        after(pe, sLR_ready, g(1) + 1)
                    for gate, o in ((0, 1), (1, 2)):
                        product(bank[o][:, :], gate * 3 + 2, xTh[p], xTl[p], True, False)
                    for gate, o in ((0, 1), (1, 2)):
                        product(bank[o][:, :], gate * 3 + 1, nmph[p], nmpl[p], False, False)
                    if st.has(1):
                        after(pe, msgl_ready, g(1) + 1)
                    product(bank[3][:, :], 2 * 3 + 1, nmph[p], nmpl[p], True, False)
                if st.has(-1):
                    after(pe, xn2T_ready, g(-1) + 1)
                    for b in range(GB):
                        ins = pe.matmul(bank[7][:, b * NE:(b + 1) * NE], xn2T[:, b * P:(b + 1) * P], routerT[:, :], start=True, stop=True)
                    ins.then_inc(logits_ps, 1)
                if st.has(0):
                    if st.has(1):
                        after(pe, A_ready, g(1) + 1)
                    product(bank[4][:, :], 2 * 3 + 2, xTh[p], xTl[p], True, True).then_inc(hn_ps, 1)
                    after(pe, yl_ready, g(0) + 1)
                    for gate, o in ((0, 1), (1, 2), (2, 3)):
                        ins = product(bank[o][:, :], gate * 3, yh, yl, False, True)
                    ins.then_inc(gates_ps, 1)
                if st.has(1):
                    p = st.side(1)
                    after(pe, Al_ready, g(1) + 1)
                    if st.has(-1):
                        after(pe, x2_ready, g(-1) + 1)
                    for b in range(GB):
                        cols = slice(b * P, (b + 1) * P)
                        o = bank[6][:, cols]
                        pe.matmul(o, msgh[:, cols], Ah[:, cols], start=True, stop=False)
                        pe.matmul(o, msgh[:, cols], Al[:, cols], start=False, stop=False)
                        ins = pe.matmul(o, msgl[:, cols], Ah[:, cols], start=False, stop=True)
                    ins.then_inc(nmp_ps, 1)

            gnn_loop(pe, body)

            pe.wait_ge(slots_ready, NG)
            pe.matmul(bank[0][:, 0:NE], ones[:, :], carry[:, :], start=True, stop=True).then_inc(totals_ps, 1)
            pe.wait_ge(table_ready, 1)

            def chunk(st, c, e):
                p = st.side(0)
                if c == 0:
                    after(pe, tTl_ready, st.g() + 1)
                after(pe, hid_ready, st.g(-1) * EC + c + 1)
                for hi, lo, o in ((w1h, w1l, bank[2 * c]), (w3h, w3l, bank[2 * c + 1])):
                    at = bass.ds(e * (EC * HC) + c * HC, HC)
                    pe.matmul(o[0:HC, :], hi[:, at], tTh[p], start=True, stop=False)
                    pe.matmul(o[0:HC, :], hi[:, at], tTl[p], start=False, stop=False)
                    ins = pe.matmul(o[0:HC, :], lo[:, at], tTh[p], start=False, stop=True)
                ins.then_inc(h13_ps, 1)

            def load_expert(t):
                return pe.value_load(tile_exp[0:1, bass.ds(t, 1)], min_val=0, max_val=NE - 1)

            def tile_body(st):
                if st.has(0):
                    e = load_expert(st.g(0))
                    chunk(st, 0, e)
                if st.has(1):
                    p = st.side(1)
                    after(pe, tile_landed[p], (st.half(1) + 1) * 16)
                    after(pe, tTl_ready, st.g(0) + 1)
                    for b in range(GB):
                        ins = pe.transpose(bank[6][:, b * P:(b + 1) * P], tile[p][:, b, 0:P], ident[:, :])
                    ins.then_inc(tileT_ps, 1)
                if st.has(0):
                    chunk(st, 1, e)
                if st.has(-1):
                    p = st.side(-1)
                    eb = load_expert(st.g(-1))
                    after(pe, hidl_ready, st.g(-1) * EC + EC)
                    after(pe, yo_ready, st.g(-2) + 1)
                    for b in range(GB):
                        o = bank[7][:, b * P:(b + 1) * P]
                        cols = slice(b * P, (b + 1) * P)
                        for c in range(EC):
                            at = bass.ds(eb * (EC * P) + c * P, P)
                            pe.matmul(o, hidh[p][c][0:HC, cols], w2h[0:HC, at], start=c == 0, stop=False)
                            pe.matmul(o, hidh[p][c][0:HC, cols], w2l[0:HC, at], start=False, stop=False)
                            ins = pe.matmul(o, hidl[p][c][0:HC, cols], w2h[0:HC, at], start=False, stop=c == EC - 1)
                    ins.then_inc(y_ps, 1)
                if st.has(0):
                    chunk(st, 2, e)

            tile_loop(pe, tile_body)


_INS = ["x", "adj"] + ["L0_gnn_" + n for n in (
    "w_se b_se conv1_w bn1_g bn1_b bn1_m bn1_v conv2_w bn2_g bn2_b bn2_m bn2_v w_msg b_msg w_ih b_ih w_hh b_hh").split()]
_INS += ["L0_ffn_" + n for n in "router_w w1 w2 w3".split()]
_OUTS = [((128 * 128 + W, 128), "float32")]


def kernel(**inputs):
    import numpy as _np
    import concourse.bacc as _bacc
    from concourse import mybir as _mybir
    from concourse.bass_utils import run_bass_kernel_spmd as _run

    nc = _bacc.Bacc("TRN2", target_bir_lowering=False, num_devices=1)
    arrays, args = {}, []
    for name in _INS:
        a = _np.ascontiguousarray(inputs[name])
        arrays[f"in_{name}_dram"] = a
        args.append(nc.dram_tensor(f"in_{name}_dram", a.shape, _mybir.dt.from_np(a.dtype), kind="ExternalInput").ap())
    for i, (shape, dtype) in enumerate(_OUTS):
        dt = _mybir.dt.from_np(_np.dtype(dtype))
        args.append(nc.dram_tensor(f"out_{i}_dram", shape, dt, kind="ExternalOutput").ap())
    build(nc, *args)
    r = _run(nc, [arrays], core_ids=[0])
    return r.results[0]["out_0_dram"][0:128 * 128].reshape(128, 128, 128)
```

```python
from contextlib import ExitStack

import concourse.bass as bass
from concourse import mybir

F32 = mybir.dt.float32
F16 = mybir.dt.float16
I32 = mybir.dt.int32
ALU = mybir.AluOpType
ACT = mybir.ActivationFunctionType
AX = mybir.AxisListType

P = 128
GB = 4
W = GB * P
WS = 16.0
EPS = 1e-5
TAPS = 17
HALF_TAPS = TAPS // 2
EVEN_TAPS = HALF_TAPS // 2
HN = P // 2
GNW = 28 + 2 * EVEN_TAPS
TU = 8
EC = 3
ROW = P + 2
VECS = 14


def build(nc, x, adj, w_se, b_se, conv1_w, bn1_g, bn1_b, bn1_m, bn1_v, conv2_w, bn2_g, bn2_b, bn2_m, bn2_v,
          w_msg, b_msg, w_ih, b_ih, w_hh, b_hh, router_w, w1, w2, w3, out):
    NB = x.shape[0]
    N = NB * P
    NG = NB // GB
    NE, H, _ = w1.shape
    HC = -(-H // EC)
    HL = H - (EC - 1) * HC
    TOPK = 2
    NT = N * TOPK // W + NE
    REGION = N + W
    XROWS = NE * REGION + NE * W
    assert out.shape[0] == N + W
    assert REGION % P == 0 and (NE - 1) * (REGION // P) + NB < 2048
    assert x.shape[1] == P and x.shape[2] == P

    routed = nc.dram_tensor("routed", [XROWS, ROW], F32).ap()

    with ExitStack() as ctx:
        def sb(name, shape, dt=F32):
            return ctx.enter_context(nc.sbuf_tensor(name, shape, dt))

        def sem(name):
            return ctx.enter_context(nc.semaphore(name))

        xres = sb("xres", [P, NB, P])
        gwh = sb("gwh", [P, GNW, P], F16)
        gwl = sb("gwl", [P, GNW, P], F16)
        w1h = sb("w1h", [P, NE * EC * HC], F16)
        w1l = sb("w1l", [P, NE * EC * HC], F16)
        w3h = sb("w3h", [P, NE * EC * HC], F16)
        w3l = sb("w3l", [P, NE * EC * HC], F16)
        w2h = sb("w2h", [P, NE * EC * P], F16)
        w2l = sb("w2l", [P, NE * EC * P], F16)
        ident = sb("ident", [P, P])
        tri = sb("tri", [P, P], F16)
        ones = sb("ones", [P, P], F16)
        vecs = sb("vecs", [P, VECS])
        coef = sb("coef", [P, 12])
        bse = sb("bse", [P, 2])
        wseh = sb("wseh", [P, 67], F16)
        wsel = sb("wsel", [P, 67], F16)
        routerT = sb("routerT", [P, NE])
        bmsg = sb("bmsg", [2, P], F16)
        enum = sb("enum", [P, GB, NE])
        half = sb("half", [P, GB])
        carry = sb("carry", [P, NE], F16)
        filler = sb("filler", [P, GB, ROW])
        upto = sb("upto", [P, NE, NE])
        tilenum = sb("tilenum", [P, NT])
        tile_row = sb("tile_row", [P, NT], I32)
        tile_exp = sb("tile_exp", [P, NT], I32)
        table_probe = sb("table_probe", [P, 1])
        tile_apart = sb("tile_apart", [P, NT], I32)
        fill_row = sb("fill_row", [P, NE], I32)
        arena = sb("arena", [P, 17536])

        RAWG = 16 * 7
        RAWV = 16 * (8 + 2 + 3 + 1)
        VSTEPS = 12
        PICK_STEPS = 8
        SLOT_STEPS = 4
        spot = [0]

        def carve(cols, dt=F32):
            a = arena[:, spot[0]:spot[0] + cols]
            spot[0] += cols
            assert spot[0] <= arena.shape[1]
            return a if dt == F32 else a.bitcast(dt)

        HP = EC * HC
        room = xres[:, :, :].rearrange("p b c -> p (b c)")
        taken = [NB // 2 * P]

        def borrow(cols):
            a = room[:, taken[0]:taken[0] + cols]
            taken[0] += cols
            assert taken[0] <= NB * P
            return a

        c2raw = borrow(P * TAPS).rearrange("p (c k) -> p c k", k=TAPS)
        wihraw = borrow(6 * P).rearrange("p (t c) -> p t c", c=P)
        whhraw = borrow(3 * P).rearrange("p (t c) -> p t c", c=P)
        csum = borrow(P * 2 * EVEN_TAPS).rearrange("p (c k) -> p c k", k=2 * EVEN_TAPS)
        c1raw = borrow(P)
        msgraw = borrow(P)
        vecraw = borrow(P)
        wseraw = borrow(P)
        routraw = borrow(P)
        bmraw = borrow(P)
        bmh = borrow(P)
        bml = borrow(P)
        vtmp = borrow(8)
        taken[0] = 0
        w1raw = borrow(NE * EC * P).rearrange("p (t c) -> p t c", c=P)
        w3raw = borrow(NE * EC * P).rearrange("p (t c) -> p t c", c=P)
        w2raw = borrow(NE * HP).rearrange("p (e h) -> p e h", h=HP)
        FREED = -(-taken[0] // W)
        assert FREED <= NG - 4

        spot[0] = 0
        adjb = [carve(W).rearrange("p (b c) -> p b c", b=GB) for _ in range(2)]
        xn = carve(W)
        xT = [carve(W) for _ in range(2)]
        xTh = [carve(W // 2, F16) for _ in range(2)]
        xTl = [carve(W // 2, F16) for _ in range(2)]
        HP1 = HN + 1
        HG = GB * HP1
        late = w1h[:, :].bitcast(F32)
        h1 = late[:, 0:2 * HG + 2]
        hsum = late[:, 2 * HG + 2:3 * HG + 2]
        h1h = [w1l[:, i * (2 * HG + 2):(i + 1) * (2 * HG + 2)] for i in range(2)]
        hsumh = [w3h[:, i * HG:(i + 1) * HG] for i in range(2)]
        h1l = [w3l[:, i * (2 * HG + 2):(i + 1) * (2 * HG + 2)] for i in range(2)]
        hsuml = [w3h[:, (2 + i) * HG:(3 + i) * HG] for i in range(2)]

        def by_parity(a):
            return a.rearrange("p (t q) -> p t q", q=HG + 1)[:, :, 0:HG].rearrange("p t (b i) -> p t b i", i=HP1)[:, :, :, 0:HN]

        def parity_of(a, t):
            return a.rearrange("p (b i t) -> p t b i", b=GB, t=2)[:, t, :, :]

        sL = carve(W)
        sR = carve(W)
        kern = carve(W)
        A = carve(W)
        Ah = carve(W // 2, F16)
        Al = carve(W // 2, F16)
        msgh = carve(W // 2, F16)
        msgl = carve(W // 2, F16)
        nmph = [carve(W // 2, F16) for _ in range(2)]
        nmpl = [carve(W // 2, F16) for _ in range(2)]
        ysum = carve(W)
        y = carve(W)
        yh = carve(W // 2, F16)
        yl = carve(W // 2, F16)
        rt = carve(W)
        zt = carve(W)
        hn = carve(W)
        rhn = carve(W)
        npre = carve(W)
        nn = carve(W)
        dxn = carve(W)
        zd = carve(W)
        gru = carve(W)
        rows = [[carve(GB * ROW).rearrange("p (b c) -> p b c", b=GB) for _ in range(TOPK)] for _ in range(2)]
        xn2T = carve(W)
        bn6 = [carve(GB * 6).rearrange("p (b c) -> p b c", b=GB) for _ in range(2)]
        mv = [carve(GB * 2).rearrange("p (b c) -> p b c", b=GB) for _ in range(2)]
        varp = [carve(GB) for _ in range(2)]
        rstd = [carve(GB) for _ in range(2)]

        def small(n=GB * NE):
            return carve(n).rearrange("p (b e) -> p b e", b=GB)

        lsum, lrec, den, dinv = [carve(GB) for _ in range(4)]
        top, lshift, lexp = [small() for _ in range(3)]
        topi = carve(GB * NE).bitcast(mybir.dt.uint32).rearrange("p (b e) -> p b e", b=GB)
        prob = carve(GB * TOPK).rearrange("p (b k) -> p b k", b=GB)
        picks = [carve(TOPK * GB * NE).rearrange("p (k b e) -> p k b e", k=TOPK, b=GB) for _ in range(2)]
        rank_of = carve(TOPK * GB * NE).rearrange("p (k b e) -> p k b e", k=TOPK, b=GB)
        picked = [carve(GB * NE // 2, F16).rearrange("p (b e) -> p b e", b=GB) for _ in range(2)]
        pickedsum = carve(NE)
        slotf = carve(TOPK * GB).rearrange("p (k b) -> p k b", k=TOPK)
        slot = [carve(TOPK * GB).bitcast(I32).rearrange("p (k b) -> p k b", k=TOPK) for _ in range(2)]

        spot[0] = 0
        total = carve(NE)
        totali = carve(NE).bitcast(I32)
        tiles = carve(NE)
        tiles_le = carve(NE * NE).rearrange("p (a e) -> p a e", e=NE)
        tile_end = carve(NE)
        past = carve(NT * NE).rearrange("p (t e) -> p t e", e=NE)
        pastn = carve(NT * NE).rearrange("p (t e) -> p t e", e=NE)
        tile_e = carve(NT)
        tile_s = carve(NT)
        tile_f = carve(NT)
        spot[0] = 2048
        tile = [carve(GB * ROW).rearrange("p (b c) -> p b c", b=GB) for _ in range(2)]
        tTh = [carve(W // 2, F16) for _ in range(2)]
        tTl = [carve(W // 2, F16) for _ in range(2)]
        act1 = [carve(W) for _ in range(EC)]
        hid = [carve(W) for _ in range(EC)]
        hidh = [[carve(W // 2, F16) for _ in range(EC)] for _ in range(2)]
        hidl = [[carve(W // 2, F16) for _ in range(EC)] for _ in range(2)]
        yo = [carve(W).rearrange("p (b c) -> p b c", b=GB) for _ in range(2)]
        meta = [carve(GB * 2).rearrange("p (b c) -> p b c", b=GB) for _ in range(2)]
        tgate = [carve(GB) for _ in range(2)]
        dest = [carve(GB).bitcast(I32) for _ in range(2)]

        bank = [ctx.enter_context(nc.psum_tensor(f"bank{i}", [P, W], F32)) for i in range(8)]

        part_e = bank[0][:, 0:GB * HN].rearrange("p (b i) -> p b i", i=HN)
        part_o = bank[0][:, GB * HN:2 * GB * HN].rearrange("p (b i) -> p b i", i=HN)
        part_s = bank[7][:, 2 * P:2 * P + GB * HN].rearrange("p (b i) -> p b i", i=HN)
        part_t = bank[7][:, P + NE:P + NE + GB]
        totals = bank[7][:, 128:128 + NE]

        def graphs(ap):
            return ap.rearrange("p (b c) -> p b c", b=GB)

        s_raw = sem("raw_landed")
        s_rawg = sem("raw_gnn_landed")
        s_rawv = sem("raw_vectors_landed")
        s_zero = sem("raw_zeroed")
        expert_zero = sem("raw_experts_zeroed")
        s_const = sem("consts_ready")
        s_cst = sem("const_step")
        s_tp = sem("weights_transposed")
        s_hi = sem("weights_high")
        s_lo = sem("weights_low")
        s_vec = sem("vecs_step")
        bmsg_ready = sem("bmsg_ready")
        s_vecp = sem("vec_power")

        gsrc = []
        for gate in range(3):
            gsrc += [wihraw[:, 2 * gate, :], wihraw[:, 2 * gate + 1, :], whhraw[:, gate, :]]
        gsrc += [c1raw[:, :], msgraw[:, :]] + [c2raw[:, :, k] for k in range(TAPS)]
        gsrc += [csum[:, :, k] for k in range(2 * EVEN_TAPS)]
        CONV1, MSG, CONV2, CSUM = 9, 10, 11, 11 + TAPS
        assert len(gsrc) == GNW and GNW % 4 == 0
        jobs, expert_jobs = [], []
        for t in range(0, GNW, 4):
            jobs.append((gwh[:, t:t + 4, :].rearrange("p t c -> p (t c)"), gwl[:, t:t + 4, :].rearrange("p t c -> p (t c)"), gsrc[t:t + 4], P, P))
        for raw, hi, lo in ((w1raw, w1h, w1l), (w3raw, w3h, w3l)):
            for t in range(0, NE * EC, 4):
                expert_jobs.append((hi[:, t * HC:(t + 4) * HC], lo[:, t * HC:(t + 4) * HC],
                             [raw[0:HC, t + j, :] for j in range(4)], P, HC))
        for t in range(0, NE * EC, 4):
            expert_jobs.append((w2h[0:HC, t * P:(t + 4) * P], w2l[0:HC, t * P:(t + 4) * P],
                         [w2raw[:, (t + j) // EC, (t + j) % EC * HC:((t + j) % EC + 1) * HC] for j in range(4)], HC, P))
        JB = 4
        EH = (4, 7)
        EJB = (0, 4, 5)
        expert_tp = sem("expert_weights_transposed")
        expert_hi = sem("expert_weights_high")
        expert_lo = sem("expert_weights_low")

        ctxb = ctx.enter_context(nc.Block())
        block = ctxb

        x_landed = [sem(f"x_landed{i}") for i in range(2)]
        adj_landed = [sem(f"adj_landed{i}") for i in range(2)]
        (ln1_stats, ln1_rstd, xn_ready, xnT_ps, xT_ready, xTh_ready, xTl_ready, conv1_ps, h1_ready, h1h_ready,
         h1l_ready, s_ps, sLR_ready, msg_ps, msgh_ready, msgl_ready, maskT_ps, dist_ps, kern_ready, A_ready,
         Ah_ready, Al_ready, nmp_ps, nmph_ready, nmpl_ready, conv2_ps, ysum_ready, y_ready, yh_ready, yl_ready,
         hn_ps, gates_ps, rt_ready, zt_ready, hn_ready, rhn_ready, npre_ready, nn_ready, dxn_ready, zd_ready,
         gru_ready, gruT_ps, hsum_ready, hsumh_ready, hsuml_ready, conv2_parts_ps, x2_ready, ln2_stats, ln2_rstd, rows_ready, xn2T_ps, xn2T_ready,
         logits_ps, lshift_ready, lexp_ready, picks_ready, rank_ps, slots_ready) = [sem(n) for n in (
            "ln1_stats ln1_rstd xn_ready xnT_ps xT_ready xTh_ready xTl_ready conv1_ps h1_ready h1h_ready "
            "h1l_ready s_ps sLR_ready msg_ps msgh_ready msgl_ready maskT_ps dist_ps kern_ready A_ready "
            "Ah_ready Al_ready nmp_ps nmph_ready nmpl_ready conv2_ps ysum_ready y_ready yh_ready yl_ready "
            "hn_ps gates_ps rt_ready zt_ready hn_ready rhn_ready npre_ready nn_ready dxn_ready zd_ready "
            "gru_ready gruT_ps hsum_ready hsumh_ready hsuml_ready conv2_parts_ps x2_ready ln2_stats ln2_rstd rows_ready xn2T_ps xn2T_ready "
            "logits_ps lshift_ready lexp_ready picks_ready rank_ps slots_ready").split()]
        ln_step = sem("ln_step")
        pick_step = sem("pick_step")
        ysum_step = sem("ysum_step")
        csum_ready = sem("csum_ready")
        slot_step = sem("slot_step")
        scattered = [sem(f"scattered{i}") for i in range(2)]
        routed_landed = sem("routed_landed")
        table_step = sem("table_step")
        totals_ps = sem("totals_ps")
        table_ready = sem("table_ready")
        apart_ready = sem("apart_ready")
        fill_row_ready = sem("fill_row_ready")
        fill_landed = sem("fill_landed")
        tile_landed = [sem(f"tile_landed{i}") for i in range(2)]
        (tileT_ps, meta_taken, meta_ready, tTh_ready, tTl_ready, h13_ps, act1_ready, hid_ready, hidh_ready,
         hidl_ready, y_ps, yo_ready) = [sem("tile_" + n) for n in (
            "tileT_ps meta_taken meta_ready tTh_ready tTl_ready h13_ps act1_ready hid_ready hidh_ready "
            "hidl_ready y_ps yo_ready").split()]
        out_scattered = [sem(f"out_scattered{i}") for i in range(2)]
        x2_stored = sem("x2_stored")
        out_v = out[0:N, :].rearrange("(b n) c -> n b c", n=P)

        def after(eng, s, n):
            if isinstance(n, int) and n <= 0:
                return
            eng.wait_ge(s, n)

        waited_apart = sem("waited_apart")

        def after_apart(eng, s, n):
            after(eng, s, n)
            if not isinstance(n, int):
                eng.sem_inc(waited_apart, 1)

        class Step:

            def __init__(self, i, par, bounded, total, unrolled=2):
                self.i, self.par, self.bounded, self.total, self.unrolled = i, par, bounded, total, unrolled

            def g(self, off=0):
                return self.i * self.unrolled + (self.par + off)

            def half(self, off=0):
                return self.i * (self.unrolled // 2) + (self.par + off) // 2

            def side(self, off=0):
                return (self.par + off) % 2

            def has(self, off=0):
                return not self.bounded or 0 <= self.g(off) < self.total

        def pipeline(eng, body, total, start, end, unrolled):
            assert total % unrolled == 0
            for g in range(start, unrolled):
                body(Step(g // 2, g % 2, True, total))
            with eng.Fori(1, total // unrolled - 1) as i:
                for u in range(unrolled):
                    body(Step(i, u, False, total, unrolled))
            for g in range(total - unrolled, end):
                body(Step(g // 2, g % 2, True, total))

        def gnn_loop(eng, body, start=-2):
            pipeline(eng, body, NG, start, NG + 2, 4)

        def tile_loop(eng, body):
            pipeline(eng, body, NT, -1, NT + 1, TU)

        def at_end(st, off=0):
            return st.bounded and st.g() == NG + off

        x_v = x.rearrange("b n c -> n b c")
        adj_v = adj.rearrange("b n m -> n b m")

        SC1, SH1, SC2, SH2, BR, BZ, BIN, BHN, NSC2 = range(9)

        @block.sync
        def _(sp):
            for dst, src in (
                (wihraw.rearrange("p (g h) c -> p g h c", h=2), w_ih.rearrange("(g o) (h c) -> o g h c", o=P, c=P)),
                (whhraw, w_hh.rearrange("(g o) c -> o g c", o=P)),
                (c2raw, conv2_w),
                (c1raw, conv1_w.rearrange("o c k -> o (c k)")),
                (msgraw, w_msg),
                (wseraw[0:3, :], w_se),
                (routraw[0:NE, :], router_w),
            ):
                sp.dma_start(dst, src).then_inc(s_rawg, 16)

            def load_vectors():
                for row, v in enumerate((bn1_g, bn1_b, bn1_m, bn1_v, bn2_g, bn2_b, bn2_m, bn2_v)):
                    sp.dma_start(vecraw[row:row + 1, :], v.rearrange("(a c) -> a c", a=1)).then_inc(s_rawv, 16)
                sp.dma_start(vecraw[8:11, :], b_ih.rearrange("(g c) -> g c", c=P)).then_inc(s_rawv, 16)
                sp.dma_start(vecraw[11:14, :], b_hh.rearrange("(g c) -> g c", c=P)).then_inc(s_rawv, 16)
                sp.wait_ge(s_zero, 2)
                for q in (0, 32, 64):
                    sp.dma_start(bse[q:q + 3, 0:1], b_se.rearrange("(c a) -> c a", a=1)).then_inc(s_rawv, 16)
                sp.dma_start(bmraw[0:2, :], b_msg.rearrange("(a c) -> a c", a=1).to_broadcast([2, P])).then_inc(s_rawv, 16)

            def body(st):
                if st.has(2):
                    g, p = st.g(2), st.side(2)
                    after(sp, ln1_stats, st.g(0) + 1)
                    sp.dma_start(xres[:, bass.ds(g * GB, GB), :], x_v[:, bass.ds(g * GB, GB), :]).then_inc(x_landed[p], 16)
                    after(sp, maskT_ps, st.g(0) + 1)
                    sp.dma_start(adjb[p], adj_v[:, bass.ds(g * GB, GB), :]).then_inc(adj_landed[p], 16)

                if at_end(st, -2 - NG):
                    load_vectors()
                if at_end(st, 2 - NG):
                    sp.wait_ge(s_const, 1)
                    for t in range(NE):
                        r0 = NE * REGION + t * W
                        sp.dma_start(routed[r0:r0 + W, :].rearrange("(p r) c -> p r c", p=P), filler[:, :, :]).then_inc(fill_landed, 16)
                    sp.dma_start(out[N:N + W, :].rearrange("(p r) c -> p r c", p=P), filler[:, :, 0:P]).then_inc(x2_stored, 16)
                if at_end(st, -2):
                    sp.wait_ge(expert_zero, 3)
                    for raw, src in ((w1raw, w1), (w3raw, w3)):
                        rv = raw.rearrange("p (e k) c -> p e k c", k=EC)
                        for k in range(EC):
                            hk = HC if k < EC - 1 else HL
                            sp.dma_start(rv[0:hk, :, k, :],
                                         src[:, k * HC:k * HC + hk, :].rearrange("e h c -> h e c")).then_inc(s_raw, 16)
                    sp.dma_start(w2raw[:, :, 0:H], w2.rearrange("e c h -> c e h")).then_inc(s_raw, 16)
                if st.has(-2):
                    g2 = st.g(-2)
                    after(sp, x2_ready, g2 + 1)
                    sp.dma_start(out_v[:, bass.ds(g2 * GB, GB), :], xres[:, bass.ds(g2 * GB, GB), :]).then_inc(x2_stored, 16)

            gnn_loop(sp, body)

            sp.wait_ge(fill_row_ready, 1)
            for e in range(NE):
                row = sp.value_load(fill_row[0:1, e:e + 1], min_val=0, max_val=NE * REGION - W)
                sp.dma_start(routed[bass.ds(row, W), :].rearrange("(p r) c -> p r c", p=P), filler[:, :, :]).then_inc(fill_landed, 16)
            sp.wait_ge(routed_landed, 1)
            sp.wait_ge(fill_landed, 2 * NE * 16)
            sp.wait_ge(table_ready, 1)

            def load_tile(st):
                p = st.side(0)
                after(sp, tileT_ps, st.g(-2) + 1)
                after(sp, meta_taken, st.g(-2) + 1)
                row = sp.value_load(tile_row[0:1, bass.ds(st.g(0), 1)], min_val=0, max_val=XROWS - W)
                sp.dma_start(tile[p], routed[bass.ds(row, W), :].rearrange("(p r) c -> p r c", p=P)).then_inc(tile_landed[p], 16)

            for t in range(2):
                load_tile(Step(0, t, True, NT))
            with sp.Fori(1, NT // 2) as i:
                load_tile(Step(i, 0, False, NT))
                load_tile(Step(i, 1, False, NT))

        @block.gpsimd
        def _(pool):
            k = [0]

            def link(ins):
                k[0] += 1
                ins.then_inc(s_cst, 1)
                pool.wait_ge(s_cst, k[0])

            pool.memset(bse[:, :], 0.0).then_inc(s_zero, 1)
            pool.memset(half[:, :], -0.5).then_inc(s_zero, 1)
            pool.wait_ge(s_zero, 2)
            link(pool.memset(ident[:, :], 0.0))
            link(pool.affine_select(out=ident[:, :], in_=ident[:, :], compare_op=ALU.not_equal, fill=1.0, base=0,
                                    pattern=[[-1, P]], channel_multiplier=1))
            link(pool.memset(ones[:, :], 1.0))
            link(pool.affine_select(out=tri[:, :], in_=ones[:, :], compare_op=ALU.is_gt, fill=0.0, base=0,
                                    pattern=[[1, P]], channel_multiplier=-1))
            link(pool.iota(rank_of[:, 0, :, :].bitcast(I32), pattern=[[0, GB], [1, NE]], base=0, channel_multiplier=0))
            link(pool.tensor_copy(enum[:, :, :], rank_of[:, 0, :, :].bitcast(I32)))
            link(pool.tensor_scalar(carry[:, :], enum[:, 0, :], float(REGION // P), None, ALU.mult))
            link(pool.memset(wseh[:, :], 0.0))
            link(pool.memset(filler[:, :, :], 0.0))
            link(pool.iota(rank_of[:, 1, 0, 0:GB].bitcast(I32), pattern=[[1, GB]], base=N, channel_multiplier=GB))
            link(pool.tensor_copy(filler[:, :, P + 1], rank_of[:, 1, 0, 0:GB].bitcast(I32)))
            link(pool.memset(upto[:, :, :], 1.0))
            link(pool.affine_select(out=upto[:, :, :], in_=upto[:, :, :], compare_op=ALU.is_ge, fill=0.0, base=0,
                                    pattern=[[1, NE], [-1, NE]], channel_multiplier=0))
            link(pool.iota(tile_row[:, :], pattern=[[1, NT]], base=0, channel_multiplier=0))
            link(pool.tensor_copy(tilenum[:, :], tile_row[:, :]))
            pool.memset(wsel[:, :], 0.0).then_inc(s_const, 1)
            for p in range(2):
                for c in range(TOPK):
                    link(pool.iota(slot[p][:, c, :], pattern=[[P, GB]], base=(p - 2) * W, channel_multiplier=1))
                    link(pool.tensor_copy(rows[p][c][:, :, P + 1], slot[p][:, c, :]))
            link(pool.memset(h1, 0.0))
            link(pool.memset(sL[0:67, :], 0.0))
            link(pool.memset(sR[0:67, :], 0.0))
            link(pool.memset(sL[64:67, :], 1.0))
            pool.memset(sR[32:35, :], 1.0).then_inc(s_const, 1)
            pool.wait_ge(s_const, 2)

            def body(st):
                g = st.g
                if at_end(st, -2):
                    pool.wait_ge(x2_stored, (1 + NG - 4) * 16)
                    pool.wait_ge(Al_ready, g() + 1)
                    for n, raw in enumerate((w1raw, w3raw)):
                        pool.memset(raw[96:HC, :, :].rearrange("p (e k) c -> p e k c", k=EC)[:, :, EC - 1, :], 0.0).then_inc(expert_zero, 1)
                        pool.wait_ge(expert_zero, n + 1)
                    pool.memset(w2raw[:, :, H:HP], 0.0).then_inc(expert_zero, 1)
                    pool.wait_ge(expert_zero, 3)

                def scatter(which):
                    if st.has(-2):
                        p = st.side(-2)
                        after_apart(pool, slots_ready, g(-2) + 1)
                        for c, b in which:
                            pool.indirect_dma_start(routed, bass.IndirectOffsetOnAxis(ap=slot[p][:, c, b:b + 1], axis=0),
                                                    rows[p][c][:, b, :], None).then_inc(scattered[p], 16)

                if st.has(-1):
                    after(pool, nn_ready, g(-1) + 1)
                    pool.tensor_tensor(dxn, xT[st.side(-1)], nn, ALU.subtract).then_inc(dxn_ready, 1)
                scatter([(0, b) for b in range(GB)])
                if st.has(2):
                    after(pool, ln1_stats, g(2) + 1)
                    pool.tensor_tensor(rstd[0], varp[0], half[:, :], ALU.pow).then_inc(ln1_rstd, 1)
                if st.has(-1):
                    after(pool, ln2_stats, g(-1) + 1)
                    pool.tensor_tensor(rstd[1], varp[1], half[:, :], ALU.pow).then_inc(ln2_rstd, 1)
                scatter([(1, b) for b in range(GB // 2)])
                if st.has(1):
                    after(pool, Ah_ready, g(1) + 1)
                    after(pool, nmp_ps, g(1))
                    pool.tensor_tensor(Al, A, Ah, ALU.subtract).then_inc(Al_ready, 1)
                scatter([(1, b) for b in range(GB // 2, GB)])

            body(Step(-1, 0, True, NG))
            pool.wait_ge(s_rawv, RAWV)
            pool.wait_ge(ln1_rstd, 1)
            bmh16 = bmh.bitcast(F16)[0:2, 0:P]
            link(pool.tensor_scalar(bmraw[0:2, :], bmraw[0:2, :], WS, None, ALU.mult))
            link(pool.tensor_copy(bmh16, bmraw[0:2, :]))
            link(pool.tensor_tensor(bml[0:2, :], bmraw[0:2, :], bmh16, ALU.subtract))
            link(pool.tensor_scalar(bml[0:2, :], bml[0:2, :], ident[0:2, 1:2], None, ALU.mult))
            link(pool.tensor_scalar(bmraw[0:2, :], bmh16, ident[0:2, 0:1], None, ALU.mult))
            pool.tensor_tensor(bmsg[:, :], bmraw[0:2, :], bml[0:2, :], ALU.add).then_inc(bmsg_ready, 1)
            pool.wait_ge(bmsg_ready, 1)
            pool.wait_ge(s_vec, 2)
            pool.tensor_tensor(vtmp[:, 4:6], vtmp[:, 0:2], half[:, 0:2], ALU.pow).then_inc(s_vecp, 1)
            gnn_loop(pool, body, -1)
            for p in range(2):
                pool.wait_ge(scattered[p], NG // 2 * TOPK * GB * 16)
            pool.sem_inc(routed_landed, 1)

            def scatter_out(st):
                if st.has(-1):
                    p = st.side(-1)
                    if st.has(-2):
                        if st.bounded:
                            more = GB * 16
                        else:
                            more = pool.value_load(tile_apart[0:1, bass.ds(st.g(-1), 1)], min_val=0, max_val=GB * 16)
                        after(pool, out_scattered[st.side(-2)], st.half(-2) * GB * 16 + more)
                    after_apart(pool, yo_ready, st.g(-1) + 1)
                    for b in range(GB):
                        pool.indirect_dma_start(out, bass.IndirectOffsetOnAxis(ap=dest[p][:, b:b + 1], axis=0),
                                                yo[p][:, b, :], None, compute_op=ALU.add).then_inc(out_scattered[p], 16)

            pool.wait_ge(apart_ready, 1)
            pool.wait_ge(x2_stored, (NG + 1) * 16)
            tile_loop(pool, scatter_out)
            for p in range(2):
                pool.wait_ge(out_scattered[p], NT // 2 * GB * 16)

        @block.scalar
        def _(act):
            for n, (hi, lo, srcs, m, w) in enumerate(jobs):
                act.wait_ge(s_tp, n + 1)
                act.activation(hi, bank[n % JB][0:m, 0:w * len(srcs)], ACT.Copy, scale=WS).then_inc(s_hi, 1)
            act.wait_ge(s_tp, len(jobs) + 1)
            act.wait_ge(s_const, 1)
            for q in (0, 32, 64):
                last = act.activation(wseh[:, q:q + 3], bank[4][:, 0:3], ACT.Copy, scale=WS)
            last.then_inc(s_hi, 1)

            act.wait_ge(s_const, 2)

            done = [0]

            def expert_high(until):
                for n in range(done[0], until):
                    hi, lo, srcs, m, w = expert_jobs[n]
                    act.wait_ge(expert_tp, n + 1)
                    act.activation(hi, bank[EJB[n % len(EJB)]][0:m, 0:w * len(srcs)], ACT.Copy, scale=WS).then_inc(expert_hi, 1)
                done[0] = until

            def body(st):
                g = st.g
                if st.has(-1):
                    after(act, gates_ps, g(-1) + 1)
                    act.activation(rt, bank[1][:, :], ACT.Tanh, bias=coef[:, BR:BR + 1], scale=0.5 / WS).then_inc(rt_ready, 1)
                if st.has(0):
                    after(act, nmp_ps, g(0) + 1)
                    after(act, gates_ps, g(-2) + 1)
                    act.activation(nmph[st.side(0)], bank[6][:, :], ACT.Copy, scale=1.0 / WS).then_inc(nmph_ready, 1)
                if st.has(-1):
                    after(act, zd_ready, g(-2) + 1)
                    act.activation(zt, bank[2][:, :], ACT.Tanh, bias=coef[:, BZ:BZ + 1], scale=0.5 / WS).then_inc(zt_ready, 1)
                    after(act, npre_ready, g(-1) + 1)
                    after(act, gru_ready, g(-2) + 1)
                    act.activation(nn, npre, ACT.Tanh, bias=coef[:, BIN:BIN + 1]).then_inc(nn_ready, 1)
                if at_end(st):
                    expert_high(EH[0])
                if st.has(1):
                    p = st.side(1)
                    after(act, xnT_ps, g(1) + 1)
                    after(act, gates_ps, g(-1) + 1)
                    act.activation(xTh[p], bank[5][:, :], ACT.Copy).then_inc(xTh_ready, 1)
                    after(act, dxn_ready, g(-1) + 1)
                    act.activation(xT[p], bank[5][:, :], ACT.Copy).then_inc(xT_ready, 1)
                    if at_end(st, -1 - NG):
                        act.wait_ge(s_vec, VSTEPS)
                    after(act, conv1_ps, g(1) + 1)
                    after(act, hsum_ready, g(0) + 1)
                    act.activation(by_parity(h1), bank[1][:, :].rearrange("p (b i t) -> p t b i", b=GB, t=2), ACT.Relu, bias=coef[:, SH1:SH1 + 1], scale=coef[:, SC1:SC1 + 1]).then_inc(h1_ready, 1)
                    after(act, conv2_ps, g(-1) + 1)
                    act.activation(by_parity(h1h[p]), bank[1][:, :].rearrange("p (b i t) -> p t b i", b=GB, t=2), ACT.Relu, bias=coef[:, SH1:SH1 + 1], scale=coef[:, SC1:SC1 + 1]).then_inc(h1h_ready, 1)
                    after(act, s_ps, g(1) + 1)
                    after(act, dist_ps, g(0) + 1)
                    act.activation(sL[0:3, :], bank[2][0:3, :], ACT.Identity, bias=bse[0:3, 0:1], scale=1.0 / WS)
                    act.activation(sL[32:35, :], bank[2][32:35, :], ACT.Square, bias=bse[32:35, 0:1], scale=1.0 / WS)
                    act.activation(sR[0:3, :], bank[2][0:3, :], ACT.Identity, bias=bse[0:3, 1:2], scale=-2.0 / WS)
                    act.activation(sR[64:67, :], bank[2][64:67, :], ACT.Square, bias=bse[64:67, 0:1], scale=1.0 / WS).then_inc(sLR_ready, 1)
                if st.has(1):
                    p = st.side(1)
                    after(act, hsum_ready, g(1) + 1)
                    act.activation(hsumh[p], hsum, ACT.Copy).then_inc(hsumh_ready, 1)
                if st.has(1):
                    after(act, msg_ps, g(1) + 1)
                    after(act, nmp_ps, g(0) + 1)
                    act.activation(msgh, bank[3][:, :], ACT.Relu).then_inc(msgh_ready, 1)
                if st.has(1):
                    after(act, dist_ps, g(1) + 1)
                    after(act, Al_ready, g(0) + 1)
                    act.activation(kern, bank[5][:, :], ACT.Exp, scale=-1.0).then_inc(kern_ready, 1)
                if st.has(0):
                    after(act, ysum_ready, g(0) + 1)
                    after(act, yl_ready, g(-1) + 1)
                    act.activation(y, ysum, ACT.Relu, bias=coef[:, SH2:SH2 + 1]).then_inc(y_ready, 1)
                    after(act, gates_ps, g(-1) + 1)
                    act.activation(yh, ysum, ACT.Relu, bias=coef[:, SH2:SH2 + 1]).then_inc(yh_ready, 1)
                if st.has(-1):
                    after(act, xn2T_ps, g(-1) + 1)
                    after(act, logits_ps, g(-2) + 1)
                    act.activation(xn2T, bank[6][:, :], ACT.Copy).then_inc(xn2T_ready, 1)
                if st.has(1):
                    after(act, A_ready, g(1) + 1)
                    act.activation(Ah, A, ACT.Copy).then_inc(Ah_ready, 1)
                if at_end(st):
                    expert_high(EH[1])
                if st.has(-1):
                    after(act, lshift_ready, g(-1) + 1)
                    act.activation(lexp, lshift, ACT.Exp).then_inc(lexp_ready, 1)
                if st.has(0):
                    after(act, hn_ps, g(0) + 1)
                    after(act, rhn_ready, g(-1) + 1)
                    act.activation(hn, bank[4][:, :], ACT.Identity, bias=coef[:, BHN:BHN + 1], scale=0.5 / WS).then_inc(hn_ready, 1)

            gnn_loop(act, body)
            act.activation(table_probe[:, :], half[:, 0:1], ACT.Silu)
            expert_high(len(expert_jobs))

            def silu(st, c):
                after(act, h13_ps, st.g() * EC + c + 1)
                act.activation(act1[c][0:HC, :], bank[2 * c][0:HC, :], ACT.Silu, scale=1.0 / WS).then_inc(act1_ready, 1)

            def hidden_high(st, off, c):
                after(act, hid_ready, st.g(off) * EC + c + 1)
                after(act, y_ps, st.g(off - 2) + 1)
                act.activation(hidh[st.side(off)][c][0:HC, :], hid[c][0:HC, :], ACT.Copy).then_inc(hidh_ready, 1)

            def tile_body(st):
                if st.has(-1):
                    hidden_high(st, -1, 2)
                if st.has(0):
                    silu(st, 0)
                if st.has(1):
                    p = st.side(1)
                    after(act, tileT_ps, st.g(1) + 1)
                    after(act, h13_ps, (st.g(-1) + 1) * EC)
                    act.activation(tTh[p], bank[6][:, :], ACT.Copy).then_inc(tTh_ready, 1)
                if st.has(0):
                    hidden_high(st, 0, 0)
                    silu(st, 1)
                    hidden_high(st, 0, 1)
                    silu(st, 2)
                if st.has(-1):
                    p = st.side(-1)
                    after(act, out_scattered[p], st.half(-1) * GB * 16)
                    after(act, y_ps, st.g(-1) + 1)
                    after(act, meta_ready, st.g(-1) + 1)
                    for b in range(GB):
                        ins = act.activation(yo[p][:, b, :], bank[7][:, b * P:(b + 1) * P], ACT.Identity, scale=tgate[p][:, b:b + 1])
                    ins.then_inc(yo_ready, 1)

            tile_loop(act, tile_body)

        @block.vector
        def _(dve):
            v = [0]

            def link(ins):
                v[0] += 1
                ins.then_inc(s_vec, 1)
                dve.wait_ge(s_vec, v[0])

            def low(n):
                hi, lo, srcs, m, w = jobs[n]
                dve.wait_ge(s_hi, n + 1)
                dve.scalar_tensor_tensor(out=lo, in0=bank[n % JB][0:m, 0:w * len(srcs)], scalar=WS, in1=hi,
                                         op0=ALU.mult, op1=ALU.subtract).then_inc(s_lo, 1)

            done = [0]

            def expert_low(until):
                for n in range(done[0], until):
                    hi, lo, srcs, m, w = expert_jobs[n]
                    dve.wait_ge(expert_hi, n + 1)
                    dve.scalar_tensor_tensor(out=lo, in0=bank[EJB[n % len(EJB)]][0:m, 0:w * len(srcs)], scalar=WS, in1=hi,
                                             op0=ALU.mult, op1=ALU.subtract).then_inc(expert_lo, 1)
                done[0] = until

            def ln1_before(st):
                return st.g() + 2 + max(0, st.g() - 1) if st.bounded else st.g() * 2 + 1

            def ln2_before(st):
                return min(NG, st.g() + 3) + st.g() - 1 if st.bounded else st.g() * 2 + 2

            def stats(src, which, count, done):
                for b in range(GB):
                    ins = dve.bn_stats(bn6[which][:, b, :], src(b))
                ins.then_inc(ln_step, 1)
                after_apart(dve, ln_step, count * 2 + 1)
                for b in range(GB):
                    ins = dve.bn_aggr(mv[which][:, b, :], bn6[which][:, b, :])
                ins.then_inc(ln_step, 1)
                dve.wait_ge(ln_step, count * 2 + 2)
                dve.tensor_scalar(varp[which], mv[which][:, :, 1], EPS, None, ALU.add).then_inc(done, 1)

            def vectors():
                link(dve.tensor_copy(vecs[:, :], bank[6][:, 0:VECS]))
                vv = vecs[:, 0:8].rearrange("p (n k) -> p n k", k=4)
                cc = coef[:, 0:4].rearrange("p (n k) -> p n k", k=2)
                link(dve.tensor_scalar(vtmp[:, 0:2], vv[:, :, 3], EPS, None, ALU.add))
                dve.wait_ge(s_vecp, 1)
                link(dve.tensor_tensor(vtmp[:, 0:2], vtmp[:, 4:6], vv[:, :, 0], ALU.mult))
                link(dve.tensor_tensor(vtmp[:, 2:4], vtmp[:, 0:2], vv[:, :, 2], ALU.mult))
                link(dve.tensor_tensor(cc[:, :, 1], vv[:, :, 1], vtmp[:, 2:4], ALU.subtract))
                link(dve.tensor_scalar(cc[:, :, 0], vtmp[:, 0:2], 1.0 / WS, None, ALU.mult))
                link(dve.tensor_tensor(vtmp[:, 6:8], vecs[:, 8:10], vecs[:, 11:13], ALU.add))
                link(dve.tensor_scalar(coef[:, BR:BZ + 1], vtmp[:, 6:8], 0.5, None, ALU.mult))
                link(dve.tensor_copy(coef[:, BIN:BIN + 1], vecs[:, 10:11]))
                link(dve.tensor_scalar(coef[:, BHN:BHN + 1], vecs[:, 13:14], 0.5, None, ALU.mult))
                link(dve.tensor_scalar(coef[:, NSC2:NSC2 + 1], coef[:, SC2:SC2 + 1], -1.0, None, ALU.mult))
                link(dve.tensor_scalar(bse[:, 1:2], bse[:, 0:1], -2.0, None, ALU.mult))
                assert v[0] == VSTEPS, v[0]

            def body(st):
                g = st.g
                if st.has(-1):
                    after(dve, hn_ready, g(-1) + 1)
                    after(dve, rt_ready, g(-1) + 1)
                    after(dve, npre_ready, g(-2) + 1)
                    dve.scalar_tensor_tensor(out=rhn, in0=rt, scalar=1.0, in1=hn, op0=ALU.add, op1=ALU.mult).then_inc(rhn_ready, 1)
                    after(dve, rhn_ready, g(-1) + 1)
                    after(dve, nn_ready, g(-2) + 1)
                    dve.scalar_tensor_tensor(out=npre, in0=bank[3][:, :], scalar=1.0 / WS, in1=rhn, op0=ALU.mult, op1=ALU.add).then_inc(npre_ready, 1)
                if st.has(-2):
                    p = st.side(-2)
                    n2 = [0]

                    def place(ins):
                        n2[0] += 1
                        ins.then_inc(slot_step, 1)
                        return g(-2) * SLOT_STEPS + n2[0]

                    rank = bank[7][:, 64:64 + GB * NE].rearrange("p (b e) -> p b e", b=GB)
                    after(dve, rank_ps, g(-2) + 1)
                    n_rank = place(dve.tensor_tensor(rank_of, picks[p], rank.unsqueeze(1).to_broadcast([P, TOPK, GB, NE]), ALU.mult))
                    n_sum = place(dve.tensor_reduce(pickedsum, picked[p].rearrange("p b e -> p e b"), AX.X, ALU.add))
                    dve.wait_ge(slot_step, n_rank)
                    n_slot = place(dve.tensor_reduce(slotf, rank_of, AX.X, ALU.add))
                    dve.wait_ge(slot_step, n_sum)
                    place(dve.tensor_tensor(carry[:, :], carry[:, :], pickedsum, ALU.add))
                    dve.wait_ge(slot_step, n_slot)
                    dve.tensor_copy(slot[p], slotf).then_inc(slots_ready, 1)
                    assert n2[0] == SLOT_STEPS
                if at_end(st):
                    expert_low(2)
                if st.has(0):
                    after(dve, nmph_ready, g(0) + 1)
                    dve.scalar_tensor_tensor(out=nmpl[st.side(0)], in0=bank[6][:, :], scalar=1.0 / WS, in1=nmph[st.side(0)],
                                             op0=ALU.mult, op1=ALU.subtract).then_inc(nmpl_ready, 1)
                if st.has(2):
                    after_apart(dve, x_landed[st.side(2)], (st.half(2) + 1) * 16)
                    stats(lambda b: xres[:, bass.ds(g(2) * GB + b, 1), :].rearrange("p b c -> p (b c)"), 0, ln1_before(st), ln1_stats)
                if st.has(1):
                    p = st.side(1)
                    after(dve, xT_ready, g(1) + 1)
                    dve.tensor_tensor(xTl[p], xT[p], xTh[p], ALU.subtract).then_inc(xTl_ready, 1)
                if at_end(st, -1 - NG):
                    vectors()
                if st.has(-1):
                    after(dve, dxn_ready, g(-1) + 1)
                    after(dve, zt_ready, g(-1) + 1)
                    dve.scalar_tensor_tensor(out=zd, in0=zt, scalar=1.0, in1=dxn, op0=ALU.add, op1=ALU.mult).then_inc(zd_ready, 1)
                    after(dve, zd_ready, g(-1) + 1)
                    after(dve, gruT_ps, g(-2) + 1)
                    dve.scalar_tensor_tensor(out=gru, in0=zd, scalar=0.5, in1=nn, op0=ALU.mult, op1=ALU.add).then_inc(gru_ready, 1)
                if at_end(st):
                    expert_low(3)
                if st.has(1):
                    p = st.side(1)
                    after(dve, h1h_ready, g(1) + 1)
                    dve.tensor_tensor(by_parity(h1l[p]), by_parity(h1), by_parity(h1h[p]), ALU.subtract).then_inc(h1l_ready, 1)
                    after(dve, hsuml_ready, g(0) + 1)
                    dve.tensor_tensor(hsum, h1[:, 0:HG], h1[:, HG:2 * HG], ALU.add).then_inc(hsum_ready, 1)
                if st.has(-1):
                    after(dve, gruT_ps, g(-1) + 1)
                    res = xres[:, bass.ds(g(-1) * GB, GB), :]
                    dve.tensor_tensor(res, graphs(bank[6][:, :]), res, ALU.add).then_inc(x2_ready, 1)
                    after_apart(dve, x2_ready, g(-1) + 1)
                    stats(lambda b: xres[:, bass.ds(g(-1) * GB + b, 1), :].rearrange("p b c -> p (b c)"), 1, ln2_before(st), ln2_stats)
                if st.has(0):
                    after(dve, conv2_parts_ps, g(0) + 1)
                    after(dve, yh_ready, g(-1) + 1)
                    ye, yo_ = parity_of(ysum, 0), parity_of(ysum, 1)
                    xt = xT[st.side(0)]
                    dve.scalar_tensor_tensor(out=ye, in0=part_o, scalar=coef[:, SC2:SC2 + 1], in1=parity_of(xt, 0),
                                             op0=ALU.mult, op1=ALU.add).then_inc(ysum_step, 1)
                    dve.scalar_tensor_tensor(out=yo_, in0=part_o, scalar=coef[:, NSC2:NSC2 + 1], in1=parity_of(xt, 1),
                                             op0=ALU.mult, op1=ALU.add).then_inc(ysum_step, 1)
                    after(dve, ysum_step, g(0) * 5 + 1)
                    dve.scalar_tensor_tensor(out=ye, in0=part_e[:, :, 0:HN], scalar=coef[:, SC2:SC2 + 1], in1=ye,
                                             op0=ALU.mult, op1=ALU.add).then_inc(ysum_step, 1)
                    after(dve, ysum_step, g(0) * 5 + 2)
                    dve.scalar_tensor_tensor(out=yo_[:, :, 0:HN - 1], in0=part_e[:, :, 1:HN], scalar=coef[:, NSC2:NSC2 + 1], in1=yo_[:, :, 0:HN - 1],
                                             op0=ALU.mult, op1=ALU.add).then_inc(ysum_step, 1)
                if at_end(st):
                    expert_low(4)
                if st.has(1):
                    p = st.side(1)
                    after(dve, hsumh_ready, g(1) + 1)
                    dve.tensor_tensor(hsuml[p], hsum, hsumh[p], ALU.subtract).then_inc(hsuml_ready, 1)
                if st.has(0):
                    after(dve, conv2_ps, g(0) + 1)
                    yo_ = parity_of(ysum, 1)[:, :, HN - 1]
                    dve.scalar_tensor_tensor(out=yo_, in0=part_t, scalar=coef[:, NSC2:NSC2 + 1], in1=yo_,
                                             op0=ALU.mult, op1=ALU.add).then_inc(ysum_step, 1)
                    after(dve, ysum_step, g(0) * 5 + 5)
                    dve.scalar_tensor_tensor(out=parity_of(ysum, 1), in0=part_s, scalar=coef[:, SC2:SC2 + 1],
                                             in1=parity_of(ysum, 1), op0=ALU.mult, op1=ALU.add).then_inc(ysum_ready, 1)
                if st.has(-1):
                    p = st.side(-1)
                    after(dve, ln2_rstd, g(-1) + 1)
                    after(dve, scattered[p], (st.half(-1)) * TOPK * GB * 16)
                    for b in range(GB):
                        src = xres[:, bass.ds(g(-1) * GB + b, 1), :].rearrange("p b c -> p (b c)")
                        ins = dve.tensor_scalar(rows[p][0][:, b, 0:P], src, mv[1][:, b, 0:1], rstd[1][:, b:b + 1], ALU.subtract, ALU.mult)
                    ins.then_inc(rows_ready, 1)
                if st.has(1):
                    after(dve, msgh_ready, g(1) + 1)
                    dve.scalar_tensor_tensor(out=msgl, in0=bank[3][:, :], scalar=0.0, in1=msgh, op0=ALU.max, op1=ALU.subtract).then_inc(msgl_ready, 1)
                if st.has(1):
                    after(dve, kern_ready, g(1) + 1)
                    after(dve, maskT_ps, g(1) + 1)
                    after(dve, Al_ready, g(0) + 1)
                    dve.tensor_tensor(A, bank[4][:, :], kern, ALU.mult).then_inc(A_ready, 1)
                if st.has(2):
                    dve.wait_ge(ln1_rstd, g(2) + 1)
                    after(dve, xnT_ps, g(1) + 1)
                    for b in range(GB):
                        src = xres[:, bass.ds(g(2) * GB + b, 1), :].rearrange("p b c -> p (b c)")
                        ins = dve.tensor_scalar(xn[:, b * P:(b + 1) * P], src, mv[0][:, b, 0:1], rstd[0][:, b:b + 1], ALU.subtract, ALU.mult)
                    ins.then_inc(xn_ready, 1)
                if st.has(-1):
                    p = st.side(-1)
                    after(dve, rows_ready, g(-1) + 1)
                    dve.tensor_copy(rows[p][1][:, :, 0:P], rows[p][0][:, :, 0:P])
                    for c in range(TOPK):
                        ids = rows[p][c][:, :, P + 1]
                        dve.tensor_scalar(ids, ids, float(2 * W), None, ALU.add)
                if at_end(st):
                    expert_low(EH[1])
                if st.has(0):
                    after(dve, yh_ready, g(0) + 1)
                    dve.tensor_tensor(yl, y, yh, ALU.subtract).then_inc(yl_ready, 1)
                if st.has(-1):
                    p = st.side(-1)
                    n = [0]

                    def step(ins):
                        n[0] += 1
                        ins.then_inc(pick_step, 1)
                        after_apart(dve, pick_step, g(-1) * PICK_STEPS + n[0])

                    logits = bank[7][:, 0:GB * NE].rearrange("p (b e) -> p b e", b=GB)
                    after_apart(dve, logits_ps, g(-1) + 1)
                    for b in range(GB):
                        ins = dve.max(top[:, b, :], logits[:, b, :])
                    step(ins)
                    dve.tensor_tensor(lshift, top, top[:, :, 0:1].to_broadcast([P, GB, NE]), ALU.subtract).then_inc(lshift_ready, 1)
                    for b in range(GB):
                        ins = dve.max_index(topi[:, b, :], top[:, b, :], logits[:, b, :])
                    step(ins)
                    step(dve.tensor_tensor(picks[p], enum[:, :, :].unsqueeze(1).to_broadcast([P, TOPK, GB, NE]),
                                           topi[:, :, 0:TOPK].rearrange("p b k -> p k b").unsqueeze(3).to_broadcast([P, TOPK, GB, NE]),
                                           ALU.is_equal))
                    dve.tensor_tensor(picked[p], picks[p][:, 0, :, :], picks[p][:, 1, :, :], ALU.add).then_inc(picks_ready, 1)
                    dve.wait_ge(lexp_ready, g(-1) + 1)
                    step(dve.tensor_reduce(lsum, lexp, AX.X, ALU.add))
                    step(dve.reciprocal(lrec, lsum))
                    step(dve.tensor_tensor(prob, lexp[:, :, 0:TOPK], lrec.unsqueeze(2).to_broadcast([P, GB, TOPK]), ALU.mult))
                    step(dve.scalar_tensor_tensor(out=den, in0=prob[:, :, 0], scalar=1e-9, in1=prob[:, :, 1], op0=ALU.add, op1=ALU.add))
                    step(dve.reciprocal(dinv, den))
                    dve.tensor_tensor(rows[p][0][:, :, P], prob[:, :, 0], dinv, ALU.mult)
                    dve.tensor_tensor(rows[p][1][:, :, P], prob[:, :, 1], dinv, ALU.mult)
                    assert n[0] == PICK_STEPS, n[0]

            dve.wait_ge(s_rawg, RAWG)
            dve.tensor_tensor(csum, c2raw[:, :, 0:TAPS - 1:2], c2raw[:, :, 1:TAPS:2], ALU.add).then_inc(csum_ready, 1)
            body(Step(-1, 0, True, NG))
            for n in range(len(jobs)):
                low(n)
            dve.wait_ge(s_hi, len(jobs) + 1)
            for q in (0, 32, 64):
                last = dve.scalar_tensor_tensor(out=wsel[:, q:q + 3], in0=bank[4][:, 0:3], scalar=WS, in1=wseh[:, q:q + 3],
                                                op0=ALU.mult, op1=ALU.subtract)
            last.then_inc(s_lo, 1)
            dve.tensor_copy(routerT[:, :], bank[7][:, 0:NE]).then_inc(s_lo, 1)
            dve.wait_ge(s_const, 2)
            gnn_loop(dve, body, -1)

            k = [0]

            def tstep(ins):
                k[0] += 1
                ins.then_inc(table_step, 1)
                dve.wait_ge(table_step, k[0])

            def by_tile(a):
                return a.unsqueeze(1).to_broadcast([P, NT, NE])

            dve.wait_ge(totals_ps, 1)
            dve.tensor_copy(fill_row[:, :], totals).then_inc(fill_row_ready, 1)
            tstep(dve.scalar_tensor_tensor(out=total, in0=enum[:, 0, :], scalar=float(-REGION), in1=totals,
                                           op0=ALU.mult, op1=ALU.add))
            tstep(dve.tensor_scalar(totali, total, float(W - 1), None, ALU.add))
            tstep(dve.tensor_scalar(totali, totali, W.bit_length() - 1, None, ALU.arith_shift_right))
            tstep(dve.tensor_copy(tiles, totali))
            tstep(dve.tensor_tensor(tiles_le, upto[:, :, :], tiles.unsqueeze(1).to_broadcast([P, NE, NE]), ALU.mult))
            tstep(dve.tensor_reduce(tile_end, tiles_le, AX.X, ALU.add))
            tstep(dve.tensor_tensor(past, tilenum[:, :].unsqueeze(2).to_broadcast([P, NT, NE]), by_tile(tile_end), ALU.is_ge))
            tstep(dve.tensor_reduce(tile_e, past, AX.X, ALU.add))
            tstep(dve.tensor_tensor(pastn, past, by_tile(tiles), ALU.mult))
            tstep(dve.tensor_reduce(tile_s, pastn, AX.X, ALU.add))
            tstep(dve.tensor_tensor(tile_s, tilenum[:, :], tile_s, ALU.subtract))
            tstep(dve.tensor_scalar(tile_s, tile_s, float(W), None, ALU.mult))
            tstep(dve.scalar_tensor_tensor(out=tile_f, in0=tile_e, scalar=float(REGION), in1=tile_s, op0=ALU.mult, op1=ALU.add))
            tstep(dve.tensor_copy(tile_row[:, :], tile_f))
            tstep(dve.tensor_scalar(tile_f, tile_e, float(NE - 1), None, ALU.min))
            dve.tensor_copy(tile_exp[:, :], tile_f).then_inc(table_ready, 1)
            tstep(dve.tensor_tensor(tile_s[:, 1:NT], tile_e[:, 1:NT], tile_e[:, 0:NT - 1], ALU.is_gt))
            tstep(dve.tensor_scalar(tile_e, tile_e, float(NE), None, ALU.is_ge))
            tstep(dve.tensor_tensor(tile_s[:, 1:NT], tile_s[:, 1:NT], tile_e[:, 1:NT], ALU.max))
            dve.tensor_scalar(tile_apart[:, 1:NT], tile_s[:, 1:NT], float(GB * 16), None, ALU.mult).then_inc(apart_ready, 1)
            expert_low(len(expert_jobs))

            def hidden(st, off, c):
                after(dve, act1_ready, st.g(off) * EC + c + 1)
                dve.scalar_tensor_tensor(out=hid[c][0:HC, :], in0=bank[2 * c + 1][0:HC, :], scalar=1.0 / WS, in1=act1[c][0:HC, :],
                                         op0=ALU.mult, op1=ALU.mult).then_inc(hid_ready, 1)

            def hidden_low(st, off, c):
                p = st.side(off)
                after(dve, hidh_ready, st.g(off) * EC + c + 1)
                dve.tensor_tensor(hidl[p][c][0:HC, :], hid[c][0:HC, :], hidh[p][c][0:HC, :], ALU.subtract).then_inc(hidl_ready, 1)

            def tile_body(st):
                if st.has(-1):
                    hidden(st, -1, 2)
                    hidden_low(st, -1, 2)
                if st.has(0):
                    hidden(st, 0, 0)
                if st.has(-1):
                    p = st.side(-1)
                    after(dve, out_scattered[p], st.half(-1) * GB * 16)
                    after(dve, yo_ready, st.g(-3) + 1)
                    after(dve, meta_taken, st.g(-1) + 1)
                    dve.tensor_scalar(tgate[p], meta[p][:, :, 0], 1.0 / WS, None, ALU.mult)
                    dve.tensor_copy(dest[p], meta[p][:, :, 1]).then_inc(meta_ready, 1)
                if st.has(1):
                    p = st.side(1)
                    after(dve, tTh_ready, st.g(1) + 1)
                    dve.tensor_tensor(tTl[p], bank[6][:, :], tTh[p], ALU.subtract).then_inc(tTl_ready, 1)
                    after(dve, tile_landed[p], (st.half(1) + 1) * 16)
                    after(dve, meta_ready, st.g(-1) + 1)
                    dve.tensor_copy(meta[p][:, :, :], tile[p][:, :, P:P + 2]).then_inc(meta_taken, 1)
                if st.has(0):
                    hidden_low(st, 0, 0)
                    hidden(st, 0, 1)
                    hidden_low(st, 0, 1)

            tile_loop(dve, tile_body)

        @block.tensor
        def _(pe):
            pe.wait_ge(s_rawg, RAWG)
            pe.wait_ge(s_cst, 2)
            for n, (hi, lo, srcs, m, w) in enumerate(jobs):
                if n >= JB:
                    pe.wait_ge(s_lo, n - JB + 1)
                if n == CSUM // 4:
                    pe.wait_ge(csum_ready, 1)
                for j, src in enumerate(srcs):
                    ins = pe.transpose(bank[n % JB][0:m, j * w:(j + 1) * w], src, ident[0:src.shape[0], 0:src.shape[0]])
                ins.then_inc(s_tp, 1)
            pe.wait_ge(s_rawv, RAWV)
            pe.transpose(bank[4][:, 0:3], wseraw[0:3, :], ident[0:3, 0:3])
            pe.transpose(bank[7][:, 0:NE], routraw[0:NE, :], ident[0:NE, 0:NE])
            pe.transpose(bank[6][:, 0:VECS], vecraw[0:VECS, :], ident[0:VECS, 0:VECS]).then_inc(s_tp, 1)

            pe.wait_ge(s_const, 2)

            def product(o, wt, xh, xl, first, last):
                pe.matmul(o, gwh[:, wt, :], xh, start=first, stop=False)
                pe.matmul(o, gwh[:, wt, :], xl, start=False, stop=False)
                return pe.matmul(o, gwl[:, wt, :], xh, start=False, stop=last)

            def middle_first(js):
                return [0] + [j for j in js if j]

            taps = [(part_e, j) for j in middle_first(range(-EVEN_TAPS, EVEN_TAPS + 1))]
            taps += [(part_o, j) for j in middle_first(range(-EVEN_TAPS, EVEN_TAPS))]
            PARTS = len(taps)
            taps += [(part_s, j) for j in middle_first(range(-EVEN_TAPS, EVEN_TAPS + 1))]

            def conv2(st, lo, hi):
                p = st.side(0)

                def nodes(a, first):
                    return a[:, first:first + HG].rearrange("p (b i) -> p b i", i=HP1)

                for n in range(lo, hi):
                    o, j = taps[n]
                    if o is part_e:
                        wt, xh, xl = CONV2 + HALF_TAPS + 2 * j, nodes(h1h[p], 0), nodes(h1l[p], 0)
                        a, b, at = max(0, -j), min(HN, HN - j), j
                    elif o is part_o:
                        wt, xh, xl = CONV2 + HALF_TAPS + 2 * j + 1, nodes(h1h[p], HG), nodes(h1l[p], HG)
                        a, b, at = max(0, -j), min(HN, HN - j), j + 1
                    else:
                        if n == PARTS:
                            after(pe, hsuml_ready, st.g(0) + 1)
                            after(pe, slots_ready, st.g(-2) + 1)
                            for t in range(-EVEN_TAPS, 0):
                                product(part_t, CONV2 + HALF_TAPS + 2 * t, nodes(h1h[p], 0)[:, :, HN + t], nodes(h1l[p], 0)[:, :, HN + t],
                                        t == -EVEN_TAPS, t == -1)
                        wt = CSUM + EVEN_TAPS + j if j < EVEN_TAPS else CONV2 + TAPS - 1
                        xh, xl = nodes(hsumh[p], 0), nodes(hsuml[p], 0)
                        a, b, at = max(0, -1 - j), min(HN, HN - j), j + 1
                    last = n + 1 == len(taps) or taps[n + 1][0] is not o
                    ins = product(o[:, :, a:b], wt, xh[:, :, a + at:b + at], xl[:, :, a + at:b + at], j == 0, last)
                    if n == PARTS - 1:
                        ins.then_inc(conv2_parts_ps, 1)
                return ins

            done = [0]

            def transpose_experts(until):
                for n in range(done[0], until):
                    hi, lo, srcs, m, w = expert_jobs[n]
                    if n >= len(EJB):
                        pe.wait_ge(expert_lo, n - len(EJB) + 1)
                    for j, src in enumerate(srcs):
                        ins = pe.transpose(bank[EJB[n % len(EJB)]][0:m, j * w:(j + 1) * w], src, ident[0:src.shape[0], 0:src.shape[0]])
                    ins.then_inc(expert_tp, 1)
                done[0] = until

            def body(st):
                g = st.g
                if at_end(st):
                    pe.wait_ge(s_raw, 16 * 7)
                    pe.wait_ge(ysum_ready, NG)
                    pe.wait_ge(hn_ready, NG)
                    transpose_experts(3)
                if st.has(0):
                    after(pe, h1l_ready, g(0) + 1)
                    after(pe, ysum_ready, g(-1) + 1)
                    conv2(st, 0, 3)
                if st.has(-2):
                    p = st.side(-2)
                    after(pe, picks_ready, g(-2) + 1)
                    rank = bank[7][:, 64:64 + GB * NE].rearrange("p (b e) -> p b e", b=GB)
                    pk = picked[p]
                    pe.matmul(rank, tri[:, :], pk, start=True, stop=False)
                    pe.matmul(rank, ones[:, :], carry[:, :].unsqueeze(1).to_broadcast([P, GB, NE]), start=False, stop=False)
                    for d in range(1, GB):
                        ins = pe.matmul(rank[:, d:GB, :], ones[:, :], pk[:, 0:GB - d, :], start=False, stop=d == GB - 1)
                    ins.then_inc(rank_ps, 1)
                if st.has(0):
                    conv2(st, 3, 9)
                if st.has(1):
                    after(pe, xn_ready, g(1) + 1)
                    after(pe, kern_ready, g(0) + 1)
                    for b in range(GB):
                        ins = pe.transpose(bank[5][:, b * P:(b + 1) * P], xn[:, b * P:(b + 1) * P], ident[:, :])
                    ins.then_inc(xnT_ps, 1)
                if st.has(0):
                    conv2(st, 9, 17)
                if st.has(1):
                    p = st.side(1)
                    after(pe, xTl_ready, g(1) + 1)
                    after(pe, rt_ready, g(-1) + 1)
                    after(pe, h1_ready, g(0) + 1)
                    if at_end(st, -1 - NG):
                        pe.wait_ge(s_lo, len(jobs) + 2)
                    product(bank[1][:, :], CONV1, xTh[p], xTl[p], True, True).then_inc(conv1_ps, 1)
                    after(pe, zt_ready, g(-1) + 1)
                    pe.matmul(bank[2][0:67, :], wseh[:, :], xTh[p], start=True, stop=False)
                    pe.matmul(bank[2][0:67, :], wseh[:, :], xTl[p], start=False, stop=False)
                    pe.matmul(bank[2][0:67, :], wsel[:, :], xTh[p], start=False, stop=True).then_inc(s_ps, 1)
                    after(pe, npre_ready, g(-1) + 1)
                    if at_end(st, -1 - NG):
                        pe.wait_ge(bmsg_ready, 1)
                    pe.matmul(graphs(bank[3][:, :]), ones[0:2, :], bmsg[:, :].unsqueeze(1).to_broadcast([2, GB, P]), start=True, stop=False)
                    for b in range(GB):
                        o = bank[3][:, b * P:(b + 1) * P]
                        th, tl = xTh[p][:, b * P:(b + 1) * P], xTl[p][:, b * P:(b + 1) * P]
                        pe.matmul(o, th, gwh[:, MSG, :], start=False, stop=False)
                        pe.matmul(o, th, gwl[:, MSG, :], start=False, stop=False)
                        ins = pe.matmul(o, tl, gwh[:, MSG, :], start=False, stop=b == GB - 1)
                    ins.then_inc(msg_ps, 1)
                if st.has(-1):
                    after(pe, gru_ready, g(-1) + 1)
                    after(pe, nmpl_ready, g(0) + 1 if st.has(0) else NG)
                    for b in range(GB):
                        ins = pe.transpose(bank[6][:, b * P:(b + 1) * P], gru[:, b * P:(b + 1) * P], ident[:, :])
                    ins.then_inc(gruT_ps, 1)
                if at_end(st):
                    transpose_experts(EH[0])
                if st.has(0):
                    conv2(st, 17, 21)
                if st.has(1):
                    p = st.side(1)
                    after(pe, adj_landed[p], (st.half(1) + 1) * 16)
                    after(pe, hn_ready, g(-1) + 1)
                    for b in range(GB):
                        ins = pe.transpose(bank[4][:, b * P:(b + 1) * P], adjb[p][:, b, :], ident[:, :])
                    ins.then_inc(maskT_ps, 1)
                    after(pe, sLR_ready, g(1) + 1)
                    after(pe, xT_ready, g(1) + 1)
                    for b in range(GB):
                        cols = slice(b * P, (b + 1) * P)
                        ins = pe.matmul(bank[5][:, cols], sL[0:67, cols], sR[0:67, cols], start=True, stop=True)
                    ins.then_inc(dist_ps, 1)
                if st.has(0):
                    conv2(st, 21, 26).then_inc(conv2_ps, 1)
                if st.has(0):
                    p = st.side(0)
                    if st.has(1):
                        after(pe, h1_ready, g(1) + 1)
                        after(pe, sLR_ready, g(1) + 1)
                    for gate, o in ((0, 1), (1, 2)):
                        product(bank[o][:, :], gate * 3 + 2, xTh[p], xTl[p], True, False)
                    for gate, o in ((0, 1), (1, 2)):
                        product(bank[o][:, :], gate * 3 + 1, nmph[p], nmpl[p], False, False)
                if st.has(-1):
                    p = st.side(-1)
                    after(pe, rows_ready, g(-1) + 1)
                    after(pe, slots_ready, g(-2) + 1)
                    for b in range(GB):
                        ins = pe.transpose(bank[6][:, b * P:(b + 1) * P], rows[p][0][:, b, 0:P], ident[:, :])
                    ins.then_inc(xn2T_ps, 1)
                if at_end(st):
                    transpose_experts(EH[1])
                if st.has(0):
                    p = st.side(0)
                    if st.has(1):
                        after(pe, msgl_ready, g(1) + 1)
                    product(bank[3][:, :], 2 * 3 + 1, nmph[p], nmpl[p], True, False)
                if st.has(0):
                    p = st.side(0)
                    if st.has(1):
                        after(pe, A_ready, g(1) + 1)
                    product(bank[4][:, :], 2 * 3 + 2, xTh[p], xTl[p], True, True).then_inc(hn_ps, 1)
                if st.has(-1):
                    after(pe, xn2T_ready, g(-1) + 1)
                    if st.has(0):
                        after(pe, ysum_ready, g(0) + 1)
                    for b in range(GB):
                        ins = pe.matmul(bank[7][:, b * NE:(b + 1) * NE], xn2T[:, b * P:(b + 1) * P], routerT[:, :], start=True, stop=True)
                    ins.then_inc(logits_ps, 1)
                if st.has(0):
                    after(pe, yl_ready, g(0) + 1)
                    for gate, o in ((0, 1), (1, 2), (2, 3)):
                        ins = product(bank[o][:, :], gate * 3, yh, yl, False, True)
                    ins.then_inc(gates_ps, 1)
                if st.has(1):
                    p = st.side(1)
                    after(pe, Al_ready, g(1) + 1)
                    if st.has(-1):
                        after(pe, x2_ready, g(-1) + 1)
                    for b in range(GB):
                        cols = slice(b * P, (b + 1) * P)
                        o = bank[6][:, cols]
                        pe.matmul(o, msgh[:, cols], Ah[:, cols], start=True, stop=False)
                        pe.matmul(o, msgh[:, cols], Al[:, cols], start=False, stop=False)
                        ins = pe.matmul(o, msgl[:, cols], Ah[:, cols], start=False, stop=True)
                    ins.then_inc(nmp_ps, 1)

            gnn_loop(pe, body)

            pe.wait_ge(slots_ready, NG)
            pe.matmul(totals, ones[:, :], carry[:, :], start=True, stop=True).then_inc(totals_ps, 1)
            transpose_experts(len(expert_jobs))
            pe.wait_ge(expert_lo, len(expert_jobs))
            pe.wait_ge(table_ready, 1)

            def chunk(st, c, e):
                p = st.side(0)
                if c == 0:
                    after(pe, tTl_ready, st.g() + 1)
                after(pe, hid_ready, st.g(-1) * EC + c + 1)
                for hi, lo, o in ((w1h, w1l, bank[2 * c]), (w3h, w3l, bank[2 * c + 1])):
                    at = bass.ds(e * (EC * HC) + c * HC, HC)
                    pe.matmul(o[0:HC, :], hi[:, at], tTh[p], start=True, stop=False)
                    pe.matmul(o[0:HC, :], hi[:, at], tTl[p], start=False, stop=False)
                    ins = pe.matmul(o[0:HC, :], lo[:, at], tTh[p], start=False, stop=True)
                ins.then_inc(h13_ps, 1)

            def load_expert(t):
                return pe.value_load(tile_exp[0:1, bass.ds(t, 1)], min_val=0, max_val=NE - 1)

            def tile_body(st):
                if st.has(-1):
                    eb = load_expert(st.g(-1))
                if st.has(0):
                    e = load_expert(st.g(0))
                    chunk(st, 0, e)
                if st.has(1):
                    p = st.side(1)
                    after(pe, tile_landed[p], (st.half(1) + 1) * 16)
                    after(pe, tTl_ready, st.g(0) + 1)
                    for b in range(GB):
                        ins = pe.transpose(bank[6][:, b * P:(b + 1) * P], tile[p][:, b, 0:P], ident[:, :])
                    ins.then_inc(tileT_ps, 1)
                if st.has(0):
                    chunk(st, 1, e)
                if st.has(-1):
                    p = st.side(-1)
                    after(pe, yo_ready, st.g(-2) + 1)
                    for c in range(EC):
                        after(pe, hidl_ready, st.g(-1) * EC + c + 1)
                        at = bass.ds(eb * (EC * P) + c * P, P)
                        for b in range(GB):
                            o = bank[7][:, b * P:(b + 1) * P]
                            cols = slice(b * P, (b + 1) * P)
                            pe.matmul(o, hidh[p][c][0:HC, cols], w2h[0:HC, at], start=c == 0 and b == 0, stop=False)
                            pe.matmul(o, hidh[p][c][0:HC, cols], w2l[0:HC, at], start=False, stop=False)
                            ins = pe.matmul(o, hidl[p][c][0:HC, cols], w2h[0:HC, at], start=False, stop=c == EC - 1 and b == GB - 1)
                    ins.then_inc(y_ps, 1)
                if st.has(0):
                    chunk(st, 2, e)

            tile_loop(pe, tile_body)


_INS = ["x", "adj"] + ["L0_gnn_" + n for n in (
    "w_se b_se conv1_w bn1_g bn1_b bn1_m bn1_v conv2_w bn2_g bn2_b bn2_m bn2_v w_msg b_msg w_ih b_ih w_hh b_hh").split()]
_INS += ["L0_ffn_" + n for n in "router_w w1 w2 w3".split()]
_OUTS = [((128 * 128 + W, 128), "float32")]


def kernel(**inputs):
    import numpy as _np
    import concourse.bacc as _bacc
    from concourse import mybir as _mybir
    from concourse.bass_utils import run_bass_kernel_spmd as _run

    nc = _bacc.Bacc("TRN2", target_bir_lowering=False, num_devices=1)
    arrays, args = {}, []
    for name in _INS:
        a = _np.ascontiguousarray(inputs[name])
        arrays[f"in_{name}_dram"] = a
        args.append(nc.dram_tensor(f"in_{name}_dram", a.shape, _mybir.dt.from_np(a.dtype), kind="ExternalInput").ap())
    for i, (shape, dtype) in enumerate(_OUTS):
        dt = _mybir.dt.from_np(_np.dtype(dtype))
        args.append(nc.dram_tensor(f"out_{i}_dram", shape, dt, kind="ExternalOutput").ap())
    build(nc, *args)
    r = _run(nc, [arrays], core_ids=[0])
    return r.results[0]["out_0_dram"][0:128 * 128].reshape(128, 128, 128)
```
